# Optimizing a Trainium2 kernel written in Bass

```python
import numpy as np
import jax
import jax.numpy as jnp

def _softmax(x, axis=-1):
    return jax.nn.softmax(x, axis=axis)

def _gelu(x):
    return jax.nn.gelu(x, approximate=True)

def _silu(x):
    return jax.nn.silu(x)

def _sigmoid(x):
    return jax.nn.sigmoid(x)

def _layernorm(x, axis=-1, eps=1e-05):
    m = jnp.mean(x, axis=axis, keepdims=True)
    v = jnp.var(x, axis=axis, keepdims=True)
    return (x - m) / jnp.sqrt(v + eps)

def _scatter_add(tgt, idx, src, axis=0):
    return tgt.at[idx].add(src)

def _segment_sum(src, seg, n):
    return jax.ops.segment_sum(src, seg, n)
kernel_name = 'mk_prb_d2_jaxref_r8_df7edb'

def setup_inputs(seed: int=0):
    np.random.seed(seed)
    _w = jnp.asarray

    def _L0_attn_setup():
        import jax, jax.numpy as jnp
        import numpy as np
        HID = 256
        HEADS = 16
        HD = HID // HEADS
        EPS = 1e-06

        def _heads(x, b, s):
            return x.reshape(b, s, HEADS, HD).transpose(0, 2, 1, 3)
        key = jax.random.key(seed)
        ks = jax.random.split(key, 9)
        s = 1.0 / np.sqrt(HID)
        return {'hidden_states': jax.random.normal(ks[0], (4, 512, HID), jnp.float32), 'q_w': jax.random.normal(ks[1], (HID, HID), jnp.float32) * s, 'q_b': jnp.zeros((HID,), jnp.float32), 'k_w': jax.random.normal(ks[2], (HID, HID), jnp.float32) * s, 'k_b': jnp.zeros((HID,), jnp.float32), 'v_w': jax.random.normal(ks[3], (HID, HID), jnp.float32) * s, 'v_b': jnp.zeros((HID,), jnp.float32), 'o_w': jax.random.normal(ks[4], (HID, HID), jnp.float32) * s, 'o_b': jnp.zeros((HID,), jnp.float32)}
    _L0_attn_in = _L0_attn_setup()

    def _L0_ffn_setup():
        import jax, jax.numpy as jnp
        import numpy as np

        def _sparsify_2to4(h):
            B, S, I = h.shape
            g = h.reshape(B, S, I // 4, 4)
            a = jnp.abs(g)
            _, idx = jax.lax.top_k(a, 2)
            pos = jnp.arange(4)
            mask = (pos == idx[..., 0:1]) | (pos == idx[..., 1:2])
            return (g * mask.astype(g.dtype)).reshape(B, S, I)
        key = jax.random.key(seed)
        k1, k2, k3, k4 = jax.random.split(key, 4)
        B, S, H, I = (4, 256, 256, 1024)
        x = jax.random.normal(k1, (B, S, H), dtype=jnp.float32)
        w_gate = jax.random.normal(k2, (H, I), dtype=jnp.float32) / np.sqrt(H)
        w_up = jax.random.normal(k3, (H, I), dtype=jnp.float32) / np.sqrt(H)
        w_down = jax.random.normal(k4, (I, H), dtype=jnp.float32) / np.sqrt(I)
        return {'x': x, 'w_gate': w_gate, 'w_up': w_up, 'w_down': w_down}
    _L0_ffn_in = _L0_ffn_setup()

    def _L1_attn_setup():
        import jax, jax.numpy as jnp
        import numpy as np
        N_HEADS = 16
        D_HEAD = 128
        D_MODEL = 256
        MAXLEN = 256
        key = jax.random.key(seed)
        ks = jax.random.split(key, 9)
        b, t = (2, 256)
        hd = N_HEADS * D_HEAD
        init = 0.02
        return {'x': jax.random.normal(ks[0], (b, t, D_MODEL), dtype=jnp.float32), 'Wq': jax.random.normal(ks[1], (D_MODEL, hd), dtype=jnp.float32) * init, 'bq': jnp.zeros((hd,), dtype=jnp.float32), 'Wk': jax.random.normal(ks[2], (D_MODEL, hd), dtype=jnp.float32) * init, 'bk': jnp.zeros((hd,), dtype=jnp.float32), 'Wv': jax.random.normal(ks[3], (D_MODEL, hd), dtype=jnp.float32) * init, 'bv': jnp.zeros((hd,), dtype=jnp.float32), 'Wo': jax.random.normal(ks[4], (hd, D_MODEL), dtype=jnp.float32) * init, 'bo': jnp.zeros((D_MODEL,), dtype=jnp.float32)}
    _L1_attn_in = _L1_attn_setup()

    def _L1_ffn_setup():
        import jax, jax.numpy as jnp
        import numpy as np
        DIM = 256
        INTER = 176
        E = 16
        TOPK = 4
        G = 4
        TOPK_G = 2
        N_SHARED = 2
        SHARED_INTER = N_SHARED * INTER
        ROUTE_SCALE = 1.0

        def _moe_forward(x, Wg, W1, W3, W2, Ws1, Ws3, Ws2):
            B, S, D = x.shape
            xt = x.reshape(-1, D)
            T = xt.shape[0]
            scores = jax.nn.softmax(xt @ Wg.T, axis=-1)
            sg = scores.reshape(T, G, E // G)
            group_scores = sg.max(axis=-1)
            gidx = jax.lax.top_k(group_scores, TOPK_G)[1]
            gmask = jax.nn.one_hot(gidx, G, dtype=jnp.float32).sum(axis=1) > 0
            masked = jnp.where(gmask[:, :, None], sg, -jnp.inf).reshape(T, E)
            topi = jax.lax.top_k(masked, TOPK)[1]
            weights = jnp.take_along_axis(scores, topi, axis=1) * ROUTE_SCALE
            combine = jnp.zeros((T, E), xt.dtype).at[jnp.arange(T)[:, None], topi].add(weights)
            h = jax.nn.silu(jnp.einsum('td,eid->eti', xt, W1)) * jnp.einsum('td,eid->eti', xt, W3)
            expert_out = jnp.einsum('eti,edi->etd', h, W2)
            y = jnp.einsum('etd,te->td', expert_out, combine)
            z = jax.nn.silu(xt @ Ws1.T) * (xt @ Ws3.T) @ Ws2.T
            return (y + z).reshape(B, S, D)
        key = jax.random.key(seed)
        ks = jax.random.split(key, 8)
        s = 0.02
        x = jax.random.normal(ks[0], (1, 256, DIM), dtype=jnp.float32)
        Wg = jax.random.normal(ks[1], (E, DIM), dtype=jnp.float32) * s
        W1 = jax.random.normal(ks[2], (E, INTER, DIM), dtype=jnp.float32) * s
        W3 = jax.random.normal(ks[3], (E, INTER, DIM), dtype=jnp.float32) * s
        W2 = jax.random.normal(ks[4], (E, DIM, INTER), dtype=jnp.float32) * s
        Ws1 = jax.random.normal(ks[5], (SHARED_INTER, DIM), dtype=jnp.float32) * s
        Ws3 = jax.random.normal(ks[6], (SHARED_INTER, DIM), dtype=jnp.float32) * s
        Ws2 = jax.random.normal(ks[7], (DIM, SHARED_INTER), dtype=jnp.float32) * s
        return {'x': x, 'Wg': Wg, 'W1': W1, 'W3': W3, 'W2': W2, 'Ws1': Ws1, 'Ws3': Ws3, 'Ws2': Ws2}
    _L1_ffn_in = _L1_ffn_setup()
    _d = {'L0_attn_hidden_states': _L0_attn_in['hidden_states'], 'L0_attn_q_w': _L0_attn_in['q_w'], 'L0_attn_q_b': _L0_attn_in['q_b'], 'L0_attn_k_w': _L0_attn_in['k_w'], 'L0_attn_k_b': _L0_attn_in['k_b'], 'L0_attn_v_w': _L0_attn_in['v_w'], 'L0_attn_v_b': _L0_attn_in['v_b'], 'L0_attn_o_w': _L0_attn_in['o_w'], 'L0_attn_o_b': _L0_attn_in['o_b'], 'L0_ffn_w_gate': _L0_ffn_in['w_gate'], 'L0_ffn_w_up': _L0_ffn_in['w_up'], 'L0_ffn_w_down': _L0_ffn_in['w_down'], 'L1_attn_Wq': _L1_attn_in['Wq'], 'L1_attn_bq': _L1_attn_in['bq'], 'L1_attn_Wk': _L1_attn_in['Wk'], 'L1_attn_bk': _L1_attn_in['bk'], 'L1_attn_Wv': _L1_attn_in['Wv'], 'L1_attn_bv': _L1_attn_in['bv'], 'L1_attn_Wo': _L1_attn_in['Wo'], 'L1_attn_bo': _L1_attn_in['bo'], 'L1_ffn_Wg': _L1_ffn_in['Wg'], 'L1_ffn_W1': _L1_ffn_in['W1'], 'L1_ffn_W3': _L1_ffn_in['W3'], 'L1_ffn_W2': _L1_ffn_in['W2'], 'L1_ffn_Ws1': _L1_ffn_in['Ws1'], 'L1_ffn_Ws3': _L1_ffn_in['Ws3'], 'L1_ffn_Ws2': _L1_ffn_in['Ws2']}
    _x0 = _d['L0_attn_hidden_states']
    _d['L0_attn_hidden_states'] = jax.random.normal(jax.random.fold_in(jax.random.key(seed), 1), (1, 2048, 256), dtype=_x0.dtype)
    del _x0
    return _d

def reference(L0_attn_hidden_states, L0_attn_q_w, L0_attn_q_b, L0_attn_k_w, L0_attn_k_b, L0_attn_v_w, L0_attn_v_b, L0_attn_o_w, L0_attn_o_b, L0_ffn_w_gate, L0_ffn_w_up, L0_ffn_w_down, L1_attn_Wq, L1_attn_bq, L1_attn_Wk, L1_attn_bk, L1_attn_Wv, L1_attn_bv, L1_attn_Wo, L1_attn_bo, L1_ffn_Wg, L1_ffn_W1, L1_ffn_W3, L1_ffn_W2, L1_ffn_Ws1, L1_ffn_Ws3, L1_ffn_Ws2):

    def _L0_attn_ref(hidden_states, q_w, q_b, k_w, k_b, v_w, v_b, o_w, o_b):
        import jax, jax.numpy as jnp
        import numpy as np
        HID = 256
        HEADS = 16
        HD = HID // HEADS
        EPS = 1e-06

        def _heads(x, b, s):
            return x.reshape(b, s, HEADS, HD).transpose(0, 2, 1, 3)
        b, s, _ = hidden_states.shape
        q = _heads(hidden_states @ q_w.T + q_b, b, s)
        k = _heads(hidden_states @ k_w.T + k_b, b, s)
        v = _heads(hidden_states @ v_w.T + v_b, b, s)
        qp = jax.nn.elu(q) + 1.0
        kp = jax.nn.elu(k) + 1.0
        kv = jnp.einsum('bhsd,bhse->bhde', kp, v)
        z = jnp.einsum('bhsd,bhd->bhs', qp, kp.sum(axis=2))[..., None]
        attn = jnp.einsum('bhsd,bhde->bhse', qp, kv) / (z + EPS)
        out = attn.transpose(0, 2, 1, 3).reshape(b, s, HID)
        return out @ o_w.T + o_b

    def _L0_ffn_ref(x, w_gate, w_up, w_down):
        import jax, jax.numpy as jnp
        import numpy as np

        def _sparsify_2to4(h):
            B, S, I = h.shape
            g = h.reshape(B, S, I // 4, 4)
            a = jnp.abs(g)
            _, idx = jax.lax.top_k(a, 2)
            pos = jnp.arange(4)
            mask = (pos == idx[..., 0:1]) | (pos == idx[..., 1:2])
            return (g * mask.astype(g.dtype)).reshape(B, S, I)
        h = jax.nn.silu(jnp.einsum('bsh,hi->bsi', x, w_gate)) * jnp.einsum('bsh,hi->bsi', x, w_up)
        h_sparse = _sparsify_2to4(h)
        return jnp.einsum('bsi,ih->bsh', h_sparse, w_down)

    def _L1_attn_ref(x, Wq, bq, Wk, bk, Wv, bv, Wo, bo):
        import jax, jax.numpy as jnp
        import numpy as np
        N_HEADS = 16
        D_HEAD = 128
        D_MODEL = 256
        MAXLEN = 256
        b, t, _ = x.shape
        h, dh = (N_HEADS, D_HEAD)
        scale = 1.0 / np.sqrt(dh).astype(np.float32)
        q = (x @ Wq + bq).reshape(b, h, t, dh)
        k = (x @ Wk + bk).reshape(b, t, h, dh).transpose(0, 2, 3, 1)
        v = (x @ Wv + bv).reshape(b, t, h, dh).transpose(0, 2, 1, 3)
        logits = jnp.einsum('bhtd,bhds->bhts', q, k) * scale
        mask = jnp.triu(jnp.full((t, t), -jnp.inf, dtype=x.dtype), k=1)
        weights = jax.nn.softmax(logits + mask, axis=-1)
        out = jnp.einsum('bhts,bhsd->bhtd', weights, v)
        out = out.transpose(0, 2, 1, 3).reshape(b, t, h * dh)
        return out @ Wo + bo

    def _L1_ffn_ref(x, Wg, W1, W3, W2, Ws1, Ws3, Ws2):
        import jax, jax.numpy as jnp
        import numpy as np
        DIM = 256
        INTER = 176
        E = 16
        TOPK = 4
        G = 4
        TOPK_G = 2
        N_SHARED = 2
        SHARED_INTER = N_SHARED * INTER
        ROUTE_SCALE = 1.0

        def _moe_forward(x, Wg, W1, W3, W2, Ws1, Ws3, Ws2):
            B, S, D = x.shape
            xt = x.reshape(-1, D)
            T = xt.shape[0]
            scores = jax.nn.softmax(xt @ Wg.T, axis=-1)
            sg = scores.reshape(T, G, E // G)
            group_scores = sg.max(axis=-1)
            gidx = jax.lax.top_k(group_scores, TOPK_G)[1]
            gmask = jax.nn.one_hot(gidx, G, dtype=jnp.float32).sum(axis=1) > 0
            masked = jnp.where(gmask[:, :, None], sg, -jnp.inf).reshape(T, E)
            topi = jax.lax.top_k(masked, TOPK)[1]
            weights = jnp.take_along_axis(scores, topi, axis=1) * ROUTE_SCALE
            combine = jnp.zeros((T, E), xt.dtype).at[jnp.arange(T)[:, None], topi].add(weights)
            h = jax.nn.silu(jnp.einsum('td,eid->eti', xt, W1)) * jnp.einsum('td,eid->eti', xt, W3)
            expert_out = jnp.einsum('eti,edi->etd', h, W2)
            y = jnp.einsum('etd,te->td', expert_out, combine)
            z = jax.nn.silu(xt @ Ws1.T) * (xt @ Ws3.T) @ Ws2.T
            return (y + z).reshape(B, S, D)
        return _moe_forward(x, Wg, W1, W3, W2, Ws1, Ws3, Ws2)
    x = L0_attn_hidden_states
    xn = _layernorm(x, axis=-1)
    x = x + _L0_attn_ref(xn, L0_attn_q_w, L0_attn_q_b, L0_attn_k_w, L0_attn_k_b, L0_attn_v_w, L0_attn_v_b, L0_attn_o_w, L0_attn_o_b) + _L0_ffn_ref(xn, L0_ffn_w_gate, L0_ffn_w_up, L0_ffn_w_down)
    xn = _layernorm(x, axis=-1)
    x = x + _L1_attn_ref(xn, L1_attn_Wq, L1_attn_bq, L1_attn_Wk, L1_attn_bk, L1_attn_Wv, L1_attn_bv, L1_attn_Wo, L1_attn_bo) + _L1_ffn_ref(xn, L1_ffn_Wg, L1_ffn_W1, L1_ffn_W3, L1_ffn_W2, L1_ffn_Ws1, L1_ffn_Ws3, L1_ffn_Ws2)
    return x

_drawn_inputs = setup_inputs


def setup_inputs(seed=0):
    import zlib

    import numpy as np

    out = dict(_drawn_inputs(seed))
    spreads = {'L0_attn_q_b': (0.0, 2.0),
     'L0_attn_k_b': (0.0, 2.0),
     'L0_attn_v_b': (0.0, 0.1),
     'L0_attn_o_b': (0.0, 0.1),
     'L1_attn_bq': (0.0, 2.0),
     'L1_attn_bk': (0.0, 2.0),
     'L1_attn_bv': (0.0, 0.504),
     'L1_attn_bo': (0.0, 0.521)}
    factors = {'L0_attn_q_w': 8.0,
     'L0_attn_k_w': 4.652,
     'L1_attn_Wq': 8.0,
     'L1_attn_Wk': 8.0,
     'L1_ffn_Wg': 8.0,
     'L1_ffn_W1': 8.0,
     'L1_ffn_W3': 8.0,
     'L1_ffn_W2': 8.0,
     'L1_ffn_Ws1': 3.385,
     'L1_ffn_Ws3': 3.341,
     'L1_ffn_Ws2': 3.34}
    for name, (base, spread) in spreads.items():
        noise = np.random.default_rng([zlib.crc32(name.encode()), seed]).standard_normal(out[name].shape)
        drawn = base * np.exp(spread * noise) if base else spread * noise
        out[name] = jnp.asarray(drawn.astype(out[name].dtype))
    for name, factor in factors.items():
        out[name] = (out[name] * factor).astype(out[name].dtype)
    return out
```

```python
from contextlib import ExitStack

import concourse.bass as bass
from concourse import mybir

F32 = mybir.dt.float32
FR = mybir.dt.float32r
BF16 = mybir.dt.bfloat16
ALU = mybir.AluOpType
ACT = mybir.ActivationFunctionType
AX = mybir.AxisListType

P = 128
T = 2048
D = 256
KT = D // P
NT = T // P
CH = 512
NCH = T // CH
TC = CH // P

INTER0 = 1024
NI0 = INTER0 // P
SG = NI0 // 4
OFF_Q = 0
OFF_O = OFF_Q + KT * D
OFF_KV = OFF_O + KT * D
OFF_GU = OFF_KV + KT * 2 * D
OFF_DN = OFF_GU + NI0 * 2 * KT * P
W0_COLS = OFF_DN + NI0 * D
STG = 2048

NH = 16
HD = 128
QC = NH
SCALE = float(1.0 / (HD ** 0.5))
NEG = -1.0e30
FROM = 1

E = 16
INTER1 = 176
SHARED = 352
ROWS = E * INTER1 + SHARED
NI1 = -(-ROWS // P)
GT = 5
NG = NI1 // GT
GW = 3 * D
GCOLS = GT * (GW + P)


SEMS = {
    "a": ("xn_rdy xT_ps xh_rdy xl_rdy q_ps kv_ps qs_rdy kvs_rdy vh_rdy vl_rdy rel_rdy mn_rdy ex_rdy "
          "f_rdy f_hi f_lo kva_ps kva_add gu_ps th_rdy s_rdy h_rdy ab_rdy win_rdy cnt_rdy hm_rdy "
          "hs_hi hs_lo y_ps y_add").split(),
    "b": "kz_rdy kz_hi kz_lo nd_ps den_rdy rec_rdy at_rdy at_hi at_lo o_ps o_add ob_add bs_rdy ag_rdy sd".split(),
    "r": "wg_in wg_hi wg_lo xn_rdy xT_ps xc_hi xc_lo xs_hi xs_lo lg_ps mx_rdy ex_rdy v_rdy c_rdy bo_add".split(),
    "t": ("wq_in wq_hi wq_lo staged wk_hi wk_lo wo_hi wo_lo pj_ps q_rdy q_hi q_lo pj_hi pj_rd s_ps mx nb_rdy ex_rdy "
          "rsum rs_rdy T_ps pt_hi pt_lo pv_ps ov_rdy o_rdy oT_ps o_hi o_lo y_ps yb_rdy y_add b_in bh_rdy").split(),
    "e": ("cp cT_ps ct_hi ct_lo w_in w_hi w_lo g_ps u_ps c_ps th_rdy s_rdy h_rdy hc_rdy h_hi h_lo y_ps y_add").split(),
}


def build(nc, d, out):
    with ExitStack() as top:
        def sem(name):
            return top.enter_context(nc.semaphore(name))

        def sbuf(stack, name, shape, dt):
            return stack.enter_context(nc.sbuf_tensor(name, shape, dt))

        sems = {f"{k}_{s}": sem(f"{k}_{s}") for k, names in SEMS.items() for s in names}

        acc = sbuf(top, "acc", [P, NT, D], F32)
        xTh = sbuf(top, "xTh", [P, KT, T], FR)
        xTl = sbuf(top, "xTl", [P, KT, T], FR)
        ident = sbuf(top, "ident", [P, P], F32)
        cb = sbuf(top, "cb", [P, NT, E + 1], F32)
        ps = top.enter_context(nc.psum_tensor("ps", [P, 8, CH], F32))
        mv = sbuf(top, "mv", [P, NT, 2], F32)
        rstd = sbuf(top, "rstd", [P, NT], F32)

        layer0(nc, top, d, acc, xTh, xTl, ident, ps, mv, rstd, sem, sems, sbuf)
        route(nc, d, acc, xTh, xTl, ident, cb, ps, mv, rstd, sem, sems, sbuf)
        attention(nc, d, acc, xTh, xTl, ident, ps, sem, sems, sbuf)
        experts(nc, d, acc, xTh, xTl, ident, cb, ps, sem, sems, sbuf)

        stored = sem("stored")
        with nc.Block() as block:
            @block.sync
            def _(sp):
                sp.dma_start(out[0].rearrange("(t p) d -> p t d", p=P), acc[:]).then_inc(stored, 16)
                sp.wait_ge(stored, 16)


def layer0(nc, top, d, acc, xTh, xTl, ident, ps, mv, rstd, sem, sems, sbuf):
    with ExitStack() as st:
        wh = sbuf(st, "w0h", [P, W0_COLS], FR)
        wl = sbuf(st, "w0l", [P, W0_COLS], FR)
        bqc = sbuf(st, "bqc", [P, KT], F32)
        bkv = sbuf(st, "bkv", [P, 2 * D], F32)
        bo = sbuf(st, "bo0", [P, D], F32)
        bd = sbuf(st, "bd", [P, P], F32)
        kvacc = sbuf(st, "kvacc", [P, KT, P + 2], F32)
        vh = sbuf(st, "vh", [P, TC, KT, P + 2], FR)
        vl = sbuf(st, "vl", [P, TC, KT, P + 2], FR)

        x_in, w_in, c_in = sem("x_in"), [sem("w_in0"), sem("w_in1")], sem("c_in")
        w_hi, w_lo = sem("w_hi"), sem("w_lo")
        st_done, ag_done, sd_done, rs_done, ms_done = (
            sem("st_done"), sem("ag_done"), sem("sd_done"), sem("rs_done"), sem("ms_done"))

        with ExitStack() as s0:
            stg = sbuf(s0, "stg", [P, 2, STG], F32)
            bst = sbuf(s0, "bst", [P, NT, 6], F32)
            with nc.Block() as block:
                @block.sync
                def _(sp):
                    for h in range(4):
                        sp.dma_start(acc[:, 4 * h:4 * h + 4, :],
                                     d["x"][0, h * CH:(h + 1) * CH].rearrange("(t p) d -> p t d", p=P)).then_inc(x_in, 16)
                    for k in range(W0_COLS // STG):
                        if k >= 2:
                            sp.wait_ge(w_hi, k - 1)
                            sp.wait_ge(w_lo, k - 1)
                        sp.dma_start(stg[:, k % 2, :], d["w0"][:, k * STG:(k + 1) * STG]).then_inc(w_in[k % 2], 16)
                    sp.dma_start(ident[:], d["ident"]).then_inc(c_in, 16)
                    sp.dma_start(bd[:], d["bd"]).then_inc(c_in, 16)
                    sp.dma_start(bqc[:], d["bq0"]).then_inc(c_in, 16)
                    sp.dma_start(bkv[:], d["bkv0"].partition_broadcast(P)).then_inc(c_in, 16)
                    sp.dma_start(bo[:], d["bo0"].partition_broadcast(P)).then_inc(c_in, 16)
                    sp.wait_ge(c_in, 80)

                @block.gpsimd
                def _(pool):
                    for s in sems.values():
                        pool.sem_inc(s, FROM)
                    nc.gpsimd.memset(kvacc[:], 0.0)
                    nc.gpsimd.memset(vh[:].bitcast(F32), 1.0)
                    nc.gpsimd.memset(vl[:].bitcast(F32), 0.0)

                @block.scalar
                def _(act):
                    act.wait_ge(sd_done, 1)
                    nc.scalar.activation(rstd[:], rstd[:], ACT.Sqrt).then_inc(sd_done, 1)
                    for k in range(W0_COLS // STG):
                        act.wait_ge(w_in[k % 2], 16 * (k // 2 + 1))
                        nc.scalar.activation(wh[:, k * STG:(k + 1) * STG], stg[:, k % 2, :], ACT.Copy).then_inc(w_hi, 1)

                @block.vector
                def _(dve):
                    dve.wait_ge(x_in, 64)
                    with dve.Fori(0, NT) as i:
                        nc.vector.bn_stats(bst[:, bass.ds(i, 1), :], acc[:, bass.ds(i, 1), :]).then_inc(st_done, 1)
                    dve.wait_ge(st_done, NT)
                    for i in range(NT):
                        nc.vector.bn_aggr(mv[:, i, :], bst[:, i, :]).then_inc(ag_done, 1)
                    dve.wait_ge(ag_done, NT)
                    nc.vector.tensor_scalar(rstd[:], mv[:, :, 1], 1e-5, None, ALU.add).then_inc(sd_done, 1)
                    dve.wait_ge(sd_done, 2)
                    nc.vector.reciprocal(rstd[:], rstd[:]).then_inc(rs_done, 1)
                    for k in range(W0_COLS // STG):
                        dve.wait_ge(w_hi, k + 1)
                        nc.vector.tensor_tensor(wl[:, k * STG:(k + 1) * STG], stg[:, k % 2, :],
                                                wh[:, k * STG:(k + 1) * STG].bitcast(F32), ALU.subtract).then_inc(w_lo, 1)

        layer0_chunks(nc, d, acc, xTh, xTl, ident, ps, mv, rstd, wh, wl, bqc, bkv, kvacc, vh, vl, sems, sbuf)
        layer0_out(nc, acc, xTh, xTl, ps, mv, rstd, wh, wl, bo, bd, kvacc, sems, sbuf)


PARTS = ((0, 0), (0, 1), (1, 0))


def layer0_chunks(nc, d, acc, qfh, qfl, ident, ps, mv, rstd, wh, wl, bqc, bkv, kvacc, vh, vl, sems, sbuf):
    with ExitStack() as st:
        xn = sbuf(st, "xn", [P, TC, D], F32)
        xh = sbuf(st, "xh", [P, KT, CH], FR)
        xl = sbuf(st, "xl", [P, KT, CH], FR)
        qs = xn[:].rearrange("p t d -> p (t d)").rearrange("p (a b) -> p a b", a=KT)
        kvs = sbuf(st, "kvs", [P, TC, 2 * D], F32)
        rel = sbuf(st, "rel", [P, 2, 2 * CH], F32)
        mn = sbuf(st, "mn", [P, 2, 2 * CH], F32)
        kfh = sbuf(st, "kfh", [P, TC, D], FR)
        kfl = sbuf(st, "kfl", [P, TC, D], FR)
        th = sbuf(st, "th", [P, 2, CH], F32)
        hh32 = sbuf(st, "hh32", [P, 4, CH], F32)
        ab = rel[:].rearrange("p s (a b) -> p (s a) b", a=2)
        win = sbuf(st, "win", [P, 6, CH], BF16)
        cnt = mn[:, 0, :].bitcast(BF16).rearrange("p (a b) -> p a b", a=4)
        hsh = sbuf(st, "hsh", [P, 4, CH], FR)
        hsl = sbuf(st, "hsl", [P, 4, CH], FR)
        w = (wh, wl)
        x = (xh, xl)
        kf, v, hs = (kfh, kfl), (vh, vl), (hsh, hsl)

        (xn_rdy, xT_ps, xh_rdy, xl_rdy, q_ps, kv_ps, qs_rdy, kvs_rdy, vh_rdy, vl_rdy, rel_rdy, mn_rdy, ex_rdy,
         f_rdy, f_hi, f_lo, kva_ps, kva_add, gu_ps, th_rdy, s_rdy, h_rdy, ab_rdy, win_rdy, cnt_rdy, hm_rdy,
         hs_hi, hs_lo, y_ps, y_add) = [sems["a_" + s] for s in SEMS["a"]]

        def feat(s, buf):
            return buf[:, s, :]

        qpre = xn[:].rearrange("p t d -> p (t d)")
        kpre = kvs[:, :, 0:D]

        def feature(s, n):
            f = feat(s, mn).rearrange("p (a b) -> p a b", a=TC if s else KT)
            if s == 0:
                return f, qfh[:, :, bass.ds(n * CH, CH)], qfl[:, :, bass.ds(n * CH, CH)]
            return f, kfh[:], kfl[:]

        with nc.Block() as block:
            @block.tensor
            def _(pe):
                with pe.Fori(0, NCH) as n:
                    pe.wait_ge(y_add, FROM + n * SG)
                    for kt in range(KT):
                        for j in range(TC):
                            pe.wait_ge(xn_rdy, FROM + n * TC + j + 1)
                            m = nc.tensor.transpose(ps[:, kt, j * P:(j + 1) * P], xn[:, j, kt * P:(kt + 1) * P], ident[:])
                        m.then_inc(xT_ps, 1)
                    pe.wait_ge(h_rdy, FROM + n * NI0)
                    pe.wait_ge(xh_rdy, FROM + n * KT + KT)
                    pe.wait_ge(xl_rdy, FROM + n * KT + KT)
                    for m2 in range(KT):
                        k = 0
                        for kt in range(KT):
                            for a, b in PARTS:
                                o = OFF_Q + kt * D + m2 * P
                                m = nc.tensor.matmul(ps[:, 2 + m2, :], w[a][:, o:o + P], x[b][:, kt, :],
                                                     start=k == 0, stop=k == 5)
                                k += 1
                        m.then_inc(q_ps, 1)
                    for j in range(TC):
                        k = 0
                        for kt in range(KT):
                            for a, b in PARTS:
                                o = OFF_KV + kt * 2 * D
                                m = nc.tensor.matmul(ps[:, 4 + j, :], x[a][:, kt, j * P:(j + 1) * P], w[b][:, o:o + 2 * D],
                                                     start=k == 0, stop=k == 5)
                                k += 1
                        m.then_inc(kv_ps, 1)

                    def gate_up(i):
                        bank = 2 + 2 * (i % 3)
                        if i == 0:
                            pe.wait_ge(qs_rdy, FROM + n * KT + KT)
                        elif i < 3:
                            pe.wait_ge(kvs_rdy, FROM + n * TC + 2 * i)
                        else:
                            pe.wait_ge(h_rdy, FROM + n * NI0 + i - 2)
                        for g in range(2):
                            k = 0
                            for kt in range(KT):
                                for a, b in PARTS:
                                    o = OFF_GU + ((i * 2 + g) * KT + kt) * P
                                    m = nc.tensor.matmul(ps[:, bank + g, :], w[a][:, o:o + P], x[b][:, kt, :],
                                                         start=k == 0, stop=k == 5)
                                    k += 1
                            m.then_inc(gu_ps, 1)

                    for i in range(4):
                        gate_up(i)
                    pe.wait_ge(f_hi, FROM + n * 2 + 2)
                    pe.wait_ge(f_lo, FROM + n * 2 + 2)
                    pe.wait_ge(vh_rdy, FROM + n + 1)
                    pe.wait_ge(vl_rdy, FROM + n + 1)
                    for m2 in range(KT):
                        k = 0
                        for j in range(TC):
                            for a, b in PARTS:
                                m = nc.tensor.matmul(ps[:, 0, m2 * (P + 2):(m2 + 1) * (P + 2)],
                                                     kf[a][:, j, m2 * P:(m2 + 1) * P], v[b][:, j, m2, :],
                                                     start=k == 0, stop=k == 3 * TC - 1)
                                k += 1
                    m.then_inc(kva_ps, 1)
                    for i in range(4, NI0):
                        gate_up(i)
                    pe.wait_ge(kva_add, FROM + n + 1)
                    for s in range(SG):
                        pe.wait_ge(hs_hi, FROM + n * SG + s + 1)
                        pe.wait_ge(hs_lo, FROM + n * SG + s + 1)
                        if s:
                            pe.wait_ge(y_add, FROM + n * SG + s)
                        for t in range(TC):
                            k = 0
                            for j in range(4):
                                for a, b in PARTS:
                                    o = OFF_DN + (s * 4 + j) * D
                                    m = nc.tensor.matmul(ps[:, t // 2, (t % 2) * D:(t % 2 + 1) * D],
                                                         hs[a][:, j, t * P:(t + 1) * P], w[b][:, o:o + D],
                                                         start=k == 0, stop=k == 11)
                                    k += 1
                        m.then_inc(y_ps, 1)

            @block.scalar
            def _(act):
                with act.Fori(0, NCH) as n:
                    act.wait_ge(gu_ps, FROM + n * 2 * NI0)
                    for kt in range(KT):
                        act.wait_ge(xT_ps, FROM + n * KT + kt + 1)
                        nc.scalar.activation(xh[:, kt, :], ps[:, kt, :], ACT.Copy).then_inc(xh_rdy, 1)
                    act.wait_ge(qs_rdy, FROM + n * KT + KT)
                    act.wait_ge(win_rdy, FROM + n * SG * 3)
                    nc.scalar.activation(feat(0, rel), qpre, ACT.Relu).then_inc(rel_rdy, 1)
                    act.wait_ge(kvs_rdy, FROM + n * TC + TC)
                    nc.scalar.activation(feat(1, rel).rearrange("p (a b) -> p a b", a=TC), kpre, ACT.Relu).then_inc(rel_rdy, 1)
                    act.wait_ge(kva_ps, FROM + n)
                    nc.scalar.activation(vh[:, :, :, 0:P], kvs[:, :, D:2 * D].rearrange("p a (m e) -> p a m e", m=KT),
                                         ACT.Copy).then_inc(vh_rdy, 1)
                    for s in range(2):
                        act.wait_ge(mn_rdy, FROM + n * 2 + s + 1)
                        nc.scalar.activation(feat(s, mn), feat(s, mn), ACT.Exp).then_inc(ex_rdy, 1)
                    act.wait_ge(kva_ps, FROM + n)
                    for s in range(2):
                        act.wait_ge(f_rdy, FROM + n * 2 + s + 1)
                        f, hi, lo = feature(s, n)
                        nc.scalar.activation(hi, f, ACT.Copy).then_inc(f_hi, 1)
                    for i in range(NI0):
                        act.wait_ge(gu_ps, FROM + n * 2 * NI0 + 2 * i + 1)
                        if i >= 2:
                            act.wait_ge(h_rdy, FROM + n * NI0 + i - 1)
                        else:
                            act.wait_ge(h_rdy, FROM + n * NI0)
                        nc.scalar.activation(th[:, i % 2, :], ps[:, 2 + 2 * (i % 3), :], ACT.Tanh, scale=0.5).then_inc(th_rdy, 1)
                        if i % 4 == 3:
                            s = i // 4
                            act.wait_ge(h_rdy, FROM + n * NI0 + i + 1)
                            act.wait_ge(win_rdy, FROM + (n * SG + s) * 3)
                            act.wait_ge(f_rdy, FROM + n * 2 + 2)
                            nc.scalar.activation(ab[:], hh32[:], ACT.Abs).then_inc(ab_rdy, 1)
                            act.wait_ge(hm_rdy, FROM + (n * SG + s) * 4 + 4)
                            act.wait_ge(y_ps, FROM + n * SG + s)
                            nc.scalar.activation(hsh[:], hh32[:], ACT.Copy).then_inc(hs_hi, 1)

            @block.gpsimd
            def _(pool):
                with pool.Fori(0, NCH) as n:
                    for s in range(2):
                        pool.wait_ge(ex_rdy, FROM + n * 2 + s + 1)
                        pool.wait_ge(rel_rdy, FROM + n * 2 + s + 1)
                        nc.gpsimd.tensor_tensor(feat(s, mn), feat(s, mn), feat(s, rel), ALU.add).then_inc(f_rdy, 1)
                        f, hi, lo = feature(s, n)
                        pool.wait_ge(f_hi, FROM + n * 2 + s + 1)
                        nc.gpsimd.tensor_tensor(lo, f, hi.bitcast(F32), ALU.subtract).then_inc(f_lo, 1)

            @block.vector
            def _(dve):
                with dve.Fori(0, NCH) as n:
                    dve.wait_ge(mn_rdy, FROM + n * 2)
                    dve.wait_ge(rel_rdy, FROM + n * 2)
                    for j in range(TC):
                        t = n * TC + j
                        nc.vector.tensor_scalar(xn[:, j, :], acc[:, bass.ds(t, 1), :].rearrange("p a b -> p (a b)"),
                                                mv[:, bass.ds(t, 1), 0:1].rearrange("p a b -> p (a b)"), rstd[:, bass.ds(t, 1)],
                                                ALU.subtract, ALU.mult).then_inc(xn_rdy, 1)
                    for kt in range(KT):
                        dve.wait_ge(xh_rdy, FROM + n * KT + kt + 1)
                        nc.vector.tensor_tensor(xl[:, kt, :], ps[:, kt, :], xh[:, kt, :].bitcast(F32), ALU.subtract).then_inc(xl_rdy, 1)
                    for m2 in range(KT):
                        dve.wait_ge(q_ps, FROM + n * KT + m2 + 1)
                        nc.vector.tensor_scalar(qs[:, m2, :], ps[:, 2 + m2, :], bqc[:, m2:m2 + 1], None, ALU.add).then_inc(qs_rdy, 1)
                    dve.wait_ge(f_lo, FROM + n * 2)
                    dve.wait_ge(hm_rdy, FROM + n * SG * 4)
                    dve.wait_ge(qs_rdy, FROM + n * KT + KT)
                    nc.vector.tensor_scalar(feat(0, mn), qpre, 0.0, None, ALU.min).then_inc(mn_rdy, 1)
                    dve.wait_ge(vh_rdy, FROM + n)
                    dve.wait_ge(vl_rdy, FROM + n)
                    for j in range(TC):
                        dve.wait_ge(kv_ps, FROM + n * TC + j + 1)
                        nc.vector.tensor_tensor(kvs[:, j, :], ps[:, 4 + j, :], bkv[:], ALU.add).then_inc(kvs_rdy, 1)
                    dve.wait_ge(kvs_rdy, FROM + n * TC + TC)
                    nc.vector.tensor_scalar(feat(1, mn).rearrange("p (a b) -> p a b", a=TC), kpre, 0.0, None, ALU.min).then_inc(mn_rdy, 1)
                    dve.wait_ge(vh_rdy, FROM + n + 1)
                    nc.vector.tensor_tensor(vl[:, :, :, 0:P], kvs[:, :, D:2 * D].rearrange("p a (m e) -> p a m e", m=KT),
                                            vh[:, :, :, 0:P].bitcast(F32), ALU.subtract).then_inc(vl_rdy, 1)
                    for i in range(NI0):
                        s = i // 4
                        u = n * NI0 + i
                        bank = 2 + 2 * (i % 3)
                        dve.wait_ge(th_rdy, FROM + u + 1)
                        nc.vector.scalar_tensor_tensor(th[:, i % 2, :], th[:, i % 2, :], 1.0, ps[:, bank, :],
                                                       ALU.add, ALU.mult).then_inc(s_rdy, 1)
                        dve.wait_ge(s_rdy, FROM + u + 1)
                        dve.wait_ge(gu_ps, FROM + 2 * u + 2)
                        dve.wait_ge(hs_lo, FROM + n * SG + s)
                        nc.vector.scalar_tensor_tensor(hh32[:, i % 4, :], th[:, i % 2, :], 0.5, ps[:, bank + 1, :],
                                                       ALU.mult, ALU.mult).then_inc(h_rdy, 1)
                        if i % 4 != 3:
                            continue
                        g = n * SG + s
                        dve.wait_ge(ab_rdy, FROM + g + 1)
                        dve.wait_ge(hm_rdy, FROM + g * 4)
                        for a, nb, o in ((0, 3, 0), (1, 2, 3), (2, 1, 5)):
                            nc.vector.tensor_tensor(win[:, o:o + nb, :], ab[:, a:a + 1, :].broadcast_to([P, nb, CH]),
                                                    ab[:, a + 1:4, :], ALU.is_ge).then_inc(win_rdy, 1)
                        dve.wait_ge(win_rdy, FROM + g * 3 + 3)
                        dve.wait_ge(f_lo, FROM + n * 2 + 2)
                        plan = ((0, 1, ALU.add, 2, ALU.add, 2.0, ALU.is_ge), (3, 4, ALU.add, 0, ALU.subtract, 1.0, ALU.is_ge),
                                (5, 1, ALU.subtract, 3, ALU.subtract, 0.0, ALU.is_ge), (2, 4, ALU.add, 5, ALU.add, 1.0, ALU.is_le))
                        for k, (a, b, op, c, op2, lim, cmp) in enumerate(plan):
                            nc.vector.tensor_tensor(cnt[:, k, :], win[:, a, :], win[:, b, :], op).then_inc(cnt_rdy, 1)
                        for k, (a, b, op, c, op2, lim, cmp) in enumerate(plan):
                            dve.wait_ge(cnt_rdy, FROM + g * 8 + k + 1)
                            nc.vector.tensor_tensor(cnt[:, k, :], cnt[:, k, :], win[:, c, :], op2).then_inc(cnt_rdy, 1)
                        for k, (a, b, op, c, op2, lim, cmp) in enumerate(plan):
                            dve.wait_ge(cnt_rdy, FROM + g * 8 + k + 5)
                            nc.vector.scalar_tensor_tensor(hh32[:, k, :], cnt[:, k, :], lim, hh32[:, k, :], cmp, ALU.mult).then_inc(hm_rdy, 1)
                        dve.wait_ge(hs_hi, FROM + g + 1)
                        nc.vector.tensor_tensor(hsl[:], hh32[:], hsh[:].bitcast(F32), ALU.subtract).then_inc(hs_lo, 1)
                        if s == 0:
                            dve.wait_ge(kva_ps, FROM + n + 1)
                            kv = kvacc[:].rearrange("p a b -> p (a b)")
                            nc.vector.tensor_tensor(kv, kv, ps[:, 0, 0:KT * (P + 2)], ALU.add).then_inc(kva_add, 1)
                    for s in range(SG):
                        dve.wait_ge(y_ps, FROM + n * SG + s + 1)
                        if s:
                            dve.wait_ge(y_add, FROM + n * SG + s)
                        a = acc[:, bass.ds(n * TC, TC), :].rearrange("p a b -> p (a b)")
                        nc.vector.tensor_tensor(a, a, ps[:, 0:2, :].rearrange("p a b -> p (a b)"), ALU.add).then_inc(y_add, 1)


def layer0_out(nc, acc, qfh, qfl, ps, mv, rstd, wh, wl, bo, bd, kvacc, sems, sbuf):
    with ExitStack() as st:
        kz = sbuf(st, "kz", [P, 4, P], F32)
        kzh = sbuf(st, "kzh", [P, 4, P], FR)
        kzl = sbuf(st, "kzl", [P, 4, P], FR)
        den = sbuf(st, "den", [P, KT, CH], F32)
        at = sbuf(st, "at", [P, KT, CH], F32)
        ath = sbuf(st, "ath", [P, KT, CH], FR)
        atl = sbuf(st, "atl", [P, KT, CH], FR)
        bst = sbuf(st, "bst1", [P, NT, 6], F32)
        kzs, qf, ats, w = (kzh, kzl), (qfh, qfl), (ath, atl), (wh, wl)
        (kz_rdy, kz_hi, kz_lo, nd_ps, den_rdy, rec_rdy, at_rdy, at_hi, at_lo, o_ps, o_add, ob_add, bs_rdy, ag_rdy, sd) = [sems["b_" + s] for s in SEMS["b"]]
        with nc.Block() as block:
            @block.tensor
            def _(pe):
                pe.wait_ge(kz_lo, FROM + 1)
                with pe.Fori(0, NCH) as n:
                    pe.wait_ge(at_rdy, FROM + n * KT)
                    for m2 in range(KT):
                        for z in range(2):
                            for k, (a, b) in enumerate(PARTS):
                                m = nc.tensor.matmul(ps[:, 2 * m2 + z, :], kzs[a][:, 2 * z + m2, :],
                                                     qf[b][:, m2, bass.ds(n * CH, CH)], start=k == 0, stop=k == 2)
                            m.then_inc(nd_ps, 1)
                    pe.wait_ge(at_hi, FROM + n * KT + KT)
                    pe.wait_ge(at_lo, FROM + n * KT + KT)
                    pe.wait_ge(o_add, FROM + n)
                    for t in range(TC):
                        k = 0
                        for m2 in range(KT):
                            for a, b in PARTS:
                                o = OFF_O + m2 * D
                                m = nc.tensor.matmul(ps[:, 4 + t // 2, (t % 2) * D:(t % 2 + 1) * D],
                                                     ats[a][:, m2, t * P:(t + 1) * P], w[b][:, o:o + D], start=k == 0, stop=k == 5)
                                k += 1
                    m.then_inc(o_ps, 1)

            @block.scalar
            def _(act):
                act.wait_ge(kz_rdy, FROM + 4)
                nc.scalar.activation(kzh[:], kz[:], ACT.Copy).then_inc(kz_hi, 1)
                with act.Fori(0, NCH) as n:
                    act.wait_ge(o_ps, FROM + n)
                    for m2 in range(KT):
                        act.wait_ge(at_rdy, FROM + n * KT + m2 + 1)
                        nc.scalar.activation(ath[:, m2, :], at[:, m2, :], ACT.Copy).then_inc(at_hi, 1)
                act.wait_ge(sd, FROM + 1)
                nc.scalar.activation(rstd[:], rstd[:], ACT.Sqrt).then_inc(sd, 1)

            @block.gpsimd
            def _(pool):
                with pool.Fori(0, NCH) as n:
                    pool.wait_ge(o_add, FROM + n + 1)
                    a = acc[:, bass.ds(n * TC, TC), :]
                    nc.gpsimd.tensor_tensor(a, a, bo[:].unsqueeze(1).broadcast_to([P, TC, D]), ALU.add).then_inc(ob_add, 1)

            @block.vector
            def _(dve):
                for m2 in range(KT):
                    nc.vector.tensor_tensor(kz[:, m2, :], kvacc[:, m2, 0:P], bd[:], ALU.mult).then_inc(kz_rdy, 1)
                    nc.vector.tensor_scalar(kz[:, 2 + m2, :], bd[:], kvacc[:, m2, P:P + 1], None, ALU.mult).then_inc(kz_rdy, 1)
                dve.wait_ge(kz_hi, FROM + 1)
                nc.vector.tensor_tensor(kzl[:], kz[:], kzh[:].bitcast(F32), ALU.subtract).then_inc(kz_lo, 1)
                with dve.Fori(0, NCH) as n:
                    dve.wait_ge(at_hi, FROM + n * KT)
                    dve.wait_ge(at_lo, FROM + n * KT)
                    for m2 in range(KT):
                        u = n * KT + m2
                        dve.wait_ge(nd_ps, FROM + 2 * u + 2)
                        nc.vector.tensor_scalar(den[:, m2, :], ps[:, 2 * m2 + 1, :], 1e-6, None, ALU.add).then_inc(den_rdy, 1)
                        dve.wait_ge(den_rdy, FROM + u + 1)
                        nc.vector.reciprocal(den[:, m2, :], den[:, m2, :]).then_inc(rec_rdy, 1)
                        dve.wait_ge(rec_rdy, FROM + u + 1)
                        nc.vector.tensor_tensor(at[:, m2, :], den[:, m2, :], ps[:, 2 * m2, :], ALU.mult).then_inc(at_rdy, 1)
                        dve.wait_ge(at_hi, FROM + u + 1)
                        nc.vector.tensor_tensor(atl[:, m2, :], at[:, m2, :], ath[:, m2, :].bitcast(F32), ALU.subtract).then_inc(at_lo, 1)
                    dve.wait_ge(o_ps, FROM + n + 1)
                    a = acc[:, bass.ds(n * TC, TC), :].rearrange("p a b -> p (a b)")
                    nc.vector.tensor_tensor(a, a, ps[:, 4:6, :].rearrange("p a b -> p (a b)"), ALU.add).then_inc(o_add, 1)
                    dve.wait_ge(ob_add, FROM + n + 1)
                    for t in range(TC):
                        nc.vector.bn_stats(bst[:, bass.ds(n * TC + t, 1), :], acc[:, bass.ds(n * TC + t, 1), :]).then_inc(bs_rdy, 1)
                dve.wait_ge(bs_rdy, FROM + NT)
                for i in range(NT):
                    nc.vector.bn_aggr(mv[:, i, :], bst[:, i, :]).then_inc(ag_rdy, 1)
                dve.wait_ge(ag_rdy, FROM + NT)
                nc.vector.tensor_scalar(rstd[:], mv[:, :, 1], 1e-5, None, ALU.add).then_inc(sd, 1)
                dve.wait_ge(sd, FROM + 2)
                nc.vector.reciprocal(rstd[:], rstd[:]).then_inc(sd, 1)


def route(nc, d, acc, xTh, xTl, ident, cb, ps, mv, rstd, sem, sems, sbuf):
    G = 4
    with ExitStack() as st:
        wg = sbuf(st, "wg", [P, KT, E], F32)
        wgh = sbuf(st, "wgh", [P, KT, E], FR)
        wgl = sbuf(st, "wgl", [P, KT, E], FR)
        tie = sbuf(st, "tie", [P, E, E], F32)
        bo = sbuf(st, "bo1", [P, D], F32)
        xn = sbuf(st, "xn1", [P, TC, D], F32)
        xch = sbuf(st, "xch", [P, KT, CH], FR)
        xcl = sbuf(st, "xcl", [P, KT, CH], FR)
        m1 = sbuf(st, "m1", [P, TC], F32)
        ex = sbuf(st, "ex", [P, TC, E], F32)
        sc = sbuf(st, "sc", [P, TC, E], F32)
        gm = sbuf(st, "gm", [P, TC, G], F32)
        cg = sbuf(st, "cg", [P, 2, TC * G * G], F32)
        keep = sbuf(st, "keep", [P, TC, G], F32)
        mk = sbuf(st, "mk", [P, TC, E], F32)
        ce = sbuf(st, "ce", [P, 2, TC * E * E], F32)
        rk = sbuf(st, "rk", [P, TC, E], F32)
        xc, wgs = (xch, xcl), (wgh, wgl)
        (wg_in, wg_hi, wg_lo, xn_rdy, xT_ps, xc_hi, xc_lo, xs_hi, xs_lo, lg_ps, mx_rdy, ex_rdy,
         v_rdy, c_rdy, bo_add) = [sems["r_" + s] for s in SEMS["r"]]
        with nc.Block() as block:
            @block.sync
            def _(sp):
                sp.dma_start(wg[:], d["wg"]).then_inc(wg_in, 16)
                sp.dma_start(tie[:].rearrange("p a b -> p (a b)"), d["tie"].partition_broadcast(P)).then_inc(wg_in, 16)
                sp.dma_start(bo[:], d["bo1"].partition_broadcast(P)).then_inc(wg_in, 16)

            @block.tensor
            def _(pe):
                pe.wait_ge(wg_hi, FROM + 1)
                pe.wait_ge(wg_lo, FROM + 1)
                with pe.Fori(0, NCH) as n:
                    pe.wait_ge(xc_lo, FROM + n * KT)
                    for kt in range(KT):
                        for j in range(TC):
                            pe.wait_ge(xn_rdy, FROM + n * TC + j + 1)
                            m = nc.tensor.transpose(ps[:, kt, j * P:(j + 1) * P], xn[:, j, kt * P:(kt + 1) * P], ident[:])
                        m.then_inc(xT_ps, 1)
                    pe.wait_ge(xc_lo, FROM + n * KT + KT)
                    pe.wait_ge(mx_rdy, FROM + n)
                    for t in range(TC):
                        k = 0
                        for kt in range(KT):
                            for a, b in PARTS:
                                m = nc.tensor.matmul(ps[:, 2, t * E:(t + 1) * E], xc[a][:, kt, t * P:(t + 1) * P], wgs[b][:, kt, :],
                                                     start=k == 0, stop=k == 5)
                                k += 1
                    m.then_inc(lg_ps, 1)

            @block.scalar
            def _(act):
                act.wait_ge(wg_in, FROM + 48)
                nc.scalar.activation(wgh[:], wg[:], ACT.Copy).then_inc(wg_hi, 1)
                with act.Fori(0, NCH) as n:
                    act.wait_ge(lg_ps, FROM + n)
                    act.wait_ge(xs_hi, FROM + n)
                    for kt in range(KT):
                        act.wait_ge(xT_ps, FROM + n * KT + kt + 1)
                        nc.scalar.activation(xch[:, kt, :], ps[:, kt, :], ACT.Copy).then_inc(xc_hi, 1)
                    act.wait_ge(mx_rdy, FROM + n + 1)
                    nc.scalar.activation(ex[:], ex[:], ACT.Exp).then_inc(ex_rdy, 1)

            @block.gpsimd
            def _(pool):
                pool.memset(cb[:, :, E:E + 1], 1.0)
                pool.wait_ge(wg_in, FROM + 48)
                with pool.Fori(0, NCH) as n:
                    pool.wait_ge(xn_rdy, FROM + n * TC + TC)
                    a = acc[:, bass.ds(n * TC, TC), :]
                    nc.gpsimd.tensor_tensor(a, a, bo[:].unsqueeze(1).broadcast_to([P, TC, D]), ALU.add).then_inc(bo_add, 1)

            @block.vector
            def _(dve):
                dve.wait_ge(wg_hi, FROM + 1)
                nc.vector.tensor_tensor(wgl[:], wg[:], wgh[:].bitcast(F32), ALU.subtract).then_inc(wg_lo, 1)
                with dve.Fori(0, NCH) as n:
                    dve.wait_ge(xT_ps, FROM + n * KT)
                    for j in range(TC):
                        t = n * TC + j
                        nc.vector.tensor_scalar(xn[:, j, :], acc[:, bass.ds(t, 1), :].rearrange("p a b -> p (a b)"),
                                                mv[:, bass.ds(t, 1), 0:1].rearrange("p a b -> p (a b)"), rstd[:, bass.ds(t, 1)],
                                                ALU.subtract, ALU.mult).then_inc(xn_rdy, 1)
                    dve.wait_ge(xs_lo, FROM + n)
                    for kt in range(KT):
                        dve.wait_ge(xc_hi, FROM + n * KT + kt + 1)
                        nc.vector.tensor_tensor(xcl[:, kt, :], ps[:, kt, :], xch[:, kt, :].bitcast(F32), ALU.subtract).then_inc(xc_lo, 1)
                    dve.wait_ge(xc_lo, FROM + n * KT + KT)
                    nc.vector.tensor_copy(xTl[:, :, bass.ds(n * CH, CH)], xcl[:].bitcast(F32)).then_inc(xs_lo, 1)
                    nc.vector.tensor_copy(xTh[:, :, bass.ds(n * CH, CH)], xch[:].bitcast(F32)).then_inc(xs_hi, 1)
                    lg = ps[:, 2, 0:TC * E].rearrange("p (t e) -> p t e", t=TC)
                    V = 16

                    def step(k, ins):
                        ins.then_inc(v_rdy, 1)
                        dve.wait_ge(v_rdy, FROM + n * V + k)

                    dve.wait_ge(lg_ps, FROM + n + 1)
                    step(1, nc.vector.tensor_reduce(m1[:], lg, AX.X, ALU.max))
                    nc.vector.tensor_tensor(ex[:], lg, m1[:].unsqueeze(2).broadcast_to([P, TC, E]), ALU.subtract).then_inc(mx_rdy, 1)
                    dve.wait_ge(ex_rdy, FROM + n + 1)
                    step(2, nc.vector.tensor_reduce(m1[:], ex[:], AX.X, ALU.add))
                    step(3, nc.vector.reciprocal(m1[:], m1[:]))
                    step(4, nc.vector.tensor_tensor(sc[:], ex[:], m1[:].unsqueeze(2).broadcast_to([P, TC, E]), ALU.mult))
                    step(5, nc.vector.tensor_reduce(gm[:], sc[:].rearrange("p t (g e) -> p t g e", g=G), AX.X, ALU.max))
                    row = gm[:].unsqueeze(3).broadcast_to([P, TC, G, G])
                    col = gm[:].unsqueeze(2).broadcast_to([P, TC, G, G])
                    c0, c1 = [cg[:, k, :].rearrange("p (t a b) -> p t a b", t=TC, a=G) for k in range(2)]
                    nc.vector.tensor_tensor(c0, col, row, ALU.is_gt).then_inc(c_rdy, 1)
                    step(6, nc.vector.tensor_tensor(c1, col, row, ALU.is_equal))
                    step(7, nc.vector.tensor_tensor(c1, c1, tie[:, 0:G, 0:G].unsqueeze(1).broadcast_to([P, TC, G, G]), ALU.mult))
                    dve.wait_ge(c_rdy, FROM + 2 * n + 1)
                    step(8, nc.vector.tensor_tensor(c0, c0, c1, ALU.add))
                    step(9, nc.vector.tensor_reduce(keep[:], c0, AX.X, ALU.add))
                    step(10, nc.vector.tensor_scalar(keep[:], keep[:], 2.0, None, ALU.is_lt))
                    kb = keep[:].unsqueeze(3).broadcast_to([P, TC, G, E // G])
                    step(11, nc.vector.tensor_tensor(mk[:].rearrange("p t (g e) -> p t g e", g=G),
                                                     sc[:].rearrange("p t (g e) -> p t g e", g=G), kb, ALU.mult))
                    step(12, nc.vector.scalar_tensor_tensor(
                        mk[:].rearrange("p t (g e) -> p (t g) e", g=G), kb.rearrange("p t g e -> p (t g) e"), -1.0,
                        mk[:].rearrange("p t (g e) -> p (t g) e", g=G), ALU.add, ALU.add))
                    row = mk[:].unsqueeze(3).broadcast_to([P, TC, E, E])
                    col = mk[:].unsqueeze(2).broadcast_to([P, TC, E, E])
                    e0, e1 = [ce[:, k, :].rearrange("p (t a b) -> p t a b", t=TC, a=E) for k in range(2)]
                    nc.vector.tensor_tensor(e0, col, row, ALU.is_gt).then_inc(c_rdy, 1)
                    step(13, nc.vector.tensor_tensor(e1, col, row, ALU.is_equal))
                    step(14, nc.vector.tensor_tensor(e1, e1, tie[:].unsqueeze(1).broadcast_to([P, TC, E, E]), ALU.mult))
                    dve.wait_ge(c_rdy, FROM + 2 * n + 2)
                    step(15, nc.vector.tensor_tensor(e0, e0, e1, ALU.add))
                    step(16, nc.vector.tensor_reduce(rk[:], e0, AX.X, ALU.add))
                    nc.vector.scalar_tensor_tensor(cb[:, bass.ds(n * TC, TC), 0:E], rk[:], 4.0, sc[:], ALU.is_lt, ALU.mult)


def attention(nc, d, acc, xTh, xTl, ident, ps, sem, sems, sbuf):
    NP = (T * NH) // (NH * P)
    CK = [-(-(i + 1) // TC) for i in range(NP)]
    PR = [-(-c // 2) for c in CK]
    cumc = [sum(CK[:i]) for i in range(NP + 1)]
    cump = [sum(PR[:i]) for i in range(NP + 1)]
    NC, NPR = cumc[NP], cump[NP]
    TWO = sum(p == 2 for p in PR)
    UN = 12
    BANK = [0, 1, 2, 3, 4, 5, 0, 1, 2, 3, 4, 5]
    WC = 2 * KT * HD + D
    RING = 3
    with ExitStack() as st:
        wqh = sbuf(st, "wqh", [P, KT, QC * HD], FR)
        wql = sbuf(st, "wql", [P, KT, QC * HD], FR)
        whh = sbuf(st, "whh", [P, WC], FR)
        whl = sbuf(st, "whl", [P, WC], FR)
        wst = sbuf(st, "wst", [P, WC], F32)
        kTh = sbuf(st, "kTh", [P, T], FR)
        kTl = sbuf(st, "kTl", [P, T], FR)
        v2 = sbuf(st, "v2", [P, NT, 2, HD], FR)
        qTh = sbuf(st, "qTh", [P, T], FR)
        qTl = sbuf(st, "qTl", [P, T], FR)
        pr = sbuf(st, "pr", [P, 2, T], F32)
        pth = sbuf(st, "pth", [P, RING, TC, P], FR)
        ptl = sbuf(st, "ptl", [P, RING, TC, P], FR)
        qb = sbuf(st, "qb", [P, 2, TC, P], F32)
        ob = sbuf(st, "ob", [P, 2, 2 * HD], F32)
        o32 = sbuf(st, "o32", [P, 2, HD], F32)
        oTh = sbuf(st, "oTh", [P, P], FR)
        oTl = sbuf(st, "oTl", [P, P], FR)
        yb = sbuf(st, "yb", [P, 2, D], F32)
        bq = sbuf(st, "bq", [P, QC], F32)
        bk = sbuf(st, "bk", [P, NH], F32)
        bv = sbuf(st, "bv", [P, NH], F32)
        bh = sbuf(st, "bh", [P, 2], F32)
        cz = sbuf(st, "cz", [P, P], F32)
        czb = sbuf(st, "czb", [P, P], BF16)
        idb = sbuf(st, "idb", [P, P], BF16)
        mx = sbuf(st, "mx", [P, 2, 2], F32)
        nb = sbuf(st, "nb", [P, 2], F32)
        rs = sbuf(st, "rs", [P, 2, 2], F32)
        ri = sbuf(st, "ri", [P, 2], F32)
        wq, wh, x = (wqh, wql), (whh, whl), (xTh, xTl)
        kT, qT, pt, oT = (kTh, kTl), (qTh, qTl), (pth, ptl), (oTh, oTl)
        WK, WV, WO = 0, KT * HD, 2 * KT * HD
        (wq_in, wq_hi, wq_lo, staged, wk_hi, wk_lo, wo_hi, wo_lo, pj_ps, q_rdy, q_hi, q_lo, pj_hi, pj_rd, s_ps, mx_s, nb_rdy,
         ex_rdy, rsum, rs_rdy, T_ps, pt_hi, pt_lo, pv_ps, ov_rdy, o_rdy, oT_ps, o_hi, o_lo, y_ps, yb_rdy, y_add, b_in, bh_rdy) = [
            sems["t_" + s] for s in SEMS["t"]]

        def qview(buf, cg):
            return buf[:].rearrange("p (t c) -> p c t", c=QC)[:, cg * TC:(cg + 1) * TC, :]

        def scores(i, c):
            return min(CH, (i + 1) * P - c * CH)

        def pair(i, q):
            return min(2 * CH, (i + 1) * P - q * 2 * CH)

        def group(a, g):
            return min(TC, a + 1 - g * TC)

        with nc.Block() as block:
            @block.sync
            def _(sp):
                sp.dma_start(wst[:], d["whead"][:, 0, :]).then_inc(staged, 16)
                for k in range(KT):
                    sp.dma_start(pr[:, k, :], d["wq"][:, k * T:(k + 1) * T]).then_inc(wq_in, 16)
                sp.dma_start(bq[:], d["bq1"]).then_inc(b_in, 16)
                sp.dma_start(bk[:], d["bk1"]).then_inc(b_in, 16)
                sp.dma_start(bv[:], d["bv1"]).then_inc(b_in, 16)
                sp.dma_start(cz[:], d["causal"]).then_inc(b_in, 16)
                with sp.Fori(0, NH) as h:
                    sp.wait_ge(wo_hi, FROM + h + 1)
                    sp.wait_ge(wo_lo, FROM + h + 1)
                    sp.dma_start(wst[:], d["whead"][:, bass.ds(h + 1, 1), :].rearrange("p a b -> p (a b)")).then_inc(staged, 16)
                sp.wait_ge(staged, FROM + 16 * (NH + 1))

            @block.tensor
            def _(pe):
                pe.wait_ge(wq_lo, FROM + KT)
                pe.wait_ge(b_in, FROM + 64 + 2)
                with pe.Fori(0, NH) as h:
                    pe.wait_ge(ex_rdy, FROM + h * NPR)
                    pe.wait_ge(wk_hi, FROM + h + 1)
                    pe.wait_ge(wk_lo, FROM + h + 1)
                    pe.wait_ge(pt_lo, FROM + h * NC)
                    for u in range(UN):
                        if 6 <= u < 10:
                            pe.wait_ge(q_rdy, FROM + h * 4 + u - 5)
                        elif u >= 10:
                            pe.wait_ge(pj_rd, FROM + h * 8 + u - 9)
                        kind, r = divmod(u, 4)
                        for j in range(TC if kind != 1 else 1):
                            k = 0
                            for kt in range(KT):
                                for a, b in PARTS:
                                    if kind == 0:
                                        c = r * TC + j
                                        l = wq[a][:, kt, c * HD:(c + 1) * HD]
                                        rr = x[b][:, kt, bass.ds(h * P, P)]
                                        o = ps[:, BANK[u], j * P:(j + 1) * P]
                                    elif kind == 1:
                                        l = wh[a][:, WK + kt * HD:WK + (kt + 1) * HD]
                                        rr = x[b][:, kt, r * CH:(r + 1) * CH]
                                        o = ps[:, BANK[u], :]
                                    else:
                                        t = r * TC + j
                                        l = x[a][:, kt, t * P:(t + 1) * P]
                                        rr = wh[b][:, WV + kt * HD:WV + (kt + 1) * HD]
                                        o = ps[:, BANK[u], j * P:(j + 1) * P]
                                    m = nc.tensor.matmul(o, l, rr, start=k == 0, stop=k == 5)
                                    k += 1
                        m.then_inc(pj_ps, 1)

                    def qk(i, c):
                        w = scores(i, c)
                        last = c == CK[i] - 1
                        for k, (a, b) in enumerate(PARTS):
                            m = nc.tensor.matmul(ps[:, c, 0:w], qT[a][:, i * P:(i + 1) * P], kT[b][:, c * CH:c * CH + w],
                                                 start=k == 0, stop=k == 2 and not last)
                        if last:
                            m = nc.tensor.matmul(ps[:, c, w - P:w], idb[:], czb[:], start=False, stop=True)
                        if last or c % 2:
                            m.then_inc(s_ps, 1)

                    def turn(a, g):
                        n = cumc[a] + g
                        if n >= 2:
                            pe.wait_ge(pt_lo, FROM + h * NC + n - 1)
                        if g == 0:
                            pe.wait_ge(ex_rdy, FROM + h * NPR + cump[a + 1])
                        for j in range(group(a, g)):
                            t = g * TC + j
                            m = nc.tensor.transpose(ps[:, 4 + n % 2, j * P:(j + 1) * P], pr[:, a % 2, t * P:(t + 1) * P], ident[:])
                        m.then_inc(T_ps, 1)

                    def pv(a, g):
                        n = cumc[a] + g
                        if g == 0:
                            pe.wait_ge(ov_rdy, FROM + h * NP + a)
                        pe.wait_ge(pt_lo, FROM + h * NC + n + 1)
                        for j in range(group(a, g)):
                            t = g * TC + j
                            nc.tensor.matmul(ps[:, 6, 0:2 * HD], pth[:, n % RING, j, :],
                                             v2[:, t, :, :].rearrange("p a b -> p (a b)"),
                                             start=t == 0, stop=False, skip_group_check=True)
                            m = nc.tensor.matmul(ps[:, 6, 0:HD], ptl[:, n % RING, j, :], v2[:, t, 0, :],
                                                 start=False, stop=t == a, skip_group_check=True)
                        m.then_inc(pv_ps, 1)

                    pe.wait_ge(pj_rd, FROM + h * 8 + 8)
                    pe.wait_ge(q_hi, FROM + 4 * h + 4)
                    pe.wait_ge(q_lo, FROM + 4 * h + 4)
                    qk(0, 0)
                    for i in range(NP + 2):
                        a, f, b = i - 1, i - 2, i + 1
                        has_a, has_f, has_b = 0 <= a < NP, 0 <= f < NP, b < NP
                        ga = CK[a] if has_a else 0
                        cbn = CK[b] if has_b else 0
                        for g in range(min(2, ga)):
                            turn(a, g)
                        if has_f:
                            pe.wait_ge(o_rdy, FROM + h * NP + f + 1)
                            pe.wait_ge(yb_rdy, FROM + h * NP + f)
                            nc.tensor.transpose(ps[:, 7, 0:P], o32[:, f % 2, :], ident[:]).then_inc(oT_ps, 1)
                        for g in range(2):
                            if g < ga:
                                pv(a, g)
                            if g + 2 < ga:
                                turn(a, g + 2)
                        for c in range(4):
                            if c < cbn:
                                if c % 2 == 0 and c < CK[i]:
                                    pe.wait_ge(ex_rdy, FROM + h * NPR + cump[i] + c // 2 + 1)
                                qk(b, c)
                            if c < 2 and c + 2 < ga:
                                pv(a, c + 2)
                            if c == 2 and has_f:
                                if f == 0:
                                    pe.wait_ge(wo_hi, FROM + h + 1)
                                    pe.wait_ge(wo_lo, FROM + h + 1)
                                pe.wait_ge(o_lo, FROM + h * NP + f + 1)
                                for k, (s, w) in enumerate(PARTS):
                                    m = nc.tensor.matmul(ps[:, 7, 0:D], oT[s][:], wh[w][:, WO:WO + D], start=k == 0, stop=k == 2)
                                m.then_inc(y_ps, 1)

            @block.scalar
            def _(act):
                for k in range(KT):
                    act.wait_ge(wq_in, FROM + 32)
                    nc.scalar.activation(wqh[:, k, :], pr[:, k, :], ACT.Copy).then_inc(wq_hi, 1)
                act.wait_ge(b_in, FROM + 64)
                nc.scalar.activation(czb[:], cz[:], ACT.Copy).then_inc(b_in, 1)
                nc.scalar.activation(idb[:], ident[:], ACT.Copy).then_inc(b_in, 1)
                act.wait_ge(staged, FROM + 16)
                nc.scalar.activation(whh[:, 0:WO], wst[:, 0:WO], ACT.Copy).then_inc(wk_hi, 1)
                with act.Fori(0, NH) as h:
                    act.wait_ge(y_ps, FROM + h * NP)
                    nc.scalar.activation(whh[:, WO:WC], wst[:, WO:WC], ACT.Copy).then_inc(wo_hi, 1)
                    nc.scalar.activation(bh[:, 0:1], bk[:, bass.ds(h, 1)], ACT.Copy).then_inc(bh_rdy, 1)
                    nc.scalar.activation(bh[:, 1:2], bv[:, bass.ds(h, 1)], ACT.Copy).then_inc(bh_rdy, 1)
                    act.wait_ge(bh_rdy, FROM + 2 * h + 2)
                    for u in range(UN):
                        kind, r = divmod(u, 4)
                        if kind == 0:
                            act.wait_ge(q_rdy, FROM + 4 * h + r + 1)
                            nc.scalar.activation(qview(qTh, r), qb[:, r % 2, :, :], ACT.Copy).then_inc(q_hi, 1)
                            continue
                        act.wait_ge(pj_ps, FROM + h * UN + u + 1)
                        if kind == 1:
                            nc.scalar.activation(kTh[:, r * CH:(r + 1) * CH], ps[:, BANK[u], :], ACT.Identity,
                                                 bias=bh[:, 0:1]).then_inc(pj_hi, 1)
                        else:
                            nc.scalar.activation(v2[:, r * TC:(r + 1) * TC, 0, :],
                                                 ps[:, BANK[u], :].rearrange("p (t e) -> p t e", t=TC), ACT.Copy).then_inc(pj_hi, 1)

                    def hi(a, g):
                        n = cumc[a] + g
                        w = group(a, g)
                        act.wait_ge(T_ps, FROM + h * NC + n + 1)
                        if n >= RING:
                            act.wait_ge(pv_ps, FROM + h * NC + n - RING + 1)
                        else:
                            act.wait_ge(pv_ps, FROM + h * NC)
                        nc.scalar.activation(pth[:, n % RING, 0:w, :], ps[:, 4 + n % 2, 0:w * P].rearrange("p (t e) -> p t e", t=w),
                                             ACT.Copy).then_inc(pt_hi, 1)

                    def exps(i, q):
                        w = pair(i, q)
                        if q == 0:
                            act.wait_ge(nb_rdy, FROM + h * NP + i + 1)
                            if i >= 2:
                                act.wait_ge(T_ps, FROM + h * NC + cumc[i - 1])
                                act.wait_ge(rs_rdy, FROM + h * NP + i - 1)
                            else:
                                act.wait_ge(T_ps, FROM + h * NC)
                                act.wait_ge(rs_rdy, FROM + h * NP)
                        nc.scalar.activation(pr[:, i % 2, q * 2 * CH:q * 2 * CH + w],
                                             ps[:, 2 * q:2 * q + 2, :].rearrange("p a b -> p (a b)")[:, 0:w], ACT.Exp,
                                             bias=nb[:, i % 2:i % 2 + 1], scale=SCALE,
                                             accum_out=rs[:, i % 2, q:q + 1]).then_inc(ex_rdy, 1)

                    for i in range(NP + 2):
                        a, f = i - 1, i - 2
                        has_a, has_f, has_i = 0 <= a < NP, 0 <= f < NP, i < NP
                        ga = CK[a] if has_a else 0
                        for g in range(min(2, ga)):
                            hi(a, g)
                        if has_i:
                            exps(i, 0)
                        if has_f:
                            act.wait_ge(oT_ps, FROM + h * NP + f + 1)
                            if f:
                                act.wait_ge(y_ps, FROM + h * NP + f)
                            nc.scalar.activation(oTh[:], ps[:, 7, 0:P], ACT.Identity, bias=bh[:, 1:2]).then_inc(o_hi, 1)
                        for g in range(2, ga):
                            hi(a, g)
                        if has_i and PR[i] == 2:
                            exps(i, 1)
                        if i == 8:
                            act.wait_ge(staged, FROM + 16 * h + 32)
                            nc.scalar.activation(whh[:, 0:WO], wst[:, 0:WO], ACT.Copy).then_inc(wk_hi, 1)
                        if has_a:
                            act.wait_ge(pv_ps, FROM + h * NC + cumc[a + 1])
                            act.wait_ge(rs_rdy, FROM + h * NP + a + 1)
                            act.wait_ge(o_rdy, FROM + h * NP + max(a - 1, 0))
                            nc.scalar.activation(ob[:, a % 2, :], ps[:, 6, 0:2 * HD], ACT.Copy, scale=ri[:, a % 2:a % 2 + 1]).then_inc(ov_rdy, 1)
                        if has_f:
                            act.wait_ge(y_ps, FROM + h * NP + f + 1)
                            act.wait_ge(y_add, FROM + h * NP + max(f - 1, 0))
                            nc.scalar.activation(yb[:, f % 2, :], ps[:, 7, 0:D], ACT.Copy).then_inc(yb_rdy, 1)

            @block.gpsimd
            def _(pool):
                pool.wait_ge(wk_hi, FROM + 1)
                nc.gpsimd.tensor_tensor(whl[:, 0:WO], wst[:, 0:WO], whh[:, 0:WO].bitcast(F32), ALU.subtract).then_inc(wk_lo, 1)
                with pool.Fori(0, NH) as h:
                    pool.wait_ge(wo_hi, FROM + h + 1)
                    nc.gpsimd.tensor_tensor(whl[:, WO:WC], wst[:, WO:WC], whh[:, WO:WC].bitcast(F32), ALU.subtract).then_inc(wo_lo, 1)
                    for r in range(4):
                        pool.wait_ge(q_hi, FROM + 4 * h + r + 1)
                        nc.gpsimd.tensor_tensor(qview(qTl, r), qb[:, r % 2, :, :], qview(qTh, r).bitcast(F32), ALU.subtract).then_inc(q_lo, 1)
                    for i in range(1, NP + 2):
                        a, f = i - 1, i - 2
                        if a < NP:
                            pool.wait_ge(ov_rdy, FROM + h * NP + a + 1)
                            pool.wait_ge(oT_ps, FROM + h * NP + max(a - 1, 0))
                            nc.gpsimd.tensor_tensor(o32[:, a % 2, :], ob[:, a % 2, 0:HD], ob[:, a % 2, HD:2 * HD], ALU.add).then_inc(o_rdy, 1)
                        if i == 8:
                            pool.wait_ge(wk_hi, FROM + h + 2)
                            nc.gpsimd.tensor_tensor(whl[:, 0:WO], wst[:, 0:WO], whh[:, 0:WO].bitcast(F32), ALU.subtract).then_inc(wk_lo, 1)
                        if f >= 0:
                            pool.wait_ge(yb_rdy, FROM + h * NP + f + 1)
                            pool.wait_ge(y_add, FROM + h * NP + f)
                            nc.gpsimd.tensor_tensor(acc[:, f, :], acc[:, f, :], yb[:, f % 2, :], ALU.add).then_inc(y_add, 1)

            @block.vector
            def _(dve):
                for k in range(KT):
                    dve.wait_ge(wq_hi, FROM + k + 1)
                    nc.vector.tensor_tensor(wql[:, k, :], pr[:, k, :], wqh[:, k, :].bitcast(F32), ALU.subtract).then_inc(wq_lo, 1)
                dve.wait_ge(b_in, FROM + 64)
                with dve.Fori(0, NH) as h:
                    for u in range(UN):
                        kind, r = divmod(u, 4)
                        if kind == 0:
                            dve.wait_ge(pj_ps, FROM + h * UN + u + 1)
                            dve.wait_ge(q_lo, FROM + 4 * h + max(r - 1, 0))
                            nc.vector.tensor_tensor(qb[:, r % 2, :, :], ps[:, BANK[u], :].rearrange("p (c t) -> p c t", c=TC),
                                                    bq[:, r * TC:(r + 1) * TC].unsqueeze(2).broadcast_to([P, TC, P]),
                                                    ALU.add).then_inc(q_rdy, 1)
                            continue
                        dve.wait_ge(pj_hi, FROM + h * 8 + u - 3)
                        if kind == 1:
                            s = slice(r * CH, (r + 1) * CH)
                            nc.vector.scalar_tensor_tensor(kTl[:, s], ps[:, BANK[u], :], bh[:, 0:1], kTh[:, s].bitcast(F32),
                                                           ALU.add, ALU.subtract).then_inc(pj_rd, 1)
                        else:
                            nc.vector.tensor_tensor(v2[:, r * TC:(r + 1) * TC, 1, :], ps[:, BANK[u], :].rearrange("p (t e) -> p t e", t=TC),
                                                    v2[:, r * TC:(r + 1) * TC, 0, :].bitcast(F32), ALU.subtract).then_inc(pj_rd, 1)

                    def maxima(i):
                        for q in range(PR[i]):
                            dve.wait_ge(s_ps, FROM + h * NPR + cump[i] + q + 1)
                            nc.vector.tensor_reduce(mx[:, i % 2, q:q + 1], ps[:, 2 * q:2 * q + 2, :].rearrange("p a b -> p (a b)")[:, 0:pair(i, q)],
                                                    AX.X, ALU.max).then_inc(mx_s, 1)
                        dve.wait_ge(mx_s, FROM + h * NPR + cump[i + 1])
                        if PR[i] == 2:
                            nc.vector.tensor_scalar(nb[:, i % 2:i % 2 + 1], mx[:, i % 2, 0:1], mx[:, i % 2, 1:2], -SCALE,
                                                    ALU.max, ALU.mult).then_inc(nb_rdy, 1)
                        else:
                            nc.vector.tensor_scalar(nb[:, i % 2:i % 2 + 1], mx[:, i % 2, 0:1], -SCALE, None, ALU.mult).then_inc(nb_rdy, 1)

                    def lo(a, g):
                        n = cumc[a] + g
                        w = group(a, g)
                        dve.wait_ge(pt_hi, FROM + h * NC + n + 1)
                        nc.vector.tensor_tensor(ptl[:, n % RING, 0:w, :], ps[:, 4 + n % 2, 0:w * P].rearrange("p (t e) -> p t e", t=w),
                                                pth[:, n % RING, 0:w, :].bitcast(F32), ALU.subtract).then_inc(pt_lo, 1)

                    maxima(0)
                    for i in range(NP + 2):
                        a, f, b = i - 1, i - 2, i + 1
                        has_a, has_f = 0 <= a < NP, 0 <= f < NP
                        ga = CK[a] if has_a else 0
                        if has_a:
                            dve.wait_ge(ex_rdy, FROM + h * NPR + cump[a + 1])
                            src = rs[:, a % 2, 0:1]
                            if PR[a] == 2:
                                nc.vector.tensor_tensor(src, src, rs[:, a % 2, 1:2], ALU.add).then_inc(rsum, 1)
                                dve.wait_ge(rsum, FROM + h * TWO + a - (NP - TWO) + 1)
                            dve.wait_ge(ov_rdy, FROM + h * NP + max(a - 1, 0))
                            nc.vector.reciprocal(ri[:, a % 2:a % 2 + 1], src).then_inc(rs_rdy, 1)
                        for g in range(min(2, ga)):
                            lo(a, g)
                        if has_f:
                            dve.wait_ge(o_hi, FROM + h * NP + f + 1)
                            nc.vector.scalar_tensor_tensor(oTl[:], ps[:, 7, 0:P], bh[:, 1:2], oTh[:].bitcast(F32),
                                                           ALU.add, ALU.subtract).then_inc(o_lo, 1)
                        for g in range(2, ga):
                            lo(a, g)
                        if b < NP:
                            maxima(b)


def experts(nc, d, acc, xTh, xTl, ident, cb, ps, sem, sems, sbuf):
    RING = 3
    U = NCH * GT
    W1, W3, W2, SEL = 0, KT * P, 2 * KT * P, GW
    TWC = GW + P
    LAG = 2
    with ExitStack() as st:
        wst = sbuf(st, "est", [P, GT, TWC], F32)
        wh = sbuf(st, "ewh", [P, GT, TWC], FR)
        wl = sbuf(st, "ewl", [P, GT, TWC], FR)
        cT32 = sbuf(st, "cT32", [P, TC, P], F32)
        cTh = sbuf(st, "cTh", [P, T], FR)
        cTl = sbuf(st, "cTl", [P, T], FR)
        th = sbuf(st, "eth", [P, 2, CH], F32)
        h32 = sbuf(st, "eh32", [P, 3, CH], F32)
        hh = sbuf(st, "ehh", [P, RING, CH], FR)
        hl = sbuf(st, "ehl", [P, RING, CH], FR)
        w, x, c, hp = (wh, wl), (xTh, xTl), (cTh, cTl), (hh, hl)
        (cp, cT_ps, ct_hi, ct_lo, w_in, w_hi, w_lo, g_ps, u_ps, c_ps, th_rdy, s_rdy, h_rdy, hc_rdy, h_hi, h_lo, y_ps, y_add) = [
            sems["e_" + s] for s in SEMS["e"]]

        with nc.Block() as block:
            @block.sync
            def _(sp):
                sp.dma_start(wst[:], d["wexp"][:, 0:GT, :]).then_inc(w_in, 16)
                with sp.Fori(1, NG) as g:
                    sp.wait_ge(w_hi, FROM + g * GT)
                    sp.wait_ge(w_lo, FROM + g * GT)
                    sp.dma_start(wst[:], d["wexp"][:, bass.ds(g * GT, GT), :]).then_inc(w_in, 16)

            @block.tensor
            def _(pe):
                for n in range(NCH):
                    pe.wait_ge(cp, FROM + n + 2)
                    if n:
                        pe.wait_ge(ct_lo, FROM + n)
                    for j in range(TC):
                        m = nc.tensor.transpose(ps[:, 0, j * P:(j + 1) * P], cT32[:, j, :], ident[:])
                    m.then_inc(cT_ps, 1)
                pe.wait_ge(ct_lo, FROM + NCH)
                with pe.Fori(0, NG) as g:
                    def up(u):
                        ch, k = divmod(u, GT)
                        if ch == 0:
                            pe.wait_ge(w_hi, FROM + g * GT + k + 1)
                            pe.wait_ge(w_lo, FROM + g * GT + k + 1)
                        if u >= 2:
                            pe.wait_ge(hc_rdy, FROM + g * U + u - 1)
                        else:
                            pe.wait_ge(hc_rdy, FROM + g * U)
                        bank = 3 * (u % 2)
                        for z, (col, s) in enumerate(((W1, g_ps), (W3, u_ps))):
                            i = 0
                            for kt in range(KT):
                                for a, b in PARTS:
                                    m = nc.tensor.matmul(ps[:, bank + z, :], w[a][:, k, col + kt * P:col + (kt + 1) * P],
                                                         x[b][:, kt, ch * CH:(ch + 1) * CH], start=i == 0, stop=i == 5)
                                    i += 1
                            m.then_inc(s, 1)
                        for i in range(2):
                            m = nc.tensor.matmul(ps[:, bank + 2, :], wh[:, k, SEL:SEL + P], c[i][:, ch * CH:(ch + 1) * CH],
                                                 start=i == 0, stop=i == 1)
                        m.then_inc(c_ps, 1)

                    def down(u):
                        ch, k = divmod(u, GT)
                        pe.wait_ge(h_lo, FROM + g * U + u + 1)
                        if k == 0:
                            pe.wait_ge(y_add, FROM + g * NCH + ch)
                        for t in range(TC):
                            for i, (a, b) in enumerate(PARTS):
                                m = nc.tensor.matmul(ps[:, 6 + t // 2, (t % 2) * D:(t % 2 + 1) * D],
                                                     hp[a][:, u % RING, t * P:(t + 1) * P], w[b][:, k, W2:W2 + D],
                                                     start=k == 0 and i == 0 and t % 2 == 0, stop=k == GT - 1 and i == 2,
                                                     skip_group_check=True)
                        m.then_inc(y_ps, 1)

                    for u in range(U + LAG):
                        if u < U:
                            up(u)
                        if u >= LAG:
                            down(u - LAG)

            @block.scalar
            def _(act):
                for n in range(NCH):
                    act.wait_ge(cT_ps, FROM + n + 1)
                    nc.scalar.activation(cTh[:, n * CH:(n + 1) * CH], ps[:, 0, :], ACT.Copy).then_inc(ct_hi, 1)

                with act.Fori(0, NG) as g:
                    act.wait_ge(w_in, FROM + 16 * g + 16)
                    for k in range(GT):
                        act.wait_ge(y_ps, FROM + g * U)
                        nc.scalar.activation(wh[:, k, :], wst[:, k, :], ACT.Copy).then_inc(w_hi, 1)

                    def split(u):
                        act.wait_ge(hc_rdy, FROM + g * U + u + 1)
                        if u >= RING:
                            act.wait_ge(y_ps, FROM + g * U + u - RING + 1)
                        nc.scalar.activation(hh[:, u % RING, :], h32[:, u % 3, :], ACT.Copy).then_inc(h_hi, 1)

                    for u in range(U + 1):
                        if u < U:
                            act.wait_ge(g_ps, FROM + g * U + u + 1)
                            act.wait_ge(h_rdy, FROM + g * U + max(u - 1, 0))
                            nc.scalar.activation(th[:, u % 2, :], ps[:, 3 * (u % 2), :], ACT.Tanh, scale=0.5).then_inc(th_rdy, 1)
                        if u:
                            split(u - 1)

            @block.gpsimd
            def _(pool):
                with pool.Fori(0, NG) as g:
                    for u in range(U):
                        pool.wait_ge(h_hi, FROM + g * U + u + 1)
                        nc.gpsimd.tensor_tensor(hl[:, u % RING, :], h32[:, u % 3, :], hh[:, u % RING, :].bitcast(F32),
                                                ALU.subtract).then_inc(h_lo, 1)

            @block.vector
            def _(dve):
                nc.vector.memset(cT32[:], 0.0).then_inc(cp, 1)
                dve.wait_ge(cp, FROM + 1)
                for n in range(NCH):
                    if n:
                        dve.wait_ge(cT_ps, FROM + n)
                    nc.vector.tensor_copy(cT32[:, :, 0:E + 1], cb[:, n * TC:(n + 1) * TC, :]).then_inc(cp, 1)
                    dve.wait_ge(ct_hi, FROM + n + 1)
                    nc.vector.tensor_tensor(cTl[:, n * CH:(n + 1) * CH], ps[:, 0, :], cTh[:, n * CH:(n + 1) * CH].bitcast(F32),
                                            ALU.subtract).then_inc(ct_lo, 1)
                with dve.Fori(0, NG) as g:
                    for k in range(GT):
                        dve.wait_ge(w_hi, FROM + g * GT + k + 1)
                        nc.vector.tensor_tensor(wl[:, k, :], wst[:, k, :], wh[:, k, :].bitcast(F32), ALU.subtract).then_inc(w_lo, 1)
                    for u in range(U):
                        n = g * U + u
                        ch, k = divmod(u, GT)
                        bank = 3 * (u % 2)
                        t = th[:, u % 2, :]
                        h = h32[:, u % 3, :]
                        dve.wait_ge(th_rdy, FROM + n + 1)
                        nc.vector.scalar_tensor_tensor(t, t, 1.0, ps[:, bank, :], ALU.add, ALU.mult).then_inc(s_rdy, 1)
                        dve.wait_ge(s_rdy, FROM + n + 1)
                        dve.wait_ge(u_ps, FROM + n + 1)
                        dve.wait_ge(h_lo, FROM + g * U + max(u - 2, 0))
                        nc.vector.scalar_tensor_tensor(h, t, 0.5, ps[:, bank + 1, :], ALU.mult, ALU.mult).then_inc(h_rdy, 1)
                        dve.wait_ge(h_rdy, FROM + n + 1)
                        dve.wait_ge(c_ps, FROM + n + 1)
                        nc.vector.tensor_tensor(h, h, ps[:, bank + 2, :], ALU.mult).then_inc(hc_rdy, 1)

                        def add(chunk):
                            a = acc[:, chunk * TC:(chunk + 1) * TC, :].rearrange("p a b -> p (a b)")
                            dve.wait_ge(y_ps, FROM + g * U + (chunk + 1) * GT)
                            dve.wait_ge(y_add, FROM + g * NCH + chunk)
                            nc.vector.tensor_tensor(a, a, ps[:, 6:8, :].rearrange("p a b -> p (a b)"), ALU.add).then_inc(y_add, 1)

                        if k == 1 and ch:
                            add(ch - 1)
                        if u == U - 1:
                            add(ch)


_OUTS = [((1, T, D), "float32")]


def kernel(**inputs):
    import numpy as np
    import concourse.bacc as bacc
    from concourse.bass_utils import run_bass_kernel_spmd

    g = {k: np.asarray(v) for k, v in inputs.items()}

    def rows(w):
        return w.reshape(-1, P, w.shape[1]).transpose(1, 0, 2)

    gate = g["L0_ffn_w_gate"].reshape(KT, P, SG, P, 4).transpose(1, 2, 4, 0, 3)
    up = g["L0_ffn_w_up"].reshape(KT, P, SG, P, 4).transpose(1, 2, 4, 0, 3)
    down = g["L0_ffn_w_down"].reshape(SG, P, 4, D).transpose(1, 0, 2, 3)
    w0 = np.concatenate([
        rows(g["L0_attn_q_w"].T).reshape(P, -1), rows(g["L0_attn_o_w"].T).reshape(P, -1),
        np.concatenate([rows(g["L0_attn_k_w"].T), rows(g["L0_attn_v_w"].T)], 2).reshape(P, -1),
        np.stack([gate, up], 3).reshape(P, -1), down.reshape(P, -1)], 1)

    wk = rows(g["L1_attn_Wk"]).reshape(P, KT, NH, HD).transpose(0, 2, 1, 3)
    wv = rows(g["L1_attn_Wv"]).reshape(P, KT, NH, HD).transpose(0, 2, 1, 3)
    wo = g["L1_attn_Wo"].reshape(NH, HD, D).transpose(1, 0, 2)
    whead = np.concatenate([wk.reshape(P, NH, -1), wv.reshape(P, NH, -1), wo], 2)
    whead = np.concatenate([whead, np.zeros_like(whead[:, :1])], 1)
    wq = rows(g["L1_attn_Wq"]).reshape(P, -1)

    pad = NI1 * P - ROWS
    zero = np.zeros((pad, D), g["L1_ffn_W1"].dtype)

    def units(routed, shared):
        return np.concatenate([routed.reshape(-1, D), shared, zero], 0)

    w1 = units(g["L1_ffn_W1"], g["L1_ffn_Ws1"]).reshape(NI1, P, KT, P).transpose(3, 0, 2, 1)
    w3 = units(g["L1_ffn_W3"], g["L1_ffn_Ws3"]).reshape(NI1, P, KT, P).transpose(3, 0, 2, 1)
    w2 = units(g["L1_ffn_W2"].transpose(0, 2, 1), g["L1_ffn_Ws2"].T).reshape(NI1, P, D).transpose(1, 0, 2)
    owner = np.minimum(np.arange(ROWS) // INTER1, E)
    sel = np.zeros((P, NI1 * P), np.float32)
    sel[owner, np.arange(ROWS)] = 1.0
    wexp = np.concatenate([w1.reshape(P, NI1, -1), w3.reshape(P, NI1, -1), w2, sel.reshape(P, NI1, P)], 2)

    i = np.arange(P)
    data = {
        "x": g["L0_attn_hidden_states"], "w0": w0, "bq0": g["L0_attn_q_b"].reshape(KT, P).T,
        "bkv0": np.concatenate([g["L0_attn_k_b"], g["L0_attn_v_b"]]), "bo0": g["L0_attn_o_b"],
        "wq": wq, "whead": whead, "bq1": g["L1_attn_bq"].reshape(QC, HD).T, "bk1": g["L1_attn_bk"].reshape(NH, HD).T,
        "bv1": g["L1_attn_bv"].reshape(NH, HD).T, "bo1": g["L1_attn_bo"], "wg": rows(g["L1_ffn_Wg"].T), "wexp": wexp,
        "ident": np.eye(P, dtype=np.float32), "bd": (i[:, None] // 16 == i[None, :] // 16).astype(np.float32),
        "causal": np.where(i[None, :] > i[:, None], np.float32(NEG), np.float32(0.0)),
        "tie": (i[None, :E] < i[:E, None]).astype(np.float32).reshape(-1),
    }
    nc = bacc.Bacc("TRN2", target_bir_lowering=False, num_devices=1)
    arrays, aps = {}, {}
    for name, a in data.items():
        a = np.ascontiguousarray(a)
        arrays["in_" + name] = a
        aps[name] = nc.dram_tensor("in_" + name, a.shape, mybir.dt.from_np(a.dtype), kind="ExternalInput").ap()
    out = nc.dram_tensor("out", _OUTS[0][0], F32, kind="ExternalOutput").ap()
    build(nc, aps, out)
    r = run_bass_kernel_spmd(nc, [arrays], core_ids=[0])
    return r.results[0]["out"]
```

```python
from contextlib import ExitStack

import concourse.bass as bass
from concourse import mybir

F32 = mybir.dt.float32
FR = mybir.dt.float32r
BF16 = mybir.dt.bfloat16
ALU = mybir.AluOpType
ACT = mybir.ActivationFunctionType
AX = mybir.AxisListType

P = 128
T = 2048
D = 256
KT = D // P
NT = T // P
CH = 512
NCH = T // CH
TC = CH // P

INTER0 = 1024
NI0 = INTER0 // P
SG = NI0 // 4
OFF_Q = 0
OFF_O = OFF_Q + KT * D
OFF_KV = OFF_O + KT * D
OFF_GU = OFF_KV + KT * 2 * D
OFF_DN = OFF_GU + NI0 * 2 * KT * P
W0_COLS = OFF_DN + NI0 * D
STG = 2048

NH = 16
HD = 128
QC = NH
SCALE = float(1.0 / (HD ** 0.5))
NEG = -1.0e30
FROM = 1

E = 16
INTER1 = 176
SHARED = 352
ROWS = E * INTER1 + SHARED
NI1 = -(-ROWS // P)
GT = 5
NG = NI1 // GT
GW = 3 * D
GCOLS = GT * (GW + P)


SEMS = {
    "a": ("xn_rdy xT_ps xh_rdy xl_rdy q_ps kv_ps qs_rdy kvs_rdy vh_rdy vl_rdy rel_rdy mn_rdy ex_rdy "
          "f_rdy f_hi f_lo kva_ps kva_add gu_ps th_rdy s_rdy h_rdy ab_rdy win_rdy cnt_rdy hm_rdy "
          "hs_hi hs_lo y_ps y_add").split(),
    "b": "kz_rdy kz_hi kz_lo nd_ps den_rdy rec_rdy at_rdy at_hi at_lo o_ps o_add ob_add bs_rdy ag_rdy sd".split(),
    "r": "wg_in wg_hi wg_lo xn_rdy xT_ps xc_hi xc_lo xs_hi xs_lo lg_ps mx_rdy ex_rdy v_rdy c_rdy bo_add".split(),
    "t": ("wq_in wq_hi wq_lo k_in o_in wk_hi wk_lo wo_hi wo_lo xq_rdy pj_ps q_rdy q_hi q_lo k_hi pj_rd v_hi v_lo s_ps mx_s "
          "nb_rdy ex_rdy rsum rs_rdy T_ps pt_hi pt_lo pv_ps o_hi o_lo y_ps y_add b_in b_bf bk_rdy bv_rdy").split(),
    "e": ("cp cT_ps ct_hi ct_lo w_in w_hi w_lo g_ps u_ps c_ps th_rdy s_rdy h_rdy hc_rdy h_hi h_lo y_ps y_add").split(),
}


def build(nc, d, out):
    with ExitStack() as top:
        def sem(name):
            return top.enter_context(nc.semaphore(name))

        def sbuf(stack, name, shape, dt):
            return stack.enter_context(nc.sbuf_tensor(name, shape, dt))

        sems = {f"{k}_{s}": sem(f"{k}_{s}") for k, names in SEMS.items() for s in names}

        acc = sbuf(top, "acc", [P, NT, D], F32)
        xTh = sbuf(top, "xTh", [P, KT, T], FR)
        xTl = sbuf(top, "xTl", [P, KT, T], FR)
        ident = sbuf(top, "ident", [P, P], F32)
        cb = sbuf(top, "cb", [P, NT, E + 1], F32)
        ps = top.enter_context(nc.psum_tensor("ps", [P, 8, CH], F32))
        mv = sbuf(top, "mv", [P, NT, 2], F32)
        rstd = sbuf(top, "rstd", [P, NT], F32)

        layer0(nc, top, d, acc, xTh, xTl, ident, ps, mv, rstd, sem, sems, sbuf)
        route(nc, d, acc, xTh, xTl, ident, cb, ps, mv, rstd, sem, sems, sbuf)
        attention(nc, d, acc, xTh, xTl, ident, ps, sem, sems, sbuf)
        experts(nc, d, acc, xTh, xTl, ident, cb, ps, sem, sems, sbuf)

        stored = sem("stored")
        with nc.Block() as block:
            @block.sync
            def _(sp):
                sp.dma_start(out[0].rearrange("(t p) d -> p t d", p=P), acc[:]).then_inc(stored, 16)
                sp.wait_ge(stored, 16)


def layer0(nc, top, d, acc, xTh, xTl, ident, ps, mv, rstd, sem, sems, sbuf):
    with ExitStack() as st:
        wh = sbuf(st, "w0h", [P, W0_COLS], FR)
        wl = sbuf(st, "w0l", [P, W0_COLS], FR)
        bqc = sbuf(st, "bqc", [P, KT], F32)
        bkv = sbuf(st, "bkv", [P, 2 * D], F32)
        bo = sbuf(st, "bo0", [P, D], F32)
        bd = sbuf(st, "bd", [P, P], F32)
        kvacc = sbuf(st, "kvacc", [P, KT, P + 2], F32)
        vh = sbuf(st, "vh", [P, TC, KT, P + 2], FR)
        vl = sbuf(st, "vl", [P, TC, KT, P + 2], FR)

        x_in, w_in, c_in = sem("x_in"), [sem("w_in0"), sem("w_in1")], sem("c_in")
        w_hi, w_lo = sem("w_hi"), sem("w_lo")
        st_done, ag_done, sd_done, rs_done, ms_done = (
            sem("st_done"), sem("ag_done"), sem("sd_done"), sem("rs_done"), sem("ms_done"))

        with ExitStack() as s0:
            stg = sbuf(s0, "stg", [P, 2, STG], F32)
            bst = sbuf(s0, "bst", [P, NT, 6], F32)
            with nc.Block() as block:
                @block.sync
                def _(sp):
                    for h in range(4):
                        sp.dma_start(acc[:, 4 * h:4 * h + 4, :],
                                     d["x"][0, h * CH:(h + 1) * CH].rearrange("(t p) d -> p t d", p=P)).then_inc(x_in, 16)
                    for k in range(W0_COLS // STG):
                        if k >= 2:
                            sp.wait_ge(w_hi, k - 1)
                            sp.wait_ge(w_lo, k - 1)
                        sp.dma_start(stg[:, k % 2, :], d["w0"][:, k * STG:(k + 1) * STG]).then_inc(w_in[k % 2], 16)
                    sp.dma_start(ident[:], d["ident"]).then_inc(c_in, 16)
                    sp.dma_start(bd[:], d["bd"]).then_inc(c_in, 16)
                    sp.dma_start(bqc[:], d["bq0"]).then_inc(c_in, 16)
                    sp.dma_start(bkv[:], d["bkv0"].partition_broadcast(P)).then_inc(c_in, 16)
                    sp.dma_start(bo[:], d["bo0"].partition_broadcast(P)).then_inc(c_in, 16)
                    sp.wait_ge(c_in, 80)

                @block.gpsimd
                def _(pool):
                    for s in sems.values():
                        pool.sem_inc(s, FROM)
                    nc.gpsimd.memset(kvacc[:], 0.0)
                    nc.gpsimd.memset(vh[:].bitcast(F32), 1.0)
                    nc.gpsimd.memset(vl[:].bitcast(F32), 0.0)

                @block.scalar
                def _(act):
                    act.wait_ge(sd_done, 1)
                    nc.scalar.activation(rstd[:], rstd[:], ACT.Sqrt).then_inc(sd_done, 1)
                    for k in range(W0_COLS // STG):
                        act.wait_ge(w_in[k % 2], 16 * (k // 2 + 1))
                        nc.scalar.activation(wh[:, k * STG:(k + 1) * STG], stg[:, k % 2, :], ACT.Copy).then_inc(w_hi, 1)

                @block.vector
                def _(dve):
                    dve.wait_ge(x_in, 64)
                    with dve.Fori(0, NT) as i:
                        nc.vector.bn_stats(bst[:, bass.ds(i, 1), :], acc[:, bass.ds(i, 1), :]).then_inc(st_done, 1)
                    dve.wait_ge(st_done, NT)
                    for i in range(NT):
                        nc.vector.bn_aggr(mv[:, i, :], bst[:, i, :]).then_inc(ag_done, 1)
                    dve.wait_ge(ag_done, NT)
                    nc.vector.tensor_scalar(rstd[:], mv[:, :, 1], 1e-5, None, ALU.add).then_inc(sd_done, 1)
                    dve.wait_ge(sd_done, 2)
                    nc.vector.reciprocal(rstd[:], rstd[:]).then_inc(rs_done, 1)
                    for k in range(W0_COLS // STG):
                        dve.wait_ge(w_hi, k + 1)
                        nc.vector.tensor_tensor(wl[:, k * STG:(k + 1) * STG], stg[:, k % 2, :],
                                                wh[:, k * STG:(k + 1) * STG].bitcast(F32), ALU.subtract).then_inc(w_lo, 1)

        layer0_chunks(nc, d, acc, xTh, xTl, ident, ps, mv, rstd, wh, wl, bqc, bkv, kvacc, vh, vl, sems, sbuf)
        layer0_out(nc, acc, xTh, xTl, ps, mv, rstd, wh, wl, bo, bd, kvacc, sems, sbuf)


PARTS = ((0, 0), (0, 1), (1, 0))


def layer0_chunks(nc, d, acc, qfh, qfl, ident, ps, mv, rstd, wh, wl, bqc, bkv, kvacc, vh, vl, sems, sbuf):
    with ExitStack() as st:
        xn = sbuf(st, "xn", [P, TC, D], F32)
        xh = sbuf(st, "xh", [P, KT, CH], FR)
        xl = sbuf(st, "xl", [P, KT, CH], FR)
        qs = xn[:].rearrange("p t d -> p (t d)").rearrange("p (a b) -> p a b", a=KT)
        kvs = sbuf(st, "kvs", [P, TC, 2 * D], F32)
        rel = sbuf(st, "rel", [P, 2, 2 * CH], F32)
        mn = sbuf(st, "mn", [P, 2, 2 * CH], F32)
        kfh = sbuf(st, "kfh", [P, TC, D], FR)
        kfl = sbuf(st, "kfl", [P, TC, D], FR)
        th = sbuf(st, "th", [P, 2, CH], F32)
        hh32 = sbuf(st, "hh32", [P, 4, CH], F32)
        ab = rel[:].rearrange("p s (a b) -> p (s a) b", a=2)
        win = sbuf(st, "win", [P, 6, CH], BF16)
        cnt = mn[:, 0, :].bitcast(BF16).rearrange("p (a b) -> p a b", a=4)
        hsh = sbuf(st, "hsh", [P, 4, CH], FR)
        hsl = sbuf(st, "hsl", [P, 4, CH], FR)
        w = (wh, wl)
        x = (xh, xl)
        kf, v, hs = (kfh, kfl), (vh, vl), (hsh, hsl)

        (xn_rdy, xT_ps, xh_rdy, xl_rdy, q_ps, kv_ps, qs_rdy, kvs_rdy, vh_rdy, vl_rdy, rel_rdy, mn_rdy, ex_rdy,
         f_rdy, f_hi, f_lo, kva_ps, kva_add, gu_ps, th_rdy, s_rdy, h_rdy, ab_rdy, win_rdy, cnt_rdy, hm_rdy,
         hs_hi, hs_lo, y_ps, y_add) = [sems["a_" + s] for s in SEMS["a"]]

        def feat(s, buf):
            return buf[:, s, :]

        qpre = xn[:].rearrange("p t d -> p (t d)")
        kpre = kvs[:, :, 0:D]

        def feature(s, n):
            f = feat(s, mn).rearrange("p (a b) -> p a b", a=TC if s else KT)
            if s == 0:
                return f, qfh[:, :, bass.ds(n * CH, CH)], qfl[:, :, bass.ds(n * CH, CH)]
            return f, kfh[:], kfl[:]

        with nc.Block() as block:
            @block.tensor
            def _(pe):
                with pe.Fori(0, NCH) as n:
                    pe.wait_ge(y_add, FROM + n * SG)
                    for kt in range(KT):
                        for j in range(TC):
                            pe.wait_ge(xn_rdy, FROM + n * TC + j + 1)
                            m = nc.tensor.transpose(ps[:, kt, j * P:(j + 1) * P], xn[:, j, kt * P:(kt + 1) * P], ident[:])
                        m.then_inc(xT_ps, 1)
                    pe.wait_ge(h_rdy, FROM + n * NI0)
                    pe.wait_ge(xh_rdy, FROM + n * KT + KT)
                    pe.wait_ge(xl_rdy, FROM + n * KT + KT)
                    for m2 in range(KT):
                        k = 0
                        for kt in range(KT):
                            for a, b in PARTS:
                                o = OFF_Q + kt * D + m2 * P
                                m = nc.tensor.matmul(ps[:, 2 + m2, :], w[a][:, o:o + P], x[b][:, kt, :],
                                                     start=k == 0, stop=k == 5)
                                k += 1
                        m.then_inc(q_ps, 1)
                    for j in range(TC):
                        k = 0
                        for kt in range(KT):
                            for a, b in PARTS:
                                o = OFF_KV + kt * 2 * D
                                m = nc.tensor.matmul(ps[:, 4 + j, :], x[a][:, kt, j * P:(j + 1) * P], w[b][:, o:o + 2 * D],
                                                     start=k == 0, stop=k == 5)
                                k += 1
                        m.then_inc(kv_ps, 1)

                    def gate_up(i):
                        bank = 2 + 2 * (i % 3)
                        if i == 0:
                            pe.wait_ge(qs_rdy, FROM + n * KT + KT)
                        elif i < 3:
                            pe.wait_ge(kvs_rdy, FROM + n * TC + 2 * i)
                        else:
                            pe.wait_ge(h_rdy, FROM + n * NI0 + i - 2)
                        for g in range(2):
                            k = 0
                            for kt in range(KT):
                                for a, b in PARTS:
                                    o = OFF_GU + ((i * 2 + g) * KT + kt) * P
                                    m = nc.tensor.matmul(ps[:, bank + g, :], w[a][:, o:o + P], x[b][:, kt, :],
                                                         start=k == 0, stop=k == 5)
                                    k += 1
                            m.then_inc(gu_ps, 1)

                    for i in range(4):
                        gate_up(i)
                    pe.wait_ge(f_hi, FROM + n * 2 + 2)
                    pe.wait_ge(f_lo, FROM + n * 2 + 2)
                    pe.wait_ge(vh_rdy, FROM + n + 1)
                    pe.wait_ge(vl_rdy, FROM + n + 1)
                    for m2 in range(KT):
                        k = 0
                        for j in range(TC):
                            for a, b in PARTS:
                                m = nc.tensor.matmul(ps[:, 0, m2 * (P + 2):(m2 + 1) * (P + 2)],
                                                     kf[a][:, j, m2 * P:(m2 + 1) * P], v[b][:, j, m2, :],
                                                     start=k == 0, stop=k == 3 * TC - 1)
                                k += 1
                    m.then_inc(kva_ps, 1)
                    for i in range(4, NI0):
                        gate_up(i)
                    pe.wait_ge(kva_add, FROM + n + 1)
                    for s in range(SG):
                        pe.wait_ge(hs_hi, FROM + n * SG + s + 1)
                        pe.wait_ge(hs_lo, FROM + n * SG + s + 1)
                        if s:
                            pe.wait_ge(y_add, FROM + n * SG + s)
                        for t in range(TC):
                            k = 0
                            for j in range(4):
                                for a, b in PARTS:
                                    o = OFF_DN + (s * 4 + j) * D
                                    m = nc.tensor.matmul(ps[:, t // 2, (t % 2) * D:(t % 2 + 1) * D],
                                                         hs[a][:, j, t * P:(t + 1) * P], w[b][:, o:o + D],
                                                         start=k == 0, stop=k == 11)
                                    k += 1
                        m.then_inc(y_ps, 1)

            @block.scalar
            def _(act):
                with act.Fori(0, NCH) as n:
                    act.wait_ge(gu_ps, FROM + n * 2 * NI0)
                    for kt in range(KT):
                        act.wait_ge(xT_ps, FROM + n * KT + kt + 1)
                        nc.scalar.activation(xh[:, kt, :], ps[:, kt, :], ACT.Copy).then_inc(xh_rdy, 1)
                    act.wait_ge(qs_rdy, FROM + n * KT + KT)
                    act.wait_ge(win_rdy, FROM + n * SG * 3)
                    nc.scalar.activation(feat(0, rel), qpre, ACT.Relu).then_inc(rel_rdy, 1)
                    act.wait_ge(kvs_rdy, FROM + n * TC + TC)
                    nc.scalar.activation(feat(1, rel).rearrange("p (a b) -> p a b", a=TC), kpre, ACT.Relu).then_inc(rel_rdy, 1)
                    act.wait_ge(kva_ps, FROM + n)
                    nc.scalar.activation(vh[:, :, :, 0:P], kvs[:, :, D:2 * D].rearrange("p a (m e) -> p a m e", m=KT),
                                         ACT.Copy).then_inc(vh_rdy, 1)
                    for s in range(2):
                        act.wait_ge(mn_rdy, FROM + n * 2 + s + 1)
                        nc.scalar.activation(feat(s, mn), feat(s, mn), ACT.Exp).then_inc(ex_rdy, 1)
                    act.wait_ge(kva_ps, FROM + n)
                    for s in range(2):
                        act.wait_ge(f_rdy, FROM + n * 2 + s + 1)
                        f, hi, lo = feature(s, n)
                        nc.scalar.activation(hi, f, ACT.Copy).then_inc(f_hi, 1)
                    for i in range(NI0):
                        act.wait_ge(gu_ps, FROM + n * 2 * NI0 + 2 * i + 1)
                        if i >= 2:
                            act.wait_ge(h_rdy, FROM + n * NI0 + i - 1)
                        else:
                            act.wait_ge(h_rdy, FROM + n * NI0)
                        nc.scalar.activation(th[:, i % 2, :], ps[:, 2 + 2 * (i % 3), :], ACT.Tanh, scale=0.5).then_inc(th_rdy, 1)
                        if i % 4 == 3:
                            s = i // 4
                            act.wait_ge(h_rdy, FROM + n * NI0 + i + 1)
                            act.wait_ge(win_rdy, FROM + (n * SG + s) * 3)
                            act.wait_ge(f_rdy, FROM + n * 2 + 2)
                            nc.scalar.activation(ab[:], hh32[:], ACT.Abs).then_inc(ab_rdy, 1)
                            act.wait_ge(hm_rdy, FROM + (n * SG + s) * 4 + 4)
                            act.wait_ge(y_ps, FROM + n * SG + s)
                            nc.scalar.activation(hsh[:], hh32[:], ACT.Copy).then_inc(hs_hi, 1)

            @block.gpsimd
            def _(pool):
                with pool.Fori(0, NCH) as n:
                    for s in range(2):
                        pool.wait_ge(ex_rdy, FROM + n * 2 + s + 1)
                        pool.wait_ge(rel_rdy, FROM + n * 2 + s + 1)
                        nc.gpsimd.tensor_tensor(feat(s, mn), feat(s, mn), feat(s, rel), ALU.add).then_inc(f_rdy, 1)
                        f, hi, lo = feature(s, n)
                        pool.wait_ge(f_hi, FROM + n * 2 + s + 1)
                        nc.gpsimd.tensor_tensor(lo, f, hi.bitcast(F32), ALU.subtract).then_inc(f_lo, 1)

            @block.vector
            def _(dve):
                with dve.Fori(0, NCH) as n:
                    dve.wait_ge(mn_rdy, FROM + n * 2)
                    dve.wait_ge(rel_rdy, FROM + n * 2)
                    for j in range(TC):
                        t = n * TC + j
                        nc.vector.tensor_scalar(xn[:, j, :], acc[:, bass.ds(t, 1), :].rearrange("p a b -> p (a b)"),
                                                mv[:, bass.ds(t, 1), 0:1].rearrange("p a b -> p (a b)"), rstd[:, bass.ds(t, 1)],
                                                ALU.subtract, ALU.mult).then_inc(xn_rdy, 1)
                    for kt in range(KT):
                        dve.wait_ge(xh_rdy, FROM + n * KT + kt + 1)
                        nc.vector.tensor_tensor(xl[:, kt, :], ps[:, kt, :], xh[:, kt, :].bitcast(F32), ALU.subtract).then_inc(xl_rdy, 1)
                    for m2 in range(KT):
                        dve.wait_ge(q_ps, FROM + n * KT + m2 + 1)
                        nc.vector.tensor_scalar(qs[:, m2, :], ps[:, 2 + m2, :], bqc[:, m2:m2 + 1], None, ALU.add).then_inc(qs_rdy, 1)
                    dve.wait_ge(f_lo, FROM + n * 2)
                    dve.wait_ge(hm_rdy, FROM + n * SG * 4)
                    dve.wait_ge(qs_rdy, FROM + n * KT + KT)
                    nc.vector.tensor_scalar(feat(0, mn), qpre, 0.0, None, ALU.min).then_inc(mn_rdy, 1)
                    dve.wait_ge(vh_rdy, FROM + n)
                    dve.wait_ge(vl_rdy, FROM + n)
                    for j in range(TC):
                        dve.wait_ge(kv_ps, FROM + n * TC + j + 1)
                        nc.vector.tensor_tensor(kvs[:, j, :], ps[:, 4 + j, :], bkv[:], ALU.add).then_inc(kvs_rdy, 1)
                    dve.wait_ge(kvs_rdy, FROM + n * TC + TC)
                    nc.vector.tensor_scalar(feat(1, mn).rearrange("p (a b) -> p a b", a=TC), kpre, 0.0, None, ALU.min).then_inc(mn_rdy, 1)
                    dve.wait_ge(vh_rdy, FROM + n + 1)
                    nc.vector.tensor_tensor(vl[:, :, :, 0:P], kvs[:, :, D:2 * D].rearrange("p a (m e) -> p a m e", m=KT),
                                            vh[:, :, :, 0:P].bitcast(F32), ALU.subtract).then_inc(vl_rdy, 1)
                    for i in range(NI0):
                        s = i // 4
                        u = n * NI0 + i
                        bank = 2 + 2 * (i % 3)
                        dve.wait_ge(th_rdy, FROM + u + 1)
                        nc.vector.scalar_tensor_tensor(th[:, i % 2, :], th[:, i % 2, :], 1.0, ps[:, bank, :],
                                                       ALU.add, ALU.mult).then_inc(s_rdy, 1)
                        dve.wait_ge(s_rdy, FROM + u + 1)
                        dve.wait_ge(gu_ps, FROM + 2 * u + 2)
                        dve.wait_ge(hs_lo, FROM + n * SG + s)
                        nc.vector.scalar_tensor_tensor(hh32[:, i % 4, :], th[:, i % 2, :], 0.5, ps[:, bank + 1, :],
                                                       ALU.mult, ALU.mult).then_inc(h_rdy, 1)
                        if i % 4 != 3:
                            continue
                        g = n * SG + s
                        dve.wait_ge(ab_rdy, FROM + g + 1)
                        dve.wait_ge(hm_rdy, FROM + g * 4)
                        for a, nb, o in ((0, 3, 0), (1, 2, 3), (2, 1, 5)):
                            nc.vector.tensor_tensor(win[:, o:o + nb, :], ab[:, a:a + 1, :].broadcast_to([P, nb, CH]),
                                                    ab[:, a + 1:4, :], ALU.is_ge).then_inc(win_rdy, 1)
                        dve.wait_ge(win_rdy, FROM + g * 3 + 3)
                        dve.wait_ge(f_lo, FROM + n * 2 + 2)
                        plan = ((0, 1, ALU.add, 2, ALU.add, 2.0, ALU.is_ge), (3, 4, ALU.add, 0, ALU.subtract, 1.0, ALU.is_ge),
                                (5, 1, ALU.subtract, 3, ALU.subtract, 0.0, ALU.is_ge), (2, 4, ALU.add, 5, ALU.add, 1.0, ALU.is_le))
                        for k, (a, b, op, c, op2, lim, cmp) in enumerate(plan):
                            nc.vector.tensor_tensor(cnt[:, k, :], win[:, a, :], win[:, b, :], op).then_inc(cnt_rdy, 1)
                        for k, (a, b, op, c, op2, lim, cmp) in enumerate(plan):
                            dve.wait_ge(cnt_rdy, FROM + g * 8 + k + 1)
                            nc.vector.tensor_tensor(cnt[:, k, :], cnt[:, k, :], win[:, c, :], op2).then_inc(cnt_rdy, 1)
                        for k, (a, b, op, c, op2, lim, cmp) in enumerate(plan):
                            dve.wait_ge(cnt_rdy, FROM + g * 8 + k + 5)
                            nc.vector.scalar_tensor_tensor(hh32[:, k, :], cnt[:, k, :], lim, hh32[:, k, :], cmp, ALU.mult).then_inc(hm_rdy, 1)
                        dve.wait_ge(hs_hi, FROM + g + 1)
                        nc.vector.tensor_tensor(hsl[:], hh32[:], hsh[:].bitcast(F32), ALU.subtract).then_inc(hs_lo, 1)
                        if s == 0:
                            dve.wait_ge(kva_ps, FROM + n + 1)
                            kv = kvacc[:].rearrange("p a b -> p (a b)")
                            nc.vector.tensor_tensor(kv, kv, ps[:, 0, 0:KT * (P + 2)], ALU.add).then_inc(kva_add, 1)
                    for s in range(SG):
                        dve.wait_ge(y_ps, FROM + n * SG + s + 1)
                        if s:
                            dve.wait_ge(y_add, FROM + n * SG + s)
                        a = acc[:, bass.ds(n * TC, TC), :].rearrange("p a b -> p (a b)")
                        nc.vector.tensor_tensor(a, a, ps[:, 0:2, :].rearrange("p a b -> p (a b)"), ALU.add).then_inc(y_add, 1)


def layer0_out(nc, acc, qfh, qfl, ps, mv, rstd, wh, wl, bo, bd, kvacc, sems, sbuf):
    with ExitStack() as st:
        kz = sbuf(st, "kz", [P, 4, P], F32)
        kzh = sbuf(st, "kzh", [P, 4, P], FR)
        kzl = sbuf(st, "kzl", [P, 4, P], FR)
        den = sbuf(st, "den", [P, KT, CH], F32)
        at = sbuf(st, "at", [P, KT, CH], F32)
        ath = sbuf(st, "ath", [P, KT, CH], FR)
        atl = sbuf(st, "atl", [P, KT, CH], FR)
        bst = sbuf(st, "bst1", [P, NT, 6], F32)
        kzs, qf, ats, w = (kzh, kzl), (qfh, qfl), (ath, atl), (wh, wl)
        (kz_rdy, kz_hi, kz_lo, nd_ps, den_rdy, rec_rdy, at_rdy, at_hi, at_lo, o_ps, o_add, ob_add, bs_rdy, ag_rdy, sd) = [sems["b_" + s] for s in SEMS["b"]]
        with nc.Block() as block:
            @block.tensor
            def _(pe):
                pe.wait_ge(kz_lo, FROM + 1)
                with pe.Fori(0, NCH) as n:
                    pe.wait_ge(at_rdy, FROM + n * KT)
                    for m2 in range(KT):
                        for z in range(2):
                            for k, (a, b) in enumerate(PARTS):
                                m = nc.tensor.matmul(ps[:, 2 * m2 + z, :], kzs[a][:, 2 * z + m2, :],
                                                     qf[b][:, m2, bass.ds(n * CH, CH)], start=k == 0, stop=k == 2)
                            m.then_inc(nd_ps, 1)
                    pe.wait_ge(at_hi, FROM + n * KT + KT)
                    pe.wait_ge(at_lo, FROM + n * KT + KT)
                    pe.wait_ge(o_add, FROM + n)
                    for t in range(TC):
                        k = 0
                        for m2 in range(KT):
                            for a, b in PARTS:
                                o = OFF_O + m2 * D
                                m = nc.tensor.matmul(ps[:, 4 + t // 2, (t % 2) * D:(t % 2 + 1) * D],
                                                     ats[a][:, m2, t * P:(t + 1) * P], w[b][:, o:o + D], start=k == 0, stop=k == 5)
                                k += 1
                    m.then_inc(o_ps, 1)

            @block.scalar
            def _(act):
                act.wait_ge(kz_rdy, FROM + 4)
                nc.scalar.activation(kzh[:], kz[:], ACT.Copy).then_inc(kz_hi, 1)
                with act.Fori(0, NCH) as n:
                    act.wait_ge(o_ps, FROM + n)
                    for m2 in range(KT):
                        act.wait_ge(at_rdy, FROM + n * KT + m2 + 1)
                        nc.scalar.activation(ath[:, m2, :], at[:, m2, :], ACT.Copy).then_inc(at_hi, 1)
                act.wait_ge(sd, FROM + 1)
                nc.scalar.activation(rstd[:], rstd[:], ACT.Sqrt).then_inc(sd, 1)

            @block.gpsimd
            def _(pool):
                with pool.Fori(0, NCH) as n:
                    pool.wait_ge(o_add, FROM + n + 1)
                    a = acc[:, bass.ds(n * TC, TC), :]
                    nc.gpsimd.tensor_tensor(a, a, bo[:].unsqueeze(1).broadcast_to([P, TC, D]), ALU.add).then_inc(ob_add, 1)

            @block.vector
            def _(dve):
                for m2 in range(KT):
                    nc.vector.tensor_tensor(kz[:, m2, :], kvacc[:, m2, 0:P], bd[:], ALU.mult).then_inc(kz_rdy, 1)
                    nc.vector.tensor_scalar(kz[:, 2 + m2, :], bd[:], kvacc[:, m2, P:P + 1], None, ALU.mult).then_inc(kz_rdy, 1)
                dve.wait_ge(kz_hi, FROM + 1)
                nc.vector.tensor_tensor(kzl[:], kz[:], kzh[:].bitcast(F32), ALU.subtract).then_inc(kz_lo, 1)
                with dve.Fori(0, NCH) as n:
                    dve.wait_ge(at_hi, FROM + n * KT)
                    dve.wait_ge(at_lo, FROM + n * KT)
                    for m2 in range(KT):
                        u = n * KT + m2
                        dve.wait_ge(nd_ps, FROM + 2 * u + 2)
                        nc.vector.tensor_scalar(den[:, m2, :], ps[:, 2 * m2 + 1, :], 1e-6, None, ALU.add).then_inc(den_rdy, 1)
                        dve.wait_ge(den_rdy, FROM + u + 1)
                        nc.vector.reciprocal(den[:, m2, :], den[:, m2, :]).then_inc(rec_rdy, 1)
                        dve.wait_ge(rec_rdy, FROM + u + 1)
                        nc.vector.tensor_tensor(at[:, m2, :], den[:, m2, :], ps[:, 2 * m2, :], ALU.mult).then_inc(at_rdy, 1)
                        dve.wait_ge(at_hi, FROM + u + 1)
                        nc.vector.tensor_tensor(atl[:, m2, :], at[:, m2, :], ath[:, m2, :].bitcast(F32), ALU.subtract).then_inc(at_lo, 1)
                    dve.wait_ge(o_ps, FROM + n + 1)
                    a = acc[:, bass.ds(n * TC, TC), :].rearrange("p a b -> p (a b)")
                    nc.vector.tensor_tensor(a, a, ps[:, 4:6, :].rearrange("p a b -> p (a b)"), ALU.add).then_inc(o_add, 1)
                    dve.wait_ge(ob_add, FROM + n + 1)
                    for t in range(TC):
                        nc.vector.bn_stats(bst[:, bass.ds(n * TC + t, 1), :], acc[:, bass.ds(n * TC + t, 1), :]).then_inc(bs_rdy, 1)
                dve.wait_ge(bs_rdy, FROM + NT)
                for i in range(NT):
                    nc.vector.bn_aggr(mv[:, i, :], bst[:, i, :]).then_inc(ag_rdy, 1)
                dve.wait_ge(ag_rdy, FROM + NT)
                nc.vector.tensor_scalar(rstd[:], mv[:, :, 1], 1e-5, None, ALU.add).then_inc(sd, 1)
                dve.wait_ge(sd, FROM + 2)
                nc.vector.reciprocal(rstd[:], rstd[:]).then_inc(sd, 1)


def route(nc, d, acc, xTh, xTl, ident, cb, ps, mv, rstd, sem, sems, sbuf):
    G = 4
    with ExitStack() as st:
        wg = sbuf(st, "wg", [P, KT, E], F32)
        wgh = sbuf(st, "wgh", [P, KT, E], FR)
        wgl = sbuf(st, "wgl", [P, KT, E], FR)
        tie = sbuf(st, "tie", [P, E, E], F32)
        bo = sbuf(st, "bo1", [P, D], F32)
        xn = sbuf(st, "xn1", [P, TC, D], F32)
        xch = sbuf(st, "xch", [P, KT, CH], FR)
        xcl = sbuf(st, "xcl", [P, KT, CH], FR)
        m1 = sbuf(st, "m1", [P, TC], F32)
        ex = sbuf(st, "ex", [P, TC, E], F32)
        sc = sbuf(st, "sc", [P, TC, E], F32)
        gm = sbuf(st, "gm", [P, TC, G], F32)
        cg = sbuf(st, "cg", [P, 2, TC * G * G], F32)
        keep = sbuf(st, "keep", [P, TC, G], F32)
        mk = sbuf(st, "mk", [P, TC, E], F32)
        ce = sbuf(st, "ce", [P, 2, TC * E * E], F32)
        rk = sbuf(st, "rk", [P, TC, E], F32)
        xc, wgs = (xch, xcl), (wgh, wgl)
        (wg_in, wg_hi, wg_lo, xn_rdy, xT_ps, xc_hi, xc_lo, xs_hi, xs_lo, lg_ps, mx_rdy, ex_rdy,
         v_rdy, c_rdy, bo_add) = [sems["r_" + s] for s in SEMS["r"]]
        with nc.Block() as block:
            @block.sync
            def _(sp):
                sp.dma_start(wg[:], d["wg"]).then_inc(wg_in, 16)
                sp.dma_start(tie[:].rearrange("p a b -> p (a b)"), d["tie"].partition_broadcast(P)).then_inc(wg_in, 16)
                sp.dma_start(bo[:], d["bo1"].partition_broadcast(P)).then_inc(wg_in, 16)

            @block.tensor
            def _(pe):
                pe.wait_ge(wg_hi, FROM + 1)
                pe.wait_ge(wg_lo, FROM + 1)
                with pe.Fori(0, NCH) as n:
                    pe.wait_ge(xc_lo, FROM + n * KT)
                    for kt in range(KT):
                        for j in range(TC):
                            pe.wait_ge(xn_rdy, FROM + n * TC + j + 1)
                            m = nc.tensor.transpose(ps[:, kt, j * P:(j + 1) * P], xn[:, j, kt * P:(kt + 1) * P], ident[:])
                        m.then_inc(xT_ps, 1)
                    pe.wait_ge(xc_lo, FROM + n * KT + KT)
                    pe.wait_ge(mx_rdy, FROM + n)
                    for t in range(TC):
                        k = 0
                        for kt in range(KT):
                            for a, b in PARTS:
                                m = nc.tensor.matmul(ps[:, 2, t * E:(t + 1) * E], xc[a][:, kt, t * P:(t + 1) * P], wgs[b][:, kt, :],
                                                     start=k == 0, stop=k == 5)
                                k += 1
                    m.then_inc(lg_ps, 1)

            @block.scalar
            def _(act):
                act.wait_ge(wg_in, FROM + 48)
                nc.scalar.activation(wgh[:], wg[:], ACT.Copy).then_inc(wg_hi, 1)
                with act.Fori(0, NCH) as n:
                    act.wait_ge(lg_ps, FROM + n)
                    act.wait_ge(xs_hi, FROM + n)
                    for kt in range(KT):
                        act.wait_ge(xT_ps, FROM + n * KT + kt + 1)
                        nc.scalar.activation(xch[:, kt, :], ps[:, kt, :], ACT.Copy).then_inc(xc_hi, 1)
                    act.wait_ge(mx_rdy, FROM + n + 1)
                    nc.scalar.activation(ex[:], ex[:], ACT.Exp).then_inc(ex_rdy, 1)

            @block.gpsimd
            def _(pool):
                pool.memset(cb[:, :, E:E + 1], 1.0)
                pool.wait_ge(wg_in, FROM + 48)
                with pool.Fori(0, NCH) as n:
                    pool.wait_ge(xn_rdy, FROM + n * TC + TC)
                    a = acc[:, bass.ds(n * TC, TC), :]
                    nc.gpsimd.tensor_tensor(a, a, bo[:].unsqueeze(1).broadcast_to([P, TC, D]), ALU.add).then_inc(bo_add, 1)

            @block.vector
            def _(dve):
                dve.wait_ge(wg_hi, FROM + 1)
                nc.vector.tensor_tensor(wgl[:], wg[:], wgh[:].bitcast(F32), ALU.subtract).then_inc(wg_lo, 1)
                with dve.Fori(0, NCH) as n:
                    dve.wait_ge(xT_ps, FROM + n * KT)
                    for j in range(TC):
                        t = n * TC + j
                        nc.vector.tensor_scalar(xn[:, j, :], acc[:, bass.ds(t, 1), :].rearrange("p a b -> p (a b)"),
                                                mv[:, bass.ds(t, 1), 0:1].rearrange("p a b -> p (a b)"), rstd[:, bass.ds(t, 1)],
                                                ALU.subtract, ALU.mult).then_inc(xn_rdy, 1)
                    dve.wait_ge(xs_lo, FROM + n)
                    for kt in range(KT):
                        dve.wait_ge(xc_hi, FROM + n * KT + kt + 1)
                        nc.vector.tensor_tensor(xcl[:, kt, :], ps[:, kt, :], xch[:, kt, :].bitcast(F32), ALU.subtract).then_inc(xc_lo, 1)
                    dve.wait_ge(xc_lo, FROM + n * KT + KT)
                    nc.vector.tensor_copy(xTl[:, :, bass.ds(n * CH, CH)], xcl[:].bitcast(F32)).then_inc(xs_lo, 1)
                    nc.vector.tensor_copy(xTh[:, :, bass.ds(n * CH, CH)], xch[:].bitcast(F32)).then_inc(xs_hi, 1)
                    lg = ps[:, 2, 0:TC * E].rearrange("p (t e) -> p t e", t=TC)
                    V = 16

                    def step(k, ins):
                        ins.then_inc(v_rdy, 1)
                        dve.wait_ge(v_rdy, FROM + n * V + k)

                    dve.wait_ge(lg_ps, FROM + n + 1)
                    step(1, nc.vector.tensor_reduce(m1[:], lg, AX.X, ALU.max))
                    nc.vector.tensor_tensor(ex[:], lg, m1[:].unsqueeze(2).broadcast_to([P, TC, E]), ALU.subtract).then_inc(mx_rdy, 1)
                    dve.wait_ge(ex_rdy, FROM + n + 1)
                    step(2, nc.vector.tensor_reduce(m1[:], ex[:], AX.X, ALU.add))
                    step(3, nc.vector.reciprocal(m1[:], m1[:]))
                    step(4, nc.vector.tensor_tensor(sc[:], ex[:], m1[:].unsqueeze(2).broadcast_to([P, TC, E]), ALU.mult))
                    step(5, nc.vector.tensor_reduce(gm[:], sc[:].rearrange("p t (g e) -> p t g e", g=G), AX.X, ALU.max))
                    row = gm[:].unsqueeze(3).broadcast_to([P, TC, G, G])
                    col = gm[:].unsqueeze(2).broadcast_to([P, TC, G, G])
                    c0, c1 = [cg[:, k, :].rearrange("p (t a b) -> p t a b", t=TC, a=G) for k in range(2)]
                    nc.vector.tensor_tensor(c0, col, row, ALU.is_gt).then_inc(c_rdy, 1)
                    step(6, nc.vector.tensor_tensor(c1, col, row, ALU.is_equal))
                    step(7, nc.vector.tensor_tensor(c1, c1, tie[:, 0:G, 0:G].unsqueeze(1).broadcast_to([P, TC, G, G]), ALU.mult))
                    dve.wait_ge(c_rdy, FROM + 2 * n + 1)
                    step(8, nc.vector.tensor_tensor(c0, c0, c1, ALU.add))
                    step(9, nc.vector.tensor_reduce(keep[:], c0, AX.X, ALU.add))
                    step(10, nc.vector.tensor_scalar(keep[:], keep[:], 2.0, None, ALU.is_lt))
                    kb = keep[:].unsqueeze(3).broadcast_to([P, TC, G, E // G])
                    step(11, nc.vector.tensor_tensor(mk[:].rearrange("p t (g e) -> p t g e", g=G),
                                                     sc[:].rearrange("p t (g e) -> p t g e", g=G), kb, ALU.mult))
                    step(12, nc.vector.scalar_tensor_tensor(
                        mk[:].rearrange("p t (g e) -> p (t g) e", g=G), kb.rearrange("p t g e -> p (t g) e"), -1.0,
                        mk[:].rearrange("p t (g e) -> p (t g) e", g=G), ALU.add, ALU.add))
                    row = mk[:].unsqueeze(3).broadcast_to([P, TC, E, E])
                    col = mk[:].unsqueeze(2).broadcast_to([P, TC, E, E])
                    e0, e1 = [ce[:, k, :].rearrange("p (t a b) -> p t a b", t=TC, a=E) for k in range(2)]
                    nc.vector.tensor_tensor(e0, col, row, ALU.is_gt).then_inc(c_rdy, 1)
                    step(13, nc.vector.tensor_tensor(e1, col, row, ALU.is_equal))
                    step(14, nc.vector.tensor_tensor(e1, e1, tie[:].unsqueeze(1).broadcast_to([P, TC, E, E]), ALU.mult))
                    dve.wait_ge(c_rdy, FROM + 2 * n + 2)
                    step(15, nc.vector.tensor_tensor(e0, e0, e1, ALU.add))
                    step(16, nc.vector.tensor_reduce(rk[:], e0, AX.X, ALU.add))
                    nc.vector.scalar_tensor_tensor(cb[:, bass.ds(n * TC, TC), 0:E], rk[:], 4.0, sc[:], ALU.is_lt, ALU.mult)


def attention(nc, d, acc, xTh, xTl, ident, ps, sem, sems, sbuf):
    NP = (T * NH) // (NH * P)
    TILE = [NP - 1 - p for p in range(NP)]
    CK = [-(-(t + 1) // TC) for t in TILE]
    PR = [-(-c // 2) for c in CK]
    cumc = [sum(CK[:i]) for i in range(NP + 1)]
    cump = [sum(PR[:i]) for i in range(NP + 1)]
    NC, NPR = cumc[NP], cump[NP]
    TWO = sum(p == 2 for p in PR)
    NPA = NP // 2
    cumv = [sum(CK[0:2 * m:2]) for m in range(NPA + 1)]
    NPV = cumv[NPA]
    UNITS = [("k", 3, 3), ("v", 3, 3), ("q", 0, 3), ("k", 2, 3), ("q", 1, 3), ("v", 2, 2),
             ("q", 2, 3), ("k", 1, 2), ("q", 3, 3), ("v", 1, 2), ("k", 0, 1), ("v", 0, 4)]
    UN = len(UNITS)
    AT = {4: 0, 5: 1, 6: 2, 7: 3, 8: 4, 9: 5, 10: 6, 11: 7, 12: 8, 13: 9, 14: 10}
    QAT = {1: 1, 3: 2, 5: 3}
    QNEXT = 13
    QN = [sum(u[0] == "q" for u in UNITS[:k]) for k in range(UN + 1)]
    KN = [sum(u[0] != "q" for u in UNITS[:k]) for k in range(UN + 1)]
    WKV = 2 * KT * HD
    with ExitStack() as st:
        wqh = sbuf(st, "wqh", [P, KT, QC * HD], FR)
        wql = sbuf(st, "wql", [P, KT, QC * HD], FR)
        wkh = sbuf(st, "wkh", [P, WKV], FR)
        wkl = sbuf(st, "wkl", [P, WKV], FR)
        woh = sbuf(st, "woh", [P, D], FR)
        wol = sbuf(st, "wol", [P, D], FR)
        kst = sbuf(st, "kst", [P, WKV + HD], F32)
        ost = sbuf(st, "ost", [P, D], F32)
        xq = sbuf(st, "xq", [P, 2, KT, P], FR)
        kTh = sbuf(st, "kTh", [P, T], FR)
        kTl = sbuf(st, "kTl", [P, T], FR)
        v2 = sbuf(st, "v2", [P, NT, 2, HD], FR)
        qs = sbuf(st, "qs", [P, T], F32)
        qTh = sbuf(st, "qTh", [P, T], FR)
        qTl = sbuf(st, "qTl", [P, T], FR)
        pr = sbuf(st, "pr", [P, 2, T], F32)
        pth = sbuf(st, "pth", [P, NT, 2, P], FR)
        ptl = sbuf(st, "ptl", [P, NT, 2, P], FR)
        oTh = sbuf(st, "oTh", [P, 2 * P], FR)
        oTl = sbuf(st, "oTl", [P, 2 * P], FR)
        vs = sbuf(st, "vs", [P, CH], F32)
        bvb = sbuf(st, "bvb", [P, HD], F32)
        bq = sbuf(st, "bq", [P, QC], F32)
        bk = sbuf(st, "bk", [P, NH], F32)
        bh = sbuf(st, "bh", [P, 1], F32)
        cz = sbuf(st, "cz", [P, P], F32)
        czb = sbuf(st, "czb", [P, P], BF16)
        idb = sbuf(st, "idb", [P, P], BF16)
        mx = sbuf(st, "mx", [P, 2, 2], F32)
        nb = sbuf(st, "nb", [P, 2], F32)
        rs = sbuf(st, "rs", [P, 2, 2], F32)
        ri = sbuf(st, "ri", [P, 4], F32)
        wq, wk, wo, x = (wqh, wql), (wkh, wkl), (woh, wol), (xTh, xTl)
        kT, qT, oT, pt = (kTh, kTl), (qTh, qTl), (oTh, oTl), (pth, ptl)
        (wq_in, wq_hi, wq_lo, k_in, o_in, wk_hi, wk_lo, wo_hi, wo_lo, xq_rdy, pj_ps, q_rdy, q_hi, q_lo, k_hi, pj_rd, v_hi, v_lo,
         s_ps, mx_s, nb_rdy, ex_rdy, rsum, rs_rdy, T_ps, pt_hi, pt_lo, pv_ps, o_hi, o_lo, y_ps, y_add, b_in,
         b_bf, bk_rdy, bv_rdy) = [sems["t_" + s] for s in SEMS["t"]]

        def scores(p, c):
            return min(CH, (TILE[p] + 1) * P - c * CH)

        def pair(p, q):
            return min(2 * CH, (TILE[p] + 1) * P - q * 2 * CH)

        def group(p, c):
            return min(TC, TILE[p] + 1 - c * TC)

        def chunks(p):
            return list(range(CK[p] - 1, -1, -1))

        def pexp(p, c):
            return (cump[p] if p >= 0 else cump[NP + p] - NPR) + PR[p] - c // 2

        def ready(i):
            m, ks = ((i - 1) // 2, (0, 1)) if i % 2 else (i // 2 - 1, (2, 3))
            return m, [k for k in ks if m >= 0 and k < CK[2 * m]]

        def done(i, first):
            m = (i - 3) // 2
            return m if i % 2 == 1 and not (m < 0 and first) else None

        def reader(p, c):
            for m in range(p // 2 - 1, -1, -1):
                if CK[2 * m] > c:
                    return cumv[m] + CK[2 * m] - c
            return 0

        with nc.Block() as block:
            @block.sync
            def _(sp):
                sp.dma_start(kst[:], d["wkv1"][:, 0, :]).then_inc(k_in, 16)
                for k in range(KT):
                    sp.dma_start(pr[:, k, :], d["wq"][:, k * T:(k + 1) * T]).then_inc(wq_in, 16)
                sp.dma_start(bq[:], d["bq1"]).then_inc(b_in, 16)
                sp.dma_start(bk[:], d["bk1"]).then_inc(b_in, 16)
                sp.dma_start(cz[:], d["causal"]).then_inc(b_in, 16)
                sp.dma_start(ost[:], d["wo1"][:, 0, :]).then_inc(o_in, 16)
                with sp.Fori(1, NH) as h:
                    sp.wait_ge(wk_hi, FROM + h)
                    sp.wait_ge(wk_lo, FROM + h)
                    sp.wait_ge(bv_rdy, FROM + h)
                    sp.dma_start(kst[:], d["wkv1"][:, bass.ds(h, 1), :].rearrange("p a b -> p (a b)")).then_inc(k_in, 16)
                    sp.wait_ge(wo_hi, FROM + h)
                    sp.wait_ge(wo_lo, FROM + h)
                    sp.dma_start(ost[:], d["wo1"][:, bass.ds(h, 1), :].rearrange("p a b -> p (a b)")).then_inc(o_in, 16)

            @block.tensor
            def _(pe):
                def unit(k, g):
                    kind, r, bank = UNITS[k]
                    if k == 0:
                        pe.wait_ge(wk_hi, FROM + g + 1)
                        pe.wait_ge(wk_lo, FROM + g + 1)
                    if kind == "q" and r == 0:
                        pe.wait_ge(xq_rdy, FROM + 2 * g + 2)
                    for e in range(k - 1, -1, -1):
                        if UNITS[e][2] == bank:
                            if UNITS[e][0] == "q":
                                pe.wait_ge(q_rdy, FROM + 4 * g + QN[e] + 1)
                            else:
                                pe.wait_ge(pj_rd, FROM + 8 * g + KN[e] + 1)
                            break
                    for j in range(1 if kind == "k" else TC):
                        n = 0
                        for kt in range(KT):
                            for a, b in PARTS:
                                if kind == "q":
                                    c = r * TC + j
                                    l, rr = wq[a][:, kt, c * HD:(c + 1) * HD], xq[:, b, kt, :]
                                elif kind == "k":
                                    l, rr = wk[a][:, kt * HD:(kt + 1) * HD], x[b][:, kt, r * CH:(r + 1) * CH]
                                else:
                                    t = r * TC + j
                                    l = x[a][:, kt, t * P:(t + 1) * P]
                                    rr = wk[b][:, (KT + kt) * HD:(KT + kt + 1) * HD]
                                o = ps[:, bank, :] if kind == "k" else ps[:, bank, j * P:(j + 1) * P]
                                m = nc.tensor.matmul(o, l, rr, start=n == 0, stop=n == 5)
                                n += 1
                    m.then_inc(pj_ps, 1)

                def qk(p, c):
                    w = scores(p, c)
                    i = TILE[p]
                    last = c == CK[p] - 1
                    for k, (a, b) in enumerate(PARTS):
                        m = nc.tensor.matmul(ps[:, c, 0:w], qT[a][:, i * P:(i + 1) * P], kT[b][:, c * CH:c * CH + w],
                                             start=k == 0, stop=k == 2 and not last)
                    if last:
                        m = nc.tensor.matmul(ps[:, c, w - P:w], idb[:], czb[:], start=False, stop=True)
                    if c % 2 == 0:
                        m.then_inc(s_ps, 1)

                def turn(p, k, h):
                    c = chunks(p)[k]
                    n = cumc[p] + k
                    pe.wait_ge(pt_lo, FROM + h * NC + n - 1)
                    if n == 0:
                        pe.wait_ge(pj_rd, FROM + 8 * h + 8)
                    pe.wait_ge(ex_rdy, FROM + h * NPR + pexp(p, c))
                    for j in range(group(p, c)):
                        t = c * TC + j
                        m = nc.tensor.transpose(ps[:, 4 + n % 2, j * P:(j + 1) * P], pr[:, p % 2, t * P:(t + 1) * P], ident[:])
                    m.then_inc(T_ps, 1)

                def pv(m, k, h):
                    A = 2 * (m % NPA)
                    c = chunks(A)[k]
                    if k == 0:
                        pe.wait_ge(o_lo, FROM + h * NPA + m)
                    if m == 0:
                        pe.wait_ge(v_lo, FROM + 4 * h + 4 - c)
                    pe.wait_ge(pt_lo, FROM + h * NC + (cumc[A + 1] if m >= 0 else cumc[A + 1] - NC) + k + 1)
                    for j in range(group(A, c)):
                        t = c * TC + j
                        n = 2 * P if t <= TILE[A + 1] else P
                        for e, (s, w) in enumerate(PARTS):
                            q = nc.tensor.matmul(ps[:, 6, 0:n], v2[:, t, s, :], pt[w][:, t, :, :].rearrange("p a b -> p (a b)")[:, 0:n],
                                                 start=k == 0 and j == 0 and e == 0,
                                                 stop=c == 0 and j == group(A, c) - 1 and e == 2, skip_group_check=True)
                    q.then_inc(pv_ps, 1)

                def project(m, h):
                    if m == 0:
                        pe.wait_ge(wo_hi, FROM + h + 1)
                        pe.wait_ge(wo_lo, FROM + h + 1)
                    pe.wait_ge(o_lo, FROM + h * NPA + m + 1)
                    pe.wait_ge(y_add, FROM + h * NP + 2 * m)
                    for e in range(2):
                        for k, (s, w) in enumerate(PARTS):
                            q = nc.tensor.matmul(ps[:, 7, e * D:(e + 1) * D], oT[s][:, e * P:(e + 1) * P], wo[w][:], start=k == 0, stop=k == 2)
                    q.then_inc(y_ps, 1)

                def tile_scores(b, h):
                    for c in chunks(b):
                        if b == 0:
                            if c == CK[0] - 1:
                                pe.wait_ge(q_hi, FROM + 4 * h + 1)
                                pe.wait_ge(q_lo, FROM + 4 * h + 1)
                            pe.wait_ge(pj_rd, FROM + 8 * h + (6 if c > 1 else 7))
                            pe.wait_ge(ex_rdy, FROM + h * NPR)
                        else:
                            if b % TC == 0 and c == CK[b] - 1:
                                pe.wait_ge(q_hi, FROM + 4 * h + b // TC + 1)
                                pe.wait_ge(q_lo, FROM + 4 * h + b // TC + 1)
                            pe.wait_ge(ex_rdy, FROM + h * NPR + pexp(b - 1, c))
                        qk(b, c)

                def step(i, h, first, last):
                    if i == 0:
                        pe.wait_ge(pt_lo, FROM + h * NC)
                        unit(UN - 1, h)
                    if i + 1 < NP:
                        tile_scores(i + 1, h)
                    elif not last:
                        tile_scores(0, h + 1)
                    m, pvs = ready(i)
                    f = done(i, first)
                    turn(i, 0, h)
                    if i % 2 == 0 and len(pvs) > 0:
                        pv(m, pvs[0], h)
                    if CK[i] > 1:
                        turn(i, 1, h)
                    if i % 2 == 0 and len(pvs) > 1:
                        pv(m, pvs[1], h)
                    if f is not None:
                        project(f, h)
                    if i in AT and not last:
                        unit(AT[i], h + 1)
                    for k in range(2, CK[i]):
                        turn(i, k, h)
                    if i % 2:
                        for k in pvs:
                            pv(m, k, h)

                def head(h, first, last):
                    for i in range(NP):
                        step(i, h, first, last)

                pe.wait_ge(wq_lo, FROM + KT)
                pe.wait_ge(b_bf, FROM + 2)
                for k in range(UN - 1):
                    unit(k, 0)
                tile_scores(0, 0)
                head(0, True, False)
                with pe.Fori(1, NH - 1) as h:
                    head(h, False, False)
                head(NH - 1, False, True)
                project(NPA - 1, NH - 1)

            @block.scalar
            def _(act):
                def unit_hi(k, g):
                    kind, r, bank = UNITS[k]
                    if kind == "k":
                        act.wait_ge(pj_ps, FROM + g * UN + k + 1)
                        nc.scalar.activation(kTh[:, r * CH:(r + 1) * CH], ps[:, bank, :], ACT.Identity, bias=bh[:, 0:1]).then_inc(k_hi, 1)
                    if kind == "v":
                        act.wait_ge(pj_rd, FROM + 8 * g + KN[k] + 1)
                        nc.scalar.activation(v2[:, r * TC:(r + 1) * TC, 0, :], vs[:].rearrange("p (t e) -> p t e", t=TC),
                                             ACT.Copy).then_inc(v_hi, 1)

                def q_split(g, n):
                    act.wait_ge(q_rdy, FROM + 4 * g + 4)
                    c = slice((3 - n) * CH, (4 - n) * CH)
                    nc.scalar.activation(qTh[:, c], qs[:, c], ACT.Copy).then_inc(q_hi, 1)

                def wk_split(g):
                    act.wait_ge(k_in, FROM + 16 * g + 16)
                    nc.scalar.activation(wkh[:], kst[:, 0:WKV], ACT.Copy).then_inc(wk_hi, 1)
                    nc.scalar.activation(bh[:, 0:1], bk[:, bass.ds(g, 1)], ACT.Copy).then_inc(bk_rdy, 1)
                    act.wait_ge(bk_rdy, FROM + g + 1)

                def hi(p, k, h):
                    c = chunks(p)[k]
                    n = cumc[p] + k
                    w = group(p, c)
                    act.wait_ge(T_ps, FROM + h * NC + n + 1)
                    if p % 2 == 0:
                        act.wait_ge(pv_ps, FROM + h * NPV + reader(p, c))
                    nc.scalar.activation(pth[:, c * TC:c * TC + w, p % 2, :], ps[:, 4 + n % 2, 0:w * P].rearrange("p (t e) -> p t e", t=w),
                                         ACT.Copy).then_inc(pt_hi, 1)

                def exps(p, q, h, start=False):
                    w = pair(p, q)
                    if q == PR[p] - 1:
                        act.wait_ge(nb_rdy, FROM + h * NP + p + 1)
                        if not start and p != 1:
                            act.wait_ge(T_ps, FROM + h * NC + (cumc[p - 1] if p else -CK[NP - 1]))
                            act.wait_ge(rs_rdy, FROM + h * NP + p - 1)
                        if p == 1:
                            act.wait_ge(T_ps, FROM + h * NC)
                            act.wait_ge(rs_rdy, FROM + h * NP)
                    nc.scalar.activation(pr[:, p % 2, q * 2 * CH:q * 2 * CH + w],
                                         ps[:, 2 * q:2 * q + 2, :].rearrange("p a b -> p (a b)")[:, 0:w], ACT.Exp,
                                         bias=nb[:, p % 2:p % 2 + 1], scale=SCALE,
                                         accum_out=rs[:, p % 2, q:q + 1]).then_inc(ex_rdy, 1)

                def out_hi(m, h):
                    act.wait_ge(pv_ps, FROM + h * NPV + (cumv[m + 1] if m >= 0 else 0))
                    act.wait_ge(y_ps, FROM + h * NPA + m)
                    nc.scalar.activation(oTh[:], ps[:, 6, 0:2 * P], ACT.Copy).then_inc(o_hi, 1)

                def step(i, h, first, last):
                    if i + 1 < NP:
                        b, g = i + 1, h
                    else:
                        b, g = 0, h + 1
                    early = 1 if i % 2 == 0 else 2
                    if i == 0:
                        unit_hi(UN - 1, h)
                    if done(i, first) is not None:
                        out_hi(done(i, first), h)
                    for k in range(min(early, CK[i])):
                        hi(i, k, h)
                    if b or not last:
                        exps(b, PR[b] - 1, g)
                    for k in range(early, min(2, CK[i])):
                        hi(i, k, h)
                    if PR[b] == 2 and (b or not last):
                        exps(b, 0, g)
                    if i in AT and not last:
                        unit_hi(AT[i], h + 1)
                    for k in range(2, CK[i]):
                        hi(i, k, h)
                    if i == 2:
                        act.wait_ge(y_ps, FROM + h * NPA)
                        act.wait_ge(o_in, FROM + 16 * h + 16)
                        nc.scalar.activation(woh[:], ost[:], ACT.Copy).then_inc(wo_hi, 1)
                    if i in QAT:
                        q_split(h, QAT[i])
                    if i == 2 and not last:
                        wk_split(h + 1)
                    if i == QNEXT and not last:
                        q_split(h + 1, 0)

                for k in range(KT):
                    act.wait_ge(wq_in, FROM + 32)
                    nc.scalar.activation(wqh[:, k, :], pr[:, k, :], ACT.Copy).then_inc(wq_hi, 1)
                act.wait_ge(b_in, FROM + 48)
                nc.scalar.activation(czb[:], cz[:], ACT.Copy).then_inc(b_bf, 1)
                nc.scalar.activation(idb[:], ident[:], ACT.Copy).then_inc(b_bf, 1)
                wk_split(0)
                for k in range(UN - 1):
                    unit_hi(k, 0)
                q_split(0, 0)
                exps(0, 1, 0, True)
                exps(0, 0, 0, True)
                for i in range(NP):
                    step(i, 0, True, False)
                with act.Fori(1, NH - 1) as h:
                    for i in range(NP):
                        step(i, h, False, False)
                for i in range(NP):
                    step(i, NH - 1, False, True)
                out_hi(NPA - 1, NH - 1)

            @block.gpsimd
            def _(pool):
                def wk_split(g):
                    pool.wait_ge(wk_hi, FROM + g + 1)
                    pool.wait_ge(pj_rd, FROM + 8 * g)
                    nc.gpsimd.tensor_tensor(wkl[:], kst[:, 0:WKV], wkh[:].bitcast(F32), ALU.subtract).then_inc(wk_lo, 1)
                    nc.gpsimd.tensor_copy(bvb[:], kst[:, WKV:WKV + HD]).then_inc(bv_rdy, 1)
                    for b in range(2):
                        nc.gpsimd.tensor_copy(xq[:, b, :, :], x[b][:, :, bass.ds(g * P, P)].bitcast(F32)).then_inc(xq_rdy, 1)

                def unit_lo(k, g):
                    kind, r, bank = UNITS[k]
                    if kind == "v":
                        pool.wait_ge(v_hi, FROM + 4 * g + 4 - r)
                        nc.gpsimd.tensor_tensor(v2[:, r * TC:(r + 1) * TC, 1, :], vs[:].rearrange("p (t e) -> p t e", t=TC),
                                                v2[:, r * TC:(r + 1) * TC, 0, :].bitcast(F32), ALU.subtract).then_inc(v_lo, 1)

                def step(i, h, last):
                    if i == 0:
                        unit_lo(UN - 1, h)
                    if i == 2:
                        pool.wait_ge(wo_hi, FROM + h + 1)
                        nc.gpsimd.tensor_tensor(wol[:], ost[:], woh[:].bitcast(F32), ALU.subtract).then_inc(wo_lo, 1)
                    if i == 2 and not last:
                        wk_split(h + 1)
                    if i in AT and not last:
                        unit_lo(AT[i], h + 1)

                wk_split(0)
                for k in range(UN - 1):
                    unit_lo(k, 0)
                for i in range(NP):
                    step(i, 0, False)
                with pool.Fori(1, NH - 1) as h:
                    for i in range(NP):
                        step(i, h, False)
                for i in range(NP):
                    step(i, NH - 1, True)

            @block.vector
            def _(dve):
                def unit_lo(k, g):
                    kind, r, bank = UNITS[k]
                    if kind == "q":
                        dve.wait_ge(pj_ps, FROM + g * UN + k + 1)
                        dve.wait_ge(q_lo, FROM + 4 * g)
                        nc.vector.tensor_tensor(qs[:].rearrange("p (t c) -> p c t", c=QC)[:, r * TC:(r + 1) * TC, :],
                                                ps[:, bank, :].rearrange("p (c t) -> p c t", c=TC),
                                                bq[:, r * TC:(r + 1) * TC].unsqueeze(2).broadcast_to([P, TC, P]),
                                                ALU.add).then_inc(q_rdy, 1)
                        return
                    if kind == "k":
                        dve.wait_ge(k_hi, FROM + g * 4 + 4 - r)
                        s = slice(r * CH, (r + 1) * CH)
                        nc.vector.scalar_tensor_tensor(kTl[:, s], ps[:, bank, :], bh[:, 0:1], kTh[:, s].bitcast(F32),
                                                       ALU.add, ALU.subtract).then_inc(pj_rd, 1)
                    else:
                        dve.wait_ge(pj_ps, FROM + g * UN + k + 1)
                        dve.wait_ge(bv_rdy, FROM + g + 1)
                        dve.wait_ge(v_lo, FROM + g * 4 + 3 - r)
                        nc.vector.tensor_tensor(vs[:].rearrange("p (t e) -> p t e", t=TC), ps[:, bank, :].rearrange("p (t e) -> p t e", t=TC),
                                                bvb[:].unsqueeze(1).broadcast_to([P, TC, HD]), ALU.add).then_inc(pj_rd, 1)

                def q_split(g, n):
                    c = slice((3 - n) * CH, (4 - n) * CH)
                    dve.wait_ge(q_hi, FROM + 4 * g + n + 1)
                    nc.vector.tensor_tensor(qTl[:, c], qs[:, c], qTh[:, c].bitcast(F32), ALU.subtract).then_inc(q_lo, 1)

                def maximum(p, q, h):
                    dve.wait_ge(s_ps, FROM + h * NPR + cump[p] + PR[p] - q)
                    nc.vector.tensor_reduce(mx[:, p % 2, q:q + 1], ps[:, 2 * q:2 * q + 2, :].rearrange("p a b -> p (a b)")[:, 0:pair(p, q)],
                                            AX.X, ALU.max).then_inc(mx_s, 1)

                def bias(p, h):
                    dve.wait_ge(mx_s, FROM + h * NPR + cump[p + 1])
                    if PR[p] == 2:
                        nc.vector.tensor_scalar(nb[:, p % 2:p % 2 + 1], mx[:, p % 2, 0:1], mx[:, p % 2, 1:2], -SCALE,
                                                ALU.max, ALU.mult).then_inc(nb_rdy, 1)
                    else:
                        nc.vector.tensor_scalar(nb[:, p % 2:p % 2 + 1], mx[:, p % 2, 0:1], -SCALE, None, ALU.mult).then_inc(nb_rdy, 1)

                def lo(p, k, h):
                    c = chunks(p)[k]
                    n = cumc[p] + k
                    w = group(p, c)
                    dve.wait_ge(pt_hi, FROM + h * NC + n + 1)
                    s = slice(c * TC, c * TC + w)
                    nc.vector.tensor_tensor(ptl[:, s, p % 2, :], ps[:, 4 + n % 2, 0:w * P].rearrange("p (t e) -> p t e", t=w),
                                            pth[:, s, p % 2, :].bitcast(F32), ALU.subtract).then_inc(pt_lo, 1)

                def row_sum(q, h):
                    dve.wait_ge(ex_rdy, FROM + h * NPR + cump[q + 1])
                    src = rs[:, q % 2, 0:1]
                    if PR[q] == 2:
                        nc.vector.tensor_tensor(src, src, rs[:, q % 2, 1:2], ALU.add).then_inc(rsum, 1)
                        dve.wait_ge(rsum, FROM + h * TWO + q + 1)
                    nc.vector.reciprocal(ri[:, q % 4:q % 4 + 1], src).then_inc(rs_rdy, 1)

                def out_lo(m, h):
                    dve.wait_ge(o_hi, FROM + h * NPA + m + 1)
                    nc.vector.tensor_tensor(oTl[:], ps[:, 6, 0:2 * P], oTh[:].bitcast(F32), ALU.subtract).then_inc(o_lo, 1)

                def add(f, h):
                    q = f % NP
                    t = TILE[q]
                    dve.wait_ge(y_ps, FROM + h * NPA + f // 2 + 1)
                    dve.wait_ge(rs_rdy, FROM + h * NP + f + 1)
                    dve.wait_ge(y_add, FROM + h * NP + max(f - 1, 0) if f >= 0 else FROM + h * NP + f - 1)
                    nc.vector.scalar_tensor_tensor(acc[:, t, :], ps[:, 7, (f % 2) * D:(f % 2 + 1) * D], ri[:, q % 4:q % 4 + 1],
                                                   acc[:, t, :], ALU.mult, ALU.add).then_inc(y_add, 1)

                def tile_bias(b, h):
                    for q in range(PR[b] - 1, -1, -1):
                        maximum(b, q, h)
                    bias(b, h)

                def step(i, h, first, last):
                    m = done(i, first)
                    if i == 0:
                        unit_lo(UN - 1, h)
                    if m is not None:
                        out_lo(m, h)
                    if i + 1 < NP:
                        tile_bias(i + 1, h)
                    elif not last:
                        tile_bias(0, h + 1)
                    for k in range(min(2, CK[i])):
                        lo(i, k, h)
                    row_sum(i, h)
                    if i in AT and not last:
                        unit_lo(AT[i], h + 1)
                    for k in range(2, CK[i]):
                        lo(i, k, h)
                    if m is not None:
                        add(2 * m, h)
                        add(2 * m + 1, h)
                    if i in QAT:
                        q_split(h, QAT[i])
                    if i == QNEXT and not last:
                        q_split(h + 1, 0)

                def head(h, first, last):
                    for i in range(NP):
                        step(i, h, first, last)

                for k in range(KT):
                    dve.wait_ge(wq_hi, FROM + k + 1)
                    nc.vector.tensor_tensor(wql[:, k, :], pr[:, k, :], wqh[:, k, :].bitcast(F32), ALU.subtract).then_inc(wq_lo, 1)
                dve.wait_ge(b_in, FROM + 48)
                for k in range(UN - 1):
                    unit_lo(k, 0)
                q_split(0, 0)
                tile_bias(0, 0)
                head(0, True, False)
                with dve.Fori(1, NH - 1) as h:
                    head(h, False, False)
                head(NH - 1, False, True)
                h = NH - 1
                out_lo(NPA - 1, h)
                add(NP - 2, h)
                add(NP - 1, h)


def experts(nc, d, acc, xTh, xTl, ident, cb, ps, sem, sems, sbuf):
    RING = 3
    U = NCH * GT
    W1, W3, W2, SEL = 0, KT * P, 2 * KT * P, GW
    TWC = GW + P
    LAG = 2
    with ExitStack() as st:
        wst = sbuf(st, "est", [P, GT, TWC], F32)
        wh = sbuf(st, "ewh", [P, GT, TWC], FR)
        wl = sbuf(st, "ewl", [P, GT, TWC], FR)
        cT32 = sbuf(st, "cT32", [P, TC, P], F32)
        cTh = sbuf(st, "cTh", [P, T], FR)
        cTl = sbuf(st, "cTl", [P, T], FR)
        th = sbuf(st, "eth", [P, 2, CH], F32)
        h32 = sbuf(st, "eh32", [P, 3, CH], F32)
        hh = sbuf(st, "ehh", [P, RING, CH], FR)
        hl = sbuf(st, "ehl", [P, RING, CH], FR)
        w, x, c, hp = (wh, wl), (xTh, xTl), (cTh, cTl), (hh, hl)
        (cp, cT_ps, ct_hi, ct_lo, w_in, w_hi, w_lo, g_ps, u_ps, c_ps, th_rdy, s_rdy, h_rdy, hc_rdy, h_hi, h_lo, y_ps, y_add) = [
            sems["e_" + s] for s in SEMS["e"]]

        with nc.Block() as block:
            @block.sync
            def _(sp):
                sp.dma_start(wst[:], d["wexp"][:, 0:GT, :]).then_inc(w_in, 16)
                with sp.Fori(1, NG) as g:
                    sp.wait_ge(w_hi, FROM + g * GT)
                    sp.wait_ge(w_lo, FROM + g * GT)
                    sp.dma_start(wst[:], d["wexp"][:, bass.ds(g * GT, GT), :]).then_inc(w_in, 16)

            @block.tensor
            def _(pe):
                for n in range(NCH):
                    pe.wait_ge(cp, FROM + n + 2)
                    if n:
                        pe.wait_ge(ct_lo, FROM + n)
                    for j in range(TC):
                        m = nc.tensor.transpose(ps[:, 0, j * P:(j + 1) * P], cT32[:, j, :], ident[:])
                    m.then_inc(cT_ps, 1)
                pe.wait_ge(ct_lo, FROM + NCH)
                with pe.Fori(0, NG) as g:
                    def up(u):
                        ch, k = divmod(u, GT)
                        if ch == 0:
                            pe.wait_ge(w_hi, FROM + g * GT + k + 1)
                            pe.wait_ge(w_lo, FROM + g * GT + k + 1)
                        if u >= 2:
                            pe.wait_ge(hc_rdy, FROM + g * U + u - 1)
                        else:
                            pe.wait_ge(hc_rdy, FROM + g * U)
                        bank = 3 * (u % 2)
                        for z, (col, s) in enumerate(((W1, g_ps), (W3, u_ps))):
                            i = 0
                            for kt in range(KT):
                                for a, b in PARTS:
                                    m = nc.tensor.matmul(ps[:, bank + z, :], w[a][:, k, col + kt * P:col + (kt + 1) * P],
                                                         x[b][:, kt, ch * CH:(ch + 1) * CH], start=i == 0, stop=i == 5)
                                    i += 1
                            m.then_inc(s, 1)
                        for i in range(2):
                            m = nc.tensor.matmul(ps[:, bank + 2, :], wh[:, k, SEL:SEL + P], c[i][:, ch * CH:(ch + 1) * CH],
                                                 start=i == 0, stop=i == 1)
                        m.then_inc(c_ps, 1)

                    def down(u):
                        ch, k = divmod(u, GT)
                        pe.wait_ge(h_lo, FROM + g * U + u + 1)
                        if k == 0:
                            pe.wait_ge(y_add, FROM + g * NCH + ch)
                        for t in range(TC):
                            for i, (a, b) in enumerate(PARTS):
                                m = nc.tensor.matmul(ps[:, 6 + t // 2, (t % 2) * D:(t % 2 + 1) * D],
                                                     hp[a][:, u % RING, t * P:(t + 1) * P], w[b][:, k, W2:W2 + D],
                                                     start=k == 0 and i == 0 and t % 2 == 0, stop=k == GT - 1 and i == 2,
                                                     skip_group_check=True)
                        m.then_inc(y_ps, 1)

                    for u in range(U + LAG):
                        if u < U:
                            up(u)
                        if u >= LAG:
                            down(u - LAG)

            @block.scalar
            def _(act):
                for n in range(NCH):
                    act.wait_ge(cT_ps, FROM + n + 1)
                    nc.scalar.activation(cTh[:, n * CH:(n + 1) * CH], ps[:, 0, :], ACT.Copy).then_inc(ct_hi, 1)

                with act.Fori(0, NG) as g:
                    act.wait_ge(w_in, FROM + 16 * g + 16)
                    for k in range(GT):
                        act.wait_ge(y_ps, FROM + g * U)
                        nc.scalar.activation(wh[:, k, :], wst[:, k, :], ACT.Copy).then_inc(w_hi, 1)

                    def split(u):
                        act.wait_ge(hc_rdy, FROM + g * U + u + 1)
                        if u >= RING:
                            act.wait_ge(y_ps, FROM + g * U + u - RING + 1)
                        nc.scalar.activation(hh[:, u % RING, :], h32[:, u % 3, :], ACT.Copy).then_inc(h_hi, 1)

                    for u in range(U + 1):
                        if u < U:
                            act.wait_ge(g_ps, FROM + g * U + u + 1)
                            act.wait_ge(h_rdy, FROM + g * U + max(u - 1, 0))
                            nc.scalar.activation(th[:, u % 2, :], ps[:, 3 * (u % 2), :], ACT.Tanh, scale=0.5).then_inc(th_rdy, 1)
                        if u:
                            split(u - 1)

            @block.gpsimd
            def _(pool):
                with pool.Fori(0, NG) as g:
                    for u in range(U):
                        pool.wait_ge(h_hi, FROM + g * U + u + 1)
                        nc.gpsimd.tensor_tensor(hl[:, u % RING, :], h32[:, u % 3, :], hh[:, u % RING, :].bitcast(F32),
                                                ALU.subtract).then_inc(h_lo, 1)

            @block.vector
            def _(dve):
                nc.vector.memset(cT32[:], 0.0).then_inc(cp, 1)
                dve.wait_ge(cp, FROM + 1)
                for n in range(NCH):
                    if n:
                        dve.wait_ge(cT_ps, FROM + n)
                    nc.vector.tensor_copy(cT32[:, :, 0:E + 1], cb[:, n * TC:(n + 1) * TC, :]).then_inc(cp, 1)
                    dve.wait_ge(ct_hi, FROM + n + 1)
                    nc.vector.tensor_tensor(cTl[:, n * CH:(n + 1) * CH], ps[:, 0, :], cTh[:, n * CH:(n + 1) * CH].bitcast(F32),
                                            ALU.subtract).then_inc(ct_lo, 1)
                with dve.Fori(0, NG) as g:
                    for k in range(GT):
                        dve.wait_ge(w_hi, FROM + g * GT + k + 1)
                        nc.vector.tensor_tensor(wl[:, k, :], wst[:, k, :], wh[:, k, :].bitcast(F32), ALU.subtract).then_inc(w_lo, 1)
                    for u in range(U):
                        n = g * U + u
                        ch, k = divmod(u, GT)
                        bank = 3 * (u % 2)
                        t = th[:, u % 2, :]
                        h = h32[:, u % 3, :]
                        dve.wait_ge(th_rdy, FROM + n + 1)
                        nc.vector.scalar_tensor_tensor(t, t, 1.0, ps[:, bank, :], ALU.add, ALU.mult).then_inc(s_rdy, 1)
                        dve.wait_ge(s_rdy, FROM + n + 1)
                        dve.wait_ge(u_ps, FROM + n + 1)
                        dve.wait_ge(h_lo, FROM + g * U + max(u - 2, 0))
                        nc.vector.scalar_tensor_tensor(h, t, 0.5, ps[:, bank + 1, :], ALU.mult, ALU.mult).then_inc(h_rdy, 1)
                        dve.wait_ge(h_rdy, FROM + n + 1)
                        dve.wait_ge(c_ps, FROM + n + 1)
                        nc.vector.tensor_tensor(h, h, ps[:, bank + 2, :], ALU.mult).then_inc(hc_rdy, 1)

                        def add(chunk):
                            a = acc[:, chunk * TC:(chunk + 1) * TC, :].rearrange("p a b -> p (a b)")
                            dve.wait_ge(y_ps, FROM + g * U + (chunk + 1) * GT)
                            dve.wait_ge(y_add, FROM + g * NCH + chunk)
                            nc.vector.tensor_tensor(a, a, ps[:, 6:8, :].rearrange("p a b -> p (a b)"), ALU.add).then_inc(y_add, 1)

                        if k == 1 and ch:
                            add(ch - 1)
                        if u == U - 1:
                            add(ch)


_OUTS = [((1, T, D), "float32")]


def kernel(**inputs):
    import numpy as np
    import concourse.bacc as bacc
    from concourse.bass_utils import run_bass_kernel_spmd

    g = {k: np.asarray(v) for k, v in inputs.items()}

    def rows(w):
        return w.reshape(-1, P, w.shape[1]).transpose(1, 0, 2)

    gate = g["L0_ffn_w_gate"].reshape(KT, P, SG, P, 4).transpose(1, 2, 4, 0, 3)
    up = g["L0_ffn_w_up"].reshape(KT, P, SG, P, 4).transpose(1, 2, 4, 0, 3)
    down = g["L0_ffn_w_down"].reshape(SG, P, 4, D).transpose(1, 0, 2, 3)
    w0 = np.concatenate([
        rows(g["L0_attn_q_w"].T).reshape(P, -1), rows(g["L0_attn_o_w"].T).reshape(P, -1),
        np.concatenate([rows(g["L0_attn_k_w"].T), rows(g["L0_attn_v_w"].T)], 2).reshape(P, -1),
        np.stack([gate, up], 3).reshape(P, -1), down.reshape(P, -1)], 1)

    wk = rows(g["L1_attn_Wk"]).reshape(P, KT, NH, HD).transpose(0, 2, 1, 3)
    wv = rows(g["L1_attn_Wv"]).reshape(P, KT, NH, HD).transpose(0, 2, 1, 3)
    wo = g["L1_attn_Wo"].reshape(NH, HD, D).transpose(1, 0, 2)
    bv = np.broadcast_to(g["L1_attn_bv"].reshape(1, NH, HD), (P, NH, HD))
    wkv = np.concatenate([wk.reshape(P, NH, -1), wv.reshape(P, NH, -1), bv], 2)
    wq = rows(g["L1_attn_Wq"]).reshape(P, -1)

    pad = NI1 * P - ROWS
    zero = np.zeros((pad, D), g["L1_ffn_W1"].dtype)

    def units(routed, shared):
        return np.concatenate([routed.reshape(-1, D), shared, zero], 0)

    w1 = units(g["L1_ffn_W1"], g["L1_ffn_Ws1"]).reshape(NI1, P, KT, P).transpose(3, 0, 2, 1)
    w3 = units(g["L1_ffn_W3"], g["L1_ffn_Ws3"]).reshape(NI1, P, KT, P).transpose(3, 0, 2, 1)
    w2 = units(g["L1_ffn_W2"].transpose(0, 2, 1), g["L1_ffn_Ws2"].T).reshape(NI1, P, D).transpose(1, 0, 2)
    owner = np.minimum(np.arange(ROWS) // INTER1, E)
    sel = np.zeros((P, NI1 * P), np.float32)
    sel[owner, np.arange(ROWS)] = 1.0
    wexp = np.concatenate([w1.reshape(P, NI1, -1), w3.reshape(P, NI1, -1), w2, sel.reshape(P, NI1, P)], 2)

    i = np.arange(P)
    data = {
        "x": g["L0_attn_hidden_states"], "w0": w0, "bq0": g["L0_attn_q_b"].reshape(KT, P).T,
        "bkv0": np.concatenate([g["L0_attn_k_b"], g["L0_attn_v_b"]]), "bo0": g["L0_attn_o_b"],
        "wq": wq, "wkv1": wkv, "wo1": wo, "bq1": g["L1_attn_bq"].reshape(QC, HD).T, "bk1": g["L1_attn_bk"].reshape(NH, HD).T,
        "bo1": g["L1_attn_bo"], "wg": rows(g["L1_ffn_Wg"].T), "wexp": wexp,
        "ident": np.eye(P, dtype=np.float32), "bd": (i[:, None] // 16 == i[None, :] // 16).astype(np.float32),
        "causal": np.where(i[None, :] > i[:, None], np.float32(NEG), np.float32(0.0)),
        "tie": (i[None, :E] < i[:E, None]).astype(np.float32).reshape(-1),
    }
    nc = bacc.Bacc("TRN2", target_bir_lowering=False, num_devices=1)
    arrays, aps = {}, {}
    for name, a in data.items():
        a = np.ascontiguousarray(a)
        arrays["in_" + name] = a
        aps[name] = nc.dram_tensor("in_" + name, a.shape, mybir.dt.from_np(a.dtype), kind="ExternalInput").ap()
    out = nc.dram_tensor("out", _OUTS[0][0], F32, kind="ExternalOutput").ap()
    build(nc, aps, out)
    r = run_bass_kernel_spmd(nc, [arrays], core_ids=[0])
    return r.results[0]["out"]
```

```python
from contextlib import ExitStack

import concourse.bass as bass
from concourse import mybir

F32 = mybir.dt.float32
FR = mybir.dt.float32r
BF16 = mybir.dt.bfloat16
ALU = mybir.AluOpType
ACT = mybir.ActivationFunctionType
AX = mybir.AxisListType

P = 128
T = 2048
D = 256
KT = D // P
NT = T // P
CH = 512
NCH = T // CH
TC = CH // P

INTER0 = 1024
NI0 = INTER0 // P
SG = NI0 // 4
OFF_Q = 0
OFF_O = OFF_Q + KT * D
OFF_KV = OFF_O + KT * D
OFF_GU = OFF_KV + KT * 2 * D
OFF_DN = OFF_GU + NI0 * 2 * KT * P
W0_COLS = OFF_DN + NI0 * D
STG = 2048

NH = 16
HD = 128
QC = NH
SCALE = float(1.0 / (HD ** 0.5))
NEG = -1.0e30
FROM = 1

E = 16
INTER1 = 176
SHARED = 352
ROWS = E * INTER1 + SHARED
NI1 = -(-ROWS // P)
GT = 5
NG = NI1 // GT
GW = 3 * D
GCOLS = GT * (GW + P)


SEMS = {
    "a": ("xn_rdy xT_ps xh_rdy xl_rdy q_ps kv_ps qs_rdy kvs_rdy vh_rdy vl_rdy rel_rdy mn_rdy ex_rdy "
          "f_rdy f_hi f_lo kva_ps kva_add gu_ps th_rdy s_rdy h_rdy ab_rdy win_rdy cnt_rdy hm_rdy "
          "hs_hi hs_lo y_ps y_add").split(),
    "b": ("wg_in wg_hi wg_lo kz_rdy kz_hi kz_lo nd_ps den_rdy rec_rdy at_rdy aT_ps at_hi at_lo o_ps ob_add o_add "
          "bs_rdy ag_rdy sd xn_rdy xT_ps x_hi x_lo lg_ps lg_rdy b1_add").split(),
    "r": "tie_in mx_rdy ex_rdy v_rdy c_rdy".split(),
    "t": ("wq_in wq_hi wq_lo k_in o_in wk_hi wk_lo wv_hi wv_lo wo_hi wo_lo xq_rdy pj_ps q_a q_rdy q_hi q_lo k_hi pj_rd v_a v_hi v_lo s_ps mx_s "
          "nb_rdy ex_rdy rsum rs_rdy T_ps pt_hi pt_lo pv_ps o_hi o_lo y_ps y_add b_in b_bf bk_rdy bv_rdy").split(),
    "e": ("cp cT_ps ct_hi ct_lo w_in w_hi w_lo g_ps u_ps c_ps th_rdy s_rdy h_rdy hc_rdy h_hi h_lo y_ps y_add").split(),
}


def build(nc, d, out):
    with ExitStack() as top:
        def sem(name):
            return top.enter_context(nc.semaphore(name))

        def sbuf(stack, name, shape, dt):
            return stack.enter_context(nc.sbuf_tensor(name, shape, dt))

        sems = {f"{k}_{s}": sem(f"{k}_{s}") for k, names in SEMS.items() for s in names}

        acc = sbuf(top, "acc", [P, NT, D], F32)
        xTh = sbuf(top, "xTh", [P, KT, T], FR)
        xTl = sbuf(top, "xTl", [P, KT, T], FR)
        ident = sbuf(top, "ident", [P, P], F32)
        lg = sbuf(top, "lg", [P, NT, E], F32)
        cb = sbuf(top, "cb", [P, NT, E + 1], F32)
        ps = top.enter_context(nc.psum_tensor("ps", [P, 8, CH], F32))
        mv = sbuf(top, "mv", [P, NT, 2], F32)
        rstd = sbuf(top, "rstd", [P, NT], F32)

        layer0(nc, top, d, acc, xTh, xTl, ident, lg, cb, ps, mv, rstd, sem, sems, sbuf)
        attention(nc, d, acc, xTh, xTl, ident, lg, cb, ps, sem, sems, sbuf)
        experts(nc, d, acc, xTh, xTl, ident, cb, ps, sem, sems, sbuf)

        stored = sem("stored")
        with nc.Block() as block:
            @block.sync
            def _(sp):
                sp.dma_start(out[0].rearrange("(t p) d -> p t d", p=P), acc[:]).then_inc(stored, 16)
                sp.wait_ge(stored, 16)


def layer0(nc, top, d, acc, xTh, xTl, ident, lg, cb, ps, mv, rstd, sem, sems, sbuf):
    with ExitStack() as st:
        wh = sbuf(st, "w0h", [P, W0_COLS], FR)
        wl = sbuf(st, "w0l", [P, W0_COLS], FR)
        bqc = sbuf(st, "bqc", [P, KT], F32)
        bkv = sbuf(st, "bkv", [P, 2 * D], F32)
        bo = sbuf(st, "bo0", [P, D], F32)
        bd = sbuf(st, "bd", [P, P], F32)
        kvacc = sbuf(st, "kvacc", [P, KT, P + 2], F32)
        vh = sbuf(st, "vh", [P, TC, KT, P + 2], FR)
        vl = sbuf(st, "vl", [P, TC, KT, P + 2], FR)

        x_in, w_in, c_in = sem("x_in"), [sem("w_in0"), sem("w_in1")], sem("c_in")
        w_hi, w_lo = sem("w_hi"), sem("w_lo")
        st_done, ag_done, sd_done, rs_done, ms_done = (
            sem("st_done"), sem("ag_done"), sem("sd_done"), sem("rs_done"), sem("ms_done"))

        with ExitStack() as s0:
            stg = sbuf(s0, "stg", [P, 2, STG], F32)
            bst = sbuf(s0, "bst", [P, NT, 6], F32)
            with nc.Block() as block:
                @block.sync
                def _(sp):
                    for h in range(4):
                        sp.dma_start(acc[:, 4 * h:4 * h + 4, :],
                                     d["x"][0, h * CH:(h + 1) * CH].rearrange("(t p) d -> p t d", p=P)).then_inc(x_in, 16)
                    for k in range(W0_COLS // STG):
                        if k >= 2:
                            sp.wait_ge(w_hi, k - 1)
                            sp.wait_ge(w_lo, k - 1)
                        sp.dma_start(stg[:, k % 2, :], d["w0"][:, k * STG:(k + 1) * STG]).then_inc(w_in[k % 2], 16)
                    sp.dma_start(ident[:], d["ident"]).then_inc(c_in, 16)
                    sp.dma_start(bd[:], d["bd"]).then_inc(c_in, 16)
                    sp.dma_start(bqc[:], d["bq0"]).then_inc(c_in, 16)
                    sp.dma_start(bkv[:], d["bkv0"].partition_broadcast(P)).then_inc(c_in, 16)
                    sp.dma_start(bo[:], d["bo0"].partition_broadcast(P)).then_inc(c_in, 16)
                    sp.wait_ge(c_in, 80)

                @block.gpsimd
                def _(pool):
                    for s in sems.values():
                        pool.sem_inc(s, FROM)
                    nc.gpsimd.memset(kvacc[:], 0.0)
                    nc.gpsimd.memset(vh[:].bitcast(F32), 1.0)
                    nc.gpsimd.memset(vl[:].bitcast(F32), 0.0)

                @block.scalar
                def _(act):
                    act.wait_ge(sd_done, 1)
                    nc.scalar.activation(rstd[:], rstd[:], ACT.Sqrt).then_inc(sd_done, 1)
                    for k in range(W0_COLS // STG):
                        act.wait_ge(w_in[k % 2], 16 * (k // 2 + 1))
                        nc.scalar.activation(wh[:, k * STG:(k + 1) * STG], stg[:, k % 2, :], ACT.Copy).then_inc(w_hi, 1)

                @block.vector
                def _(dve):
                    dve.wait_ge(x_in, 64)
                    with dve.Fori(0, NT) as i:
                        nc.vector.bn_stats(bst[:, bass.ds(i, 1), :], acc[:, bass.ds(i, 1), :]).then_inc(st_done, 1)
                    dve.wait_ge(st_done, NT)
                    for i in range(NT):
                        nc.vector.bn_aggr(mv[:, i, :], bst[:, i, :]).then_inc(ag_done, 1)
                    dve.wait_ge(ag_done, NT)
                    nc.vector.tensor_scalar(rstd[:], mv[:, :, 1], 1e-5, None, ALU.add).then_inc(sd_done, 1)
                    dve.wait_ge(sd_done, 2)
                    nc.vector.reciprocal(rstd[:], rstd[:]).then_inc(rs_done, 1)
                    for k in range(W0_COLS // STG):
                        dve.wait_ge(w_hi, k + 1)
                        nc.vector.tensor_tensor(wl[:, k * STG:(k + 1) * STG], stg[:, k % 2, :],
                                                wh[:, k * STG:(k + 1) * STG].bitcast(F32), ALU.subtract).then_inc(w_lo, 1)

        layer0_chunks(nc, d, acc, xTh, xTl, ident, ps, mv, rstd, wh, wl, bqc, bkv, kvacc, vh, vl, sems, sbuf)
        layer0_out(nc, d, acc, xTh, xTl, ident, lg, cb, ps, mv, rstd, wh, wl, bo, bd, kvacc, sems, sbuf)


PARTS = ((0, 0), (0, 1), (1, 0))


def layer0_chunks(nc, d, acc, qfh, qfl, ident, ps, mv, rstd, wh, wl, bqc, bkv, kvacc, vh, vl, sems, sbuf):
    with ExitStack() as st:
        xn = sbuf(st, "xn", [P, TC, D], F32)
        xh = sbuf(st, "xh", [P, KT, CH], FR)
        xl = sbuf(st, "xl", [P, KT, CH], FR)
        qs = xn[:].rearrange("p t d -> p (t d)").rearrange("p (a b) -> p a b", a=KT)
        kvs = sbuf(st, "kvs", [P, TC, 2 * D], F32)
        rel = sbuf(st, "rel", [P, 2, 2 * CH], F32)
        mn = sbuf(st, "mn", [P, 2, 2 * CH], F32)
        kfh = sbuf(st, "kfh", [P, TC, D], FR)
        kfl = sbuf(st, "kfl", [P, TC, D], FR)
        th = sbuf(st, "th", [P, 2, CH], F32)
        hh32 = sbuf(st, "hh32", [P, 4, CH], F32)
        ab = rel[:].rearrange("p s (a b) -> p (s a) b", a=2)
        win = sbuf(st, "win", [P, 6, CH], BF16)
        cnt = mn[:, 0, :].bitcast(BF16).rearrange("p (a b) -> p a b", a=4)
        hh = (hh32[:], kvs[:].rearrange("p t d -> p (t d)").rearrange("p (a b) -> p a b", a=4))
        hsh = sbuf(st, "hsh", [P, 4, CH], FR)
        hsl = sbuf(st, "hsl", [P, 4, CH], FR)
        w = (wh, wl)
        x = (xh, xl)
        kf, v, hs = (kfh, kfl), (vh, vl), (hsh, hsl)

        (xn_rdy, xT_ps, xh_rdy, xl_rdy, q_ps, kv_ps, qs_rdy, kvs_rdy, vh_rdy, vl_rdy, rel_rdy, mn_rdy, ex_rdy,
         f_rdy, f_hi, f_lo, kva_ps, kva_add, gu_ps, th_rdy, s_rdy, h_rdy, ab_rdy, win_rdy, cnt_rdy, hm_rdy,
         hs_hi, hs_lo, y_ps, y_add) = [sems["a_" + s] for s in SEMS["a"]]

        def feat(s, buf):
            return buf[:, s, :]

        qpre = xn[:].rearrange("p t d -> p (t d)")
        kpre = kvs[:, :, 0:D]

        def feature(s, n):
            f = feat(s, mn).rearrange("p (a b) -> p a b", a=TC if s else KT)
            if s == 0:
                return f, qfh[:, :, bass.ds(n * CH, CH)], qfl[:, :, bass.ds(n * CH, CH)]
            return f, kfh[:], kfl[:]

        def gate_bank(i):
            return 2 + 2 * ((i + 1) % 3)

        with nc.Block() as block:
            @block.tensor
            def _(pe):
                def turn(n, first=False):
                    if not first:
                        pe.wait_ge(h_rdy, FROM + n * NI0 - 2)
                    for kt in range(KT):
                        for j in range(TC):
                            pe.wait_ge(xn_rdy, FROM + n * TC + j + 1)
                            m = nc.tensor.transpose(ps[:, 2 + kt, j * P:(j + 1) * P], xn[:, j, kt * P:(kt + 1) * P], ident[:])
                        m.then_inc(xT_ps, 1)

                def queries(n, first=False):
                    if not first:
                        pe.wait_ge(h_rdy, FROM + n * NI0 - 1)
                    pe.wait_ge(xh_rdy, FROM + n * KT + KT)
                    pe.wait_ge(xl_rdy, FROM + n * KT + KT)
                    for m2 in range(KT):
                        k = 0
                        for kt in range(KT):
                            for a, b in PARTS:
                                o = OFF_Q + kt * D + m2 * P
                                m = nc.tensor.matmul(ps[:, 4 + m2, :], w[a][:, o:o + P], x[b][:, kt, :],
                                                     start=k == 0, stop=k == 5)
                                k += 1
                        m.then_inc(q_ps, 1)

                def keys_values(n):
                    pe.wait_ge(h_rdy, FROM + n * NI0)
                    for j in range(TC):
                        k = 0
                        for kt in range(KT):
                            for a, b in PARTS:
                                o = OFF_KV + kt * 2 * D
                                m = nc.tensor.matmul(ps[:, 2 + (4 + j) % 6, :], x[a][:, kt, j * P:(j + 1) * P], w[b][:, o:o + 2 * D],
                                                     start=k == 0, stop=k == 5)
                                k += 1
                        m.then_inc(kv_ps, 1)

                def gate_up(n, i):
                    bank = gate_bank(i)
                    if i == 0:
                        pe.wait_ge(qs_rdy, FROM + n * KT + KT)
                    elif i < 3:
                        pe.wait_ge(kvs_rdy, FROM + n * TC + 2 * i)
                    else:
                        pe.wait_ge(h_rdy, FROM + n * NI0 + i - 2)
                    for g in range(2):
                        k = 0
                        for kt in range(KT):
                            for a, b in PARTS:
                                o = OFF_GU + ((i * 2 + g) * KT + kt) * P
                                m = nc.tensor.matmul(ps[:, bank + g, :], w[a][:, o:o + P], x[b][:, kt, :],
                                                     start=k == 0, stop=k == 5)
                                k += 1
                        m.then_inc(gu_ps, 1)

                def key_value_sum(n):
                    pe.wait_ge(y_add, FROM + n)
                    pe.wait_ge(f_hi, FROM + n * 2 + 2)
                    pe.wait_ge(f_lo, FROM + n * 2 + 2)
                    pe.wait_ge(vh_rdy, FROM + n + 1)
                    pe.wait_ge(vl_rdy, FROM + n + 1)
                    for m2 in range(KT):
                        k = 0
                        for j in range(TC):
                            for a, b in PARTS:
                                m = nc.tensor.matmul(ps[:, 0, m2 * (P + 2):(m2 + 1) * (P + 2)],
                                                     kf[a][:, j, m2 * P:(m2 + 1) * P], v[b][:, j, m2, :],
                                                     start=k == 0, stop=k == 3 * TC - 1)
                                k += 1
                    m.then_inc(kva_ps, 1)

                def down(n, s):
                    if s == 0:
                        pe.wait_ge(kva_add, FROM + n + 1)
                    pe.wait_ge(hs_hi, FROM + n * NI0 + 4 * s + 4)
                    pe.wait_ge(hs_lo, FROM + n * NI0 + 4 * s + 4)
                    for t in range(TC):
                        k = 0
                        for j in range(4):
                            for a, b in PARTS:
                                o = OFF_DN + (s * 4 + j) * D
                                m = nc.tensor.matmul(ps[:, t // 2, (t % 2) * D:(t % 2 + 1) * D],
                                                     hs[a][:, j, t * P:(t + 1) * P], w[b][:, o:o + D],
                                                     start=s == 0 and t % 2 == 0 and k == 0,
                                                     stop=s == SG - 1 and t % 2 == 1 and k == 11, skip_group_check=True)
                                k += 1
                    m.then_inc(y_ps, 1)

                def chunk(n, last):
                    keys_values(n)
                    for i in range(NI0):
                        gate_up(n, i)
                    key_value_sum(n)
                    if not last:
                        turn(n + 1)
                    down(n, 0)
                    if not last:
                        queries(n + 1)
                    down(n, 1)

                turn(0, True)
                queries(0, True)
                with pe.Fori(0, NCH - 1) as n:
                    chunk(n, False)
                chunk(NCH - 1, True)

            @block.scalar
            def _(act):
                def input_hi(n):
                    act.wait_ge(gu_ps, FROM + n * 2 * NI0)
                    for kt in range(KT):
                        act.wait_ge(xT_ps, FROM + n * KT + kt + 1)
                        nc.scalar.activation(xh[:, kt, :], ps[:, 2 + kt, :], ACT.Copy).then_inc(xh_rdy, 1)

                def chunk(n, last):
                    act.wait_ge(qs_rdy, FROM + n * KT + KT)
                    act.wait_ge(win_rdy, FROM + n * SG * 3)
                    nc.scalar.activation(feat(0, rel), qpre, ACT.Relu).then_inc(rel_rdy, 1)
                    act.wait_ge(kvs_rdy, FROM + n * TC + TC)
                    nc.scalar.activation(feat(1, rel).rearrange("p (a b) -> p a b", a=TC), kpre, ACT.Relu).then_inc(rel_rdy, 1)
                    act.wait_ge(kva_ps, FROM + n)
                    nc.scalar.activation(vh[:, :, :, 0:P], kvs[:, :, D:2 * D].rearrange("p a (m e) -> p a m e", m=KT),
                                         ACT.Copy).then_inc(vh_rdy, 1)
                    def tanh(i):
                        act.wait_ge(gu_ps, FROM + n * 2 * NI0 + 2 * i + 1)
                        if i >= 2:
                            act.wait_ge(h_rdy, FROM + n * NI0 + i - 1)
                        else:
                            act.wait_ge(h_rdy, FROM + n * NI0)
                        nc.scalar.activation(th[:, i % 2, :], ps[:, gate_bank(i), :], ACT.Tanh, scale=0.5).then_inc(th_rdy, 1)

                    def exp(s):
                        act.wait_ge(mn_rdy, FROM + n * 2 + s + 1)
                        nc.scalar.activation(feat(s, mn), feat(s, mn), ACT.Exp).then_inc(ex_rdy, 1)

                    def feature_hi(s):
                        act.wait_ge(kva_ps, FROM + n)
                        act.wait_ge(f_rdy, FROM + n * 2 + s + 1)
                        f, hi, lo = feature(s, n)
                        nc.scalar.activation(hi, f, ACT.Copy).then_inc(f_hi, 1)

                    def magnitude(i):
                        if i % 4 == 0:
                            act.wait_ge(win_rdy, FROM + (n * SG + i // 4) * 3)
                            act.wait_ge(f_rdy, FROM + n * 2 + 2)
                        act.wait_ge(h_rdy, FROM + n * NI0 + i + 1)
                        nc.scalar.activation(ab[:, i % 4, :], hh[i // 4][:, i % 4, :], ACT.Abs).then_inc(ab_rdy, 1)

                    def kept_hi(i):
                        if i % 4 == 0:
                            act.wait_ge(y_ps, FROM + n * SG + i // 4)
                        act.wait_ge(hm_rdy, FROM + n * NI0 + i + 1)
                        nc.scalar.activation(hsh[:, i % 4, :], hh[i // 4][:, i % 4, :], ACT.Copy).then_inc(hs_hi, 1)

                    exp(0)
                    tanh(0)
                    exp(1)
                    tanh(1)
                    feature_hi(0)
                    tanh(2)
                    tanh(3)
                    feature_hi(1)
                    for i in range(4):
                        magnitude(i)
                    tanh(4)
                    tanh(5)
                    for i in range(4):
                        kept_hi(i)
                    if not last:
                        input_hi(n + 1)
                    tanh(6)
                    magnitude(4)
                    magnitude(5)
                    tanh(7)
                    magnitude(6)
                    magnitude(7)
                    for i in range(4, 8):
                        kept_hi(i)

                input_hi(0)
                with act.Fori(0, NCH - 1) as n:
                    chunk(n, False)
                chunk(NCH - 1, True)

            @block.gpsimd
            def _(pool):
                with pool.Fori(0, NCH) as n:
                    for s in range(2):
                        pool.wait_ge(ex_rdy, FROM + n * 2 + s + 1)
                        pool.wait_ge(rel_rdy, FROM + n * 2 + s + 1)
                        nc.gpsimd.tensor_tensor(feat(s, mn), feat(s, mn), feat(s, rel), ALU.add).then_inc(f_rdy, 1)
                        f, hi, lo = feature(s, n)
                        pool.wait_ge(f_hi, FROM + n * 2 + s + 1)
                        nc.gpsimd.tensor_tensor(lo, f, hi.bitcast(F32), ALU.subtract).then_inc(f_lo, 1)

            @block.vector
            def _(dve):
                def norm(n):
                    dve.wait_ge(mn_rdy, FROM + n * 2)
                    dve.wait_ge(rel_rdy, FROM + n * 2)
                    for j in range(TC):
                        t = n * TC + j
                        nc.vector.tensor_scalar(xn[:, j, :], acc[:, bass.ds(t, 1), :].rearrange("p a b -> p (a b)"),
                                                mv[:, bass.ds(t, 1), 0:1].rearrange("p a b -> p (a b)"), rstd[:, bass.ds(t, 1)],
                                                ALU.subtract, ALU.mult).then_inc(xn_rdy, 1)

                def input_lo(n):
                    for kt in range(KT):
                        dve.wait_ge(xh_rdy, FROM + n * KT + kt + 1)
                        nc.vector.tensor_tensor(xl[:, kt, :], ps[:, 2 + kt, :], xh[:, kt, :].bitcast(F32), ALU.subtract).then_inc(xl_rdy, 1)

                def chunk(n, last):
                    for m2 in range(KT):
                        dve.wait_ge(q_ps, FROM + n * KT + m2 + 1)
                        nc.vector.tensor_scalar(qs[:, m2, :], ps[:, 4 + m2, :], bqc[:, m2:m2 + 1], None, ALU.add).then_inc(qs_rdy, 1)
                    dve.wait_ge(f_lo, FROM + n * 2)
                    dve.wait_ge(hm_rdy, FROM + n * SG * 4)
                    dve.wait_ge(qs_rdy, FROM + n * KT + KT)
                    nc.vector.tensor_scalar(feat(0, mn), qpre, 0.0, None, ALU.min).then_inc(mn_rdy, 1)
                    dve.wait_ge(vh_rdy, FROM + n)
                    dve.wait_ge(vl_rdy, FROM + n)
                    dve.wait_ge(hs_hi, FROM + n * NI0)
                    dve.wait_ge(hs_lo, FROM + n * NI0)
                    for j in range(TC):
                        dve.wait_ge(kv_ps, FROM + n * TC + j + 1)
                        nc.vector.tensor_tensor(kvs[:, j, :], ps[:, 2 + (4 + j) % 6, :], bkv[:], ALU.add).then_inc(kvs_rdy, 1)
                    dve.wait_ge(kvs_rdy, FROM + n * TC + TC)
                    nc.vector.tensor_scalar(feat(1, mn).rearrange("p (a b) -> p a b", a=TC), kpre, 0.0, None, ALU.min).then_inc(mn_rdy, 1)
                    dve.wait_ge(vh_rdy, FROM + n + 1)
                    nc.vector.tensor_tensor(vl[:, :, :, 0:P], kvs[:, :, D:2 * D].rearrange("p a (m e) -> p a m e", m=KT),
                                            vh[:, :, :, 0:P].bitcast(F32), ALU.subtract).then_inc(vl_rdy, 1)
                    def member(i):
                        u = n * NI0 + i
                        bank = gate_bank(i)
                        dve.wait_ge(th_rdy, FROM + u + 1)
                        nc.vector.scalar_tensor_tensor(th[:, i % 2, :], th[:, i % 2, :], 1.0, ps[:, bank, :],
                                                       ALU.add, ALU.mult).then_inc(s_rdy, 1)
                        dve.wait_ge(s_rdy, FROM + u + 1)
                        dve.wait_ge(gu_ps, FROM + 2 * u + 2)
                        if i == 0:
                            dve.wait_ge(hs_lo, FROM + n * NI0)
                        if i == 4:
                            dve.wait_ge(rel_rdy, FROM + n * 2 + 2)
                            dve.wait_ge(mn_rdy, FROM + n * 2 + 2)
                            dve.wait_ge(vl_rdy, FROM + n + 1)
                        nc.vector.scalar_tensor_tensor(hh[i // 4][:, i % 4, :], th[:, i % 2, :], 0.5, ps[:, bank + 1, :],
                                                       ALU.mult, ALU.mult).then_inc(h_rdy, 1)

                    def compare(s):
                        g = n * SG + s
                        dve.wait_ge(ab_rdy, FROM + g * 4 + 4)
                        dve.wait_ge(hm_rdy, FROM + g * 4)
                        for a, nb, o in ((0, 3, 0), (1, 2, 3), (2, 1, 5)):
                            nc.vector.tensor_tensor(win[:, o:o + nb, :], ab[:, a:a + 1, :].broadcast_to([P, nb, CH]),
                                                    ab[:, a + 1:4, :], ALU.is_ge).then_inc(win_rdy, 1)

                    def keep(s):
                        g = n * SG + s
                        dve.wait_ge(win_rdy, FROM + g * 3 + 3)
                        dve.wait_ge(f_lo, FROM + n * 2 + 2)
                        plan = ((0, 1, ALU.add, 2, ALU.add, 2.0, ALU.is_ge), (3, 4, ALU.add, 0, ALU.subtract, 1.0, ALU.is_ge),
                                (5, 1, ALU.subtract, 3, ALU.subtract, 0.0, ALU.is_ge), (2, 4, ALU.add, 5, ALU.add, 1.0, ALU.is_le))
                        for k, (a, b, op, c, op2, lim, cmp) in enumerate(plan):
                            nc.vector.tensor_tensor(cnt[:, k, :], win[:, a, :], win[:, b, :], op).then_inc(cnt_rdy, 1)
                        for k, (a, b, op, c, op2, lim, cmp) in enumerate(plan):
                            dve.wait_ge(cnt_rdy, FROM + g * 8 + k + 1)
                            nc.vector.tensor_tensor(cnt[:, k, :], cnt[:, k, :], win[:, c, :], op2).then_inc(cnt_rdy, 1)

                        def kept_lo(k):
                            dve.wait_ge(hs_hi, FROM + g * 4 + k + 1)
                            nc.vector.tensor_tensor(hsl[:, k, :], hh[s][:, k, :], hsh[:, k, :].bitcast(F32), ALU.subtract).then_inc(hs_lo, 1)

                        for k, (a, b, op, c, op2, lim, cmp) in enumerate(plan):
                            dve.wait_ge(cnt_rdy, FROM + g * 8 + k + 5)
                            nc.vector.scalar_tensor_tensor(hh[s][:, k, :], cnt[:, k, :], lim, hh[s][:, k, :], cmp, ALU.mult).then_inc(hm_rdy, 1)
                            if k:
                                kept_lo(k - 1)
                        kept_lo(3)

                    for i in range(4):
                        member(i)
                    compare(0)
                    member(4)
                    member(5)
                    if not last:
                        norm(n + 1)
                    keep(0)
                    dve.wait_ge(kva_ps, FROM + n + 1)
                    kv = kvacc[:].rearrange("p a b -> p (a b)")
                    nc.vector.tensor_tensor(kv, kv, ps[:, 0, 0:KT * (P + 2)], ALU.add).then_inc(kva_add, 1)
                    member(6)
                    member(7)
                    if not last:
                        input_lo(n + 1)
                    compare(1)
                    keep(1)
                    dve.wait_ge(y_ps, FROM + n * SG + SG)
                    a = acc[:, bass.ds(n * TC, TC), :].rearrange("p a b -> p (a b)")
                    nc.vector.tensor_tensor(a, a, ps[:, 0:2, :].rearrange("p a b -> p (a b)"), ALU.add).then_inc(y_add, 1)

                norm(0)
                input_lo(0)
                with dve.Fori(0, NCH - 1) as n:
                    chunk(n, False)
                chunk(NCH - 1, True)


def layer0_out(nc, d, acc, xTh, xTl, ident, lg, cb, ps, mv, rstd, wh, wl, bo, bd, kvacc, sems, sbuf):
    NHD = P // 16
    W = P + NHD
    with ExitStack() as st:
        kz = sbuf(st, "kz", [P, KT, W], F32)
        kzh = sbuf(st, "kzh", [P, KT, W], FR)
        kzl = sbuf(st, "kzl", [P, KT, W], FR)
        den = sbuf(st, "den", [P, TC, KT, NHD], F32)
        at = sbuf(st, "at", [P, TC, D], F32)
        ath = sbuf(st, "ath", [P, KT, CH], FR)
        atl = sbuf(st, "atl", [P, KT, CH], FR)
        xn = sbuf(st, "xn1", [P, TC, D], F32)
        bst = sbuf(st, "bst1", [P, NT, 6], F32)
        wg = sbuf(st, "wg", [P, KT, E], F32)
        wgh = sbuf(st, "wgh", [P, KT, E], FR)
        wgl = sbuf(st, "wgl", [P, KT, E], FR)
        bo1 = sbuf(st, "bo1", [P, D], F32)
        kzs, qf, ats, w, wgs, x = (kzh, kzl), (xTh, xTl), (ath, atl), (wh, wl), (wgh, wgl), (xTh, xTl)
        (wg_in, wg_hi, wg_lo, kz_rdy, kz_hi, kz_lo, nd_ps, den_rdy, rec_rdy, at_rdy, aT_ps, at_hi, at_lo, o_ps, ob_add, o_add,
         bs_rdy, ag_rdy, sd, xn_rdy, xT_ps, x_hi, x_lo, lg_ps, lg_rdy, b1_add) = [sems["b_" + s] for s in SEMS["b"]]

        with nc.Block() as block:
            @block.sync
            def _(sp):
                sp.dma_start(wg[:], d["wg"]).then_inc(wg_in, 16)
                sp.dma_start(bo1[:], d["bo1"].partition_broadcast(P)).then_inc(wg_in, 16)

            @block.tensor
            def _(pe):
                def quotient(n):
                    pe.wait_ge(at_rdy, FROM + n * TC)
                    for j in range(TC):
                        t = n * TC + j
                        for m2 in range(KT):
                            for k, (a, b) in enumerate(PARTS):
                                m = nc.tensor.matmul(ps[:, j, m2 * W:(m2 + 1) * W], qf[a][:, m2, t * P:(t + 1) * P],
                                                     kzs[b][:, m2, :], start=k == 0, stop=k == 2)
                    m.then_inc(nd_ps, 1)

                def att_turn(n):
                    if n >= 2:
                        pe.wait_ge(x_lo, FROM + (n - 1) * KT)
                    for kt in range(KT):
                        if n >= 2 and kt == 1:
                            pe.wait_ge(lg_rdy, FROM + n - 1)
                        for j in range(TC):
                            pe.wait_ge(at_rdy, FROM + n * TC + j + 1)
                            m = nc.tensor.transpose(ps[:, 4 + kt, j * P:(j + 1) * P], at[:, j, kt * P:(kt + 1) * P], ident[:])
                        m.then_inc(aT_ps, 1)

                def project(n):
                    pe.wait_ge(at_hi, FROM + n * KT + KT)
                    pe.wait_ge(at_lo, FROM + n * KT + KT)
                    pe.wait_ge(o_add, FROM + n)
                    for t in range(TC):
                        k = 0
                        for m2 in range(KT):
                            for a, b in PARTS:
                                o = OFF_O + m2 * D
                                m = nc.tensor.matmul(ps[:, 6 + t // 2, (t % 2) * D:(t % 2 + 1) * D],
                                                     ats[a][:, m2, t * P:(t + 1) * P], w[b][:, o:o + D], start=k == 0, stop=k == 5)
                                k += 1
                    m.then_inc(o_ps, 1)

                def norm_turn(n):
                    pe.wait_ge(at_lo, FROM + min(n + 2, NCH) * KT)
                    for kt in range(KT):
                        for j in range(TC):
                            pe.wait_ge(xn_rdy, FROM + n * TC + j + 1)
                            m = nc.tensor.transpose(ps[:, 4 + kt, j * P:(j + 1) * P], xn[:, j, kt * P:(kt + 1) * P], ident[:])
                        m.then_inc(xT_ps, 1)

                def logits(n):
                    pe.wait_ge(x_hi, FROM + n * KT + KT)
                    pe.wait_ge(x_lo, FROM + n * KT + KT)
                    for j in range(TC):
                        t = n * TC + j
                        k = 0
                        for kt in range(KT):
                            for a, b in PARTS:
                                m = nc.tensor.matmul(ps[:, 5, j * E:(j + 1) * E], x[a][:, kt, t * P:(t + 1) * P], wgs[b][:, kt, :],
                                                     start=k == 0, stop=k == 5)
                                k += 1
                    m.then_inc(lg_ps, 1)

                pe.wait_ge(kz_lo, FROM + 1)
                quotient(0)
                pe.wait_ge(wg_lo, FROM + 1)
                for n in range(NCH + 1):
                    if n < NCH:
                        att_turn(n)
                    if n + 1 < NCH:
                        quotient(n + 1)
                    if n:
                        norm_turn(n - 1)
                    if n < NCH:
                        project(n)
                    if n:
                        logits(n - 1)

            @block.scalar
            def _(act):
                act.wait_ge(kz_rdy, FROM + 4)
                nc.scalar.activation(kzh[:], kz[:], ACT.Copy).then_inc(kz_hi, 1)
                act.wait_ge(wg_in, FROM + 32)
                nc.scalar.activation(wgh[:], wg[:], ACT.Copy).then_inc(wg_hi, 1)
                for n in range(NCH + 1):
                    for kt in range(KT if n < NCH else 0):
                        act.wait_ge(aT_ps, FROM + n * KT + kt + 1)
                        act.wait_ge(o_ps, FROM + n)
                        nc.scalar.activation(ath[:, kt, :], ps[:, 4 + kt, :], ACT.Copy).then_inc(at_hi, 1)
                    for kt in range(KT if n else 0):
                        act.wait_ge(xT_ps, FROM + (n - 1) * KT + kt + 1)
                        nc.scalar.activation(xTh[:, kt, (n - 1) * CH:n * CH], ps[:, 4 + kt, :], ACT.Copy).then_inc(x_hi, 1)
                    if n < NCH:
                        act.wait_ge(sd, FROM + 3 * n + 1)
                        r = rstd[:, n * TC:(n + 1) * TC]
                        nc.scalar.activation(r, r, ACT.Sqrt).then_inc(sd, 1)

            @block.gpsimd
            def _(pool):
                nc.gpsimd.memset(cb[:, :, E:E + 1], 1.0)
                for n in range(NCH):
                    a = acc[:, n * TC:(n + 1) * TC, :]
                    nc.gpsimd.tensor_tensor(a, a, bo[:].unsqueeze(1).broadcast_to([P, TC, D]), ALU.add).then_inc(ob_add, 1)
                pool.wait_ge(wg_in, FROM + 32)
                for n in range(NCH):
                    pool.wait_ge(xn_rdy, FROM + n * TC + TC)
                    a = acc[:, n * TC:(n + 1) * TC, :]
                    nc.gpsimd.tensor_tensor(a, a, bo1[:].unsqueeze(1).broadcast_to([P, TC, D]), ALU.add).then_inc(b1_add, 1)

            @block.vector
            def _(dve):
                def divide(n):
                    dve.wait_ge(nd_ps, FROM + n + 1)
                    nd = ps[:, 0:TC, 0:KT * W].rearrange("p t (m w) -> p t m w", m=KT)
                    nc.vector.tensor_scalar(den[:], nd[:, :, :, P:W], 1e-6, None, ALU.add).then_inc(den_rdy, 1)
                    dve.wait_ge(den_rdy, FROM + n + 1)
                    nc.vector.reciprocal(den[:], den[:]).then_inc(rec_rdy, 1)
                    dve.wait_ge(rec_rdy, FROM + n + 1)
                    dve.wait_ge(aT_ps, FROM + n * KT)
                    for j in range(TC):
                        nc.vector.tensor_tensor(at[:, j, :].rearrange("p (m h e) -> p m h e", m=KT, h=NHD),
                                                nd[:, j, :, 0:P].rearrange("p m (h e) -> p m h e", h=NHD),
                                                den[:, j, :, :].unsqueeze(3).broadcast_to([P, KT, NHD, P // NHD]),
                                                ALU.mult).then_inc(at_rdy, 1)

                for m2 in range(KT):
                    nc.vector.tensor_tensor(kz[:, m2, 0:P], kvacc[:, m2, 0:P], bd[:], ALU.mult).then_inc(kz_rdy, 1)
                    nc.vector.tensor_scalar(kz[:, m2, P:W], bd[:, 0:P:P // NHD], kvacc[:, m2, P:P + 1], None, ALU.mult).then_inc(kz_rdy, 1)
                dve.wait_ge(kz_hi, FROM + 1)
                nc.vector.tensor_tensor(kzl[:], kz[:], kzh[:].bitcast(F32), ALU.subtract).then_inc(kz_lo, 1)
                dve.wait_ge(wg_hi, FROM + 1)
                nc.vector.tensor_tensor(wgl[:], wg[:], wgh[:].bitcast(F32), ALU.subtract).then_inc(wg_lo, 1)
                divide(0)
                for n in range(NCH + 1):
                    for kt in range(KT if n < NCH else 0):
                        dve.wait_ge(at_hi, FROM + n * KT + kt + 1)
                        nc.vector.tensor_tensor(atl[:, kt, :], ps[:, 4 + kt, :], ath[:, kt, :].bitcast(F32), ALU.subtract).then_inc(at_lo, 1)
                    if n + 1 < NCH:
                        divide(n + 1)
                    for kt in range(KT if n else 0):
                        c = slice((n - 1) * CH, n * CH)
                        dve.wait_ge(x_hi, FROM + (n - 1) * KT + kt + 1)
                        nc.vector.tensor_tensor(xTl[:, kt, c], ps[:, 4 + kt, :], xTh[:, kt, c].bitcast(F32), ALU.subtract).then_inc(x_lo, 1)
                    s = slice(n * TC, (n + 1) * TC)
                    if n < NCH:
                        dve.wait_ge(o_ps, FROM + n + 1)
                        dve.wait_ge(ob_add, FROM + n + 1)
                        a = acc[:, s, :].rearrange("p a b -> p (a b)")
                        nc.vector.tensor_tensor(a, a, ps[:, 6:8, :].rearrange("p a b -> p (a b)"), ALU.add).then_inc(o_add, 1)
                        dve.wait_ge(o_add, FROM + n + 1)
                        for t in range(n * TC, (n + 1) * TC):
                            nc.vector.bn_stats(bst[:, t, :], acc[:, t, :]).then_inc(bs_rdy, 1)
                    if n:
                        dve.wait_ge(lg_ps, FROM + n)
                        nc.vector.tensor_copy(lg[:, (n - 1) * TC:n * TC, :], ps[:, 5, 0:TC * E].rearrange("p (t e) -> p t e", t=TC)).then_inc(lg_rdy, 1)
                    if n < NCH:
                        dve.wait_ge(bs_rdy, FROM + (n + 1) * TC)
                        for t in range(n * TC, (n + 1) * TC):
                            nc.vector.bn_aggr(mv[:, t, :], bst[:, t, :]).then_inc(ag_rdy, 1)
                        dve.wait_ge(ag_rdy, FROM + (n + 1) * TC)
                        nc.vector.tensor_scalar(rstd[:, s], mv[:, s, 1], 1e-5, None, ALU.add).then_inc(sd, 1)
                        dve.wait_ge(sd, FROM + 3 * n + 2)
                        nc.vector.reciprocal(rstd[:, s], rstd[:, s]).then_inc(sd, 1)
                        dve.wait_ge(sd, FROM + 3 * n + 3)
                        dve.wait_ge(xT_ps, FROM + n * KT)
                        for j in range(TC):
                            t = n * TC + j
                            nc.vector.tensor_scalar(xn[:, j, :], acc[:, t, :], mv[:, t, 0:1], rstd[:, t:t + 1],
                                                    ALU.subtract, ALU.mult).then_inc(xn_rdy, 1)


def attention(nc, d, acc, xTh, xTl, ident, lg, cb, ps, sem, sems, sbuf):
    NP = (T * NH) // (NH * P)
    TILE = [NP - 1 - p for p in range(NP)]
    CK = [-(-(t + 1) // TC) for t in TILE]
    PR = [-(-c // 2) for c in CK]
    cumc = [sum(CK[:i]) for i in range(NP + 1)]
    cump = [sum(PR[:i]) for i in range(NP + 1)]
    NC, NPR = cumc[NP], cump[NP]
    TWO = sum(p == 2 for p in PR)
    NPA = NP // 2
    cumv = [sum(CK[0:2 * m:2]) for m in range(NPA + 1)]
    NPV = cumv[NPA]
    UNITS = [("k", 3, 3), ("v", 7, 3), ("v", 6, 3), ("q", 0, 3), ("q", 1, 3), ("k", 2, 2), ("q", 2, 3), ("v", 5, 2),
             ("q", 3, 3), ("v", 4, 2), ("q", 4, 2), ("q", 5, 3), ("k", 1, 2), ("q", 6, 3), ("v", 3, 1), ("q", 7, 3),
             ("v", 2, 2), ("k", 0, 1), ("v", 1, 6), ("v", 0, 7)]
    UN = len(UNITS)
    OWN = 2
    MID = {3: 0, 4: 1, 5: 2, 6: 3, 7: 4, 8: 6, 9: 8, 10: 10, 11: 12, 12: 14, 13: 16, 14: 17}
    END = {7: 5, 8: 7, 9: 9, 10: 11, 11: 13, 12: 15}
    QAT = {1: 1, 3: 2, 4: 3}
    QNEXT = 13
    QN = [sum(u[0] == "q" for u in UNITS[:k]) for k in range(UN + 1)]
    KN = [sum(u[0] != "q" for u in UNITS[:k]) for k in range(UN + 1)]
    FIRST_Q = [u[0] for u in UNITS].index("q")
    KV, VN, NQ = KN[UN], NT // 2, QC // 2
    WK = KT * HD
    with ExitStack() as st:
        wqh = sbuf(st, "wqh", [P, KT, QC * HD], FR)
        wql = sbuf(st, "wql", [P, KT, QC * HD], FR)
        wkh = sbuf(st, "wkh", [P, WK], FR)
        wkl = sbuf(st, "wkl", [P, WK], FR)
        wv = sbuf(st, "wv", [P, KT, 2, HD], FR)
        woh = sbuf(st, "woh", [P, D], FR)
        wol = sbuf(st, "wol", [P, D], FR)
        kst = sbuf(st, "kst", [P, 2 * WK + HD], F32)
        ost = sbuf(st, "ost", [P, D], F32)
        xq = sbuf(st, "xq", [P, KT, 2, P], FR)
        kTh = sbuf(st, "kTh", [P, T], FR)
        kTl = sbuf(st, "kTl", [P, T], FR)
        v2 = sbuf(st, "v2", [P, NT, 2, HD], FR)
        qs = sbuf(st, "qs", [P, T], F32)
        qTh = sbuf(st, "qTh", [P, T], FR)
        qTl = sbuf(st, "qTl", [P, T], FR)
        pr = sbuf(st, "pr", [P, 2, T], F32)
        pth = sbuf(st, "pth", [P, NT, 2, P], FR)
        ptl = sbuf(st, "ptl", [P, NT, 2, P], FR)
        oTh = sbuf(st, "oTh", [P, 2 * P], FR)
        oTl = sbuf(st, "oTl", [P, 2 * P], FR)
        vs = sbuf(st, "vs", [P, 2, 2 * HD], F32)
        bvb = sbuf(st, "bvb", [P, HD], F32)
        bq = sbuf(st, "bq", [P, QC], F32)
        bk = sbuf(st, "bk", [P, NH], F32)
        bh = sbuf(st, "bh", [P, 1], F32)
        cz = sbuf(st, "cz", [P, P], F32)
        czb = sbuf(st, "czb", [P, P], BF16)
        idb = sbuf(st, "idb", [P, P], BF16)
        mx = sbuf(st, "mx", [P, 2, 2], F32)
        nb = sbuf(st, "nb", [P, 2], F32)
        rs = sbuf(st, "rs", [P, 2, 2], F32)
        ri = sbuf(st, "ri", [P, 8], F32)
        wq, wk, wo, x = (wqh, wql), (wkh, wkl), (woh, wol), (xTh, xTl)
        kT, qT, oT, pt = (kTh, kTl), (qTh, qTl), (oTh, oTl), (pth, ptl)
        (wq_in, wq_hi, wq_lo, k_in, o_in, wk_hi, wk_lo, wv_hi, wv_lo, wo_hi, wo_lo, xq_rdy,
         pj_ps, q_a, q_rdy, q_hi, q_lo, k_hi, pj_rd, v_a, v_hi, v_lo,
         s_ps, mx_s, nb_rdy, ex_rdy, rsum, rs_rdy, T_ps, pt_hi, pt_lo, pv_ps, o_hi, o_lo, y_ps, y_add, b_in,
         b_bf, bk_rdy, bv_rdy) = [sems["t_" + s] for s in SEMS["t"]]

        def scores(p, c):
            return min(CH, (TILE[p] + 1) * P - c * CH)

        def pair(p, q):
            return min(2 * CH, (TILE[p] + 1) * P - q * 2 * CH)

        def group(p, c):
            return min(TC, TILE[p] + 1 - c * TC)

        def chunks(p):
            return list(range(CK[p] - 1, -1, -1))

        def pexp(p, c):
            return (cump[p] if p >= 0 else cump[NP + p] - NPR) + PR[p] - c // 2

        G = 4
        free = pr[:].rearrange("p a b -> p (a b)")
        ex, sc, mk, rk = [free[:, k * NT * E:(k + 1) * NT * E].rearrange("p (t e) -> p t e", t=NT) for k in range(4)]
        tie = free[:, 1024:1280].rearrange("p (a b) -> p a b", a=E)
        m1 = free[:, 1280:1280 + NT]
        gm, keep = [free[:, 1344 + 64 * k:1408 + 64 * k].rearrange("p (t g) -> p t g", t=NT) for k in range(2)]
        c0, c1 = [free[:, 1536 + 256 * k:1792 + 256 * k].rearrange("p (t a b) -> p t a b", t=NT, a=G) for k in range(2)]
        e0, e1 = [free[:, 2048 + 1024 * k:3072 + 1024 * k].rearrange("p (t a b) -> p t a b", t=TC, a=E) for k in range(2)]
        (tie_in, r_mx, r_ex, r_v, r_c) = [sems["r_" + s] for s in SEMS["r"]]

        def ready(i):
            m, ks = ((i - 1) // 2, (0, 1)) if i % 2 else (i // 2 - 1, (2, 3))
            return m, [k for k in ks if m >= 0 and k < CK[2 * m]]

        def pair_at(i, lag, first):
            m = (i - lag) // 2
            return m if (i - lag) % 2 == 0 and not (m < 0 and first) else None

        def reader(p, c):
            for m in range(p // 2 - 1, -1, -1):
                if CK[2 * m] > c:
                    return cumv[m] + CK[2 * m] - c
            return 0

        def bank_of(k, g, early=False):
            return k % 4 if early else UNITS[k][2]

        def need(c):
            return max(KN[e] + 1 for e, (kind, r, bank) in enumerate(UNITS) if kind != "q" and (bank == c or (kind, r) == ("k", c)))

        with nc.Block() as block:
            @block.sync
            def _(sp):
                sp.dma_start(kst[:], d["wkv1"][:, 0, :]).then_inc(k_in, 16)
                sp.dma_start(bk[:], d["bk1"]).then_inc(b_in, 16)
                sp.dma_start(bq[:], d["bq1"]).then_inc(b_in, 16)
                sp.dma_start(cz[:], d["causal"]).then_inc(b_in, 16)
                for k in range(KT):
                    sp.dma_start(pr[:, k, :], d["wq"][:, k * T:(k + 1) * T]).then_inc(wq_in, 16)
                sp.dma_start(ost[:], d["wo1"][:, 0, :]).then_inc(o_in, 16)
                sp.wait_ge(wq_lo, FROM + KT)
                sp.dma_start(tie.rearrange("p a b -> p (a b)"), d["tie"].partition_broadcast(P)).then_inc(tie_in, 16)
                with sp.Fori(1, NH) as h:
                    sp.wait_ge(wk_hi, FROM + h)
                    sp.wait_ge(wv_hi, FROM + h)
                    sp.wait_ge(wk_lo, FROM + h)
                    sp.wait_ge(wv_lo, FROM + h)
                    sp.wait_ge(bv_rdy, FROM + h)
                    sp.dma_start(kst[:], d["wkv1"][:, bass.ds(h, 1), :].rearrange("p a b -> p (a b)")).then_inc(k_in, 16)
                    sp.wait_ge(wo_hi, FROM + h)
                    sp.wait_ge(wo_lo, FROM + h)
                    sp.dma_start(ost[:], d["wo1"][:, bass.ds(h, 1), :].rearrange("p a b -> p (a b)")).then_inc(o_in, 16)

            @block.tensor
            def _(pe):
                def unit(k, g, early=False):
                    kind, r, _ = UNITS[k]
                    bank = bank_of(k, g, early)
                    if k == 0:
                        pe.wait_ge(wk_hi, FROM + g + 1)
                        pe.wait_ge(wv_hi, FROM + g + 1)
                        pe.wait_ge(wk_lo, FROM + g + 1)
                        pe.wait_ge(wv_lo, FROM + g + 1)
                    if kind == "q" and r == 0:
                        pe.wait_ge(xq_rdy, FROM + 2 * g + 2)
                    for e in range(k - 1, -1, -1):
                        if bank_of(e, g, early) == bank:
                            if UNITS[e][0] == "q":
                                pe.wait_ge(q_rdy, FROM + NQ * g + QN[e] + 1)
                            else:
                                pe.wait_ge(pj_rd, FROM + KV * g + KN[e] + 1)
                            break
                    if kind == "k":
                        n = 0
                        for kt in range(KT):
                            for a, b in PARTS:
                                m = nc.tensor.matmul(ps[:, bank, :], wk[a][:, kt * HD:(kt + 1) * HD], x[b][:, kt, r * CH:(r + 1) * CH],
                                                     start=n == 0, stop=n == 5)
                                n += 1
                    else:
                        for j in range(2):
                            c = 2 * r + j
                            for kt in range(KT):
                                if kind == "q":
                                    hi, lo = [wq[a][:, kt, c * HD:(c + 1) * HD] for a in range(2)]
                                    both, one = xq[:, kt, :, :].rearrange("p a b -> p (a b)"), xq[:, kt, 0, :]
                                else:
                                    hi, lo = [x[a][:, kt, c * P:(c + 1) * P] for a in range(2)]
                                    both, one = wv[:, kt, :, :].rearrange("p a b -> p (a b)"), wv[:, kt, 0, :]
                                o = 2 * P * j
                                nc.tensor.matmul(ps[:, bank, o:o + 2 * P], hi, both, start=kt == 0, stop=False, skip_group_check=True)
                                m = nc.tensor.matmul(ps[:, bank, o:o + P], lo, one, start=False, stop=kt == KT - 1, skip_group_check=True)
                    m.then_inc(pj_ps, 1)

                def qk(p, c):
                    w = scores(p, c)
                    i = TILE[p]
                    last = c == CK[p] - 1
                    for k, (a, b) in enumerate(PARTS):
                        m = nc.tensor.matmul(ps[:, c, 0:w], qT[a][:, i * P:(i + 1) * P], kT[b][:, c * CH:c * CH + w],
                                             start=k == 0, stop=k == 2 and not last)
                    if last:
                        m = nc.tensor.matmul(ps[:, c, w - P:w], idb[:], czb[:], start=False, stop=True)
                    if c % 2 == 0:
                        m.then_inc(s_ps, 1)

                def turn(p, k, h):
                    c = chunks(p)[k]
                    n = cumc[p] + k
                    pe.wait_ge(pt_lo, FROM + h * NC + n - 1)
                    pe.wait_ge(ex_rdy, FROM + h * NPR + pexp(p, c))
                    for j in range(group(p, c)):
                        t = c * TC + j
                        m = nc.tensor.transpose(ps[:, 4 + n % 2, j * P:(j + 1) * P], pr[:, p % 2, t * P:(t + 1) * P], ident[:])
                    m.then_inc(T_ps, 1)

                def pv(m, k, h):
                    A = 2 * (m % NPA)
                    c = chunks(A)[k]
                    if k == 0:
                        pe.wait_ge(o_lo, FROM + h * NPA + m)
                        if m == 0:
                            pe.wait_ge(pj_rd, FROM + KV * h + KV)
                    if m == 0:
                        pe.wait_ge(v_lo, FROM + VN * h + VN - 2 * c)
                    pe.wait_ge(pt_lo, FROM + h * NC + (cumc[A + 1] if m >= 0 else cumc[A + 1] - NC) + k + 1)
                    for j in range(group(A, c)):
                        t = c * TC + j
                        n = 2 * P if t <= TILE[A + 1] else P
                        for e, (s, w) in enumerate(PARTS):
                            q = nc.tensor.matmul(ps[:, 6, 0:n], v2[:, t, s, :], pt[w][:, t, :, :].rearrange("p a b -> p (a b)")[:, 0:n],
                                                 start=k == 0 and j == 0 and e == 0,
                                                 stop=c == 0 and j == group(A, c) - 1 and e == 2, skip_group_check=True)
                    q.then_inc(pv_ps, 1)

                def project(m, h):
                    if m == 0:
                        pe.wait_ge(wo_hi, FROM + h + 1)
                        pe.wait_ge(wo_lo, FROM + h + 1)
                    pe.wait_ge(o_lo, FROM + h * NPA + m + 1)
                    pe.wait_ge(y_add, FROM + h * NP + 2 * m)
                    if m == -1:
                        pe.wait_ge(pj_rd, FROM + KV * h + KV)
                    for e in range(2):
                        for k, (s, w) in enumerate(PARTS):
                            q = nc.tensor.matmul(ps[:, 7, e * D:(e + 1) * D], oT[s][:, e * P:(e + 1) * P], wo[w][:], start=k == 0, stop=k == 2)
                    q.then_inc(y_ps, 1)

                def chunk_scores(b, c, h):
                    if b == 0:
                        if c == CK[0] - 1:
                            pe.wait_ge(q_hi, FROM + 4 * h + 1)
                            pe.wait_ge(q_lo, FROM + 4 * h + 1)
                        pe.wait_ge(pj_rd, FROM + KV * h + need(c))
                        pe.wait_ge(ex_rdy, FROM + h * NPR)
                    else:
                        if b % TC == 0 and c == CK[b] - 1:
                            pe.wait_ge(q_hi, FROM + 4 * h + b // TC + 1)
                            pe.wait_ge(q_lo, FROM + 4 * h + b // TC + 1)
                        pe.wait_ge(ex_rdy, FROM + h * NPR + pexp(b - 1, c))
                    qk(b, c)

                def step(i, h, first, last):
                    b, g = (i + 1, h) if i + 1 < NP else (0, h + 1)
                    todo = chunks(b) if b or not last else []
                    m, pvs = ready(i)
                    if i % 2 == 0 and i:
                        for c in todo:
                            chunk_scores(b, c, g)
                        for k in range(min(2, CK[i])):
                            turn(i, k, h)
                            if k < len(pvs):
                                pv(m, pvs[k], h)
                        pvs = []
                    else:
                        for c in todo[0:2]:
                            chunk_scores(b, c, g)
                        for k in range(2):
                            if k < CK[i]:
                                turn(i, k, h)
                            for c in todo[2 + k:3 + k]:
                                chunk_scores(b, c, g)
                    f = pair_at(i, 3, first)
                    if f is not None:
                        project(f, h)
                    if i == 0:
                        pe.wait_ge(o_lo, FROM + h * NPA)
                        if not first:
                            pe.wait_ge(y_add, FROM + h * NP - 2)
                        for k in range(UN - OWN, UN):
                            unit(k, h)
                    if i in MID and not last:
                        unit(MID[i], h + 1)
                    for k in range(2, 4):
                        if k < CK[i]:
                            turn(i, k, h)
                        if k - 2 < len(pvs):
                            pv(m, pvs[k - 2], h)
                    if i in END and not last:
                        unit(END[i], h + 1)

                def head(h, first, last):
                    for i in range(NP):
                        step(i, h, first, last)

                for k in range(UN - OWN):
                    if k == FIRST_Q:
                        pe.wait_ge(wq_lo, FROM + KT)
                    unit(k, 0, True)
                pe.wait_ge(b_bf, FROM + 2)
                pe.wait_ge(pj_rd, FROM + KV - OWN)
                for c in chunks(0):
                    chunk_scores(0, c, 0)
                head(0, True, False)
                with pe.Fori(1, NH - 1) as h:
                    head(h, False, False)
                head(NH - 1, False, True)
                project(NPA - 1, NH - 1)

            @block.scalar
            def _(act):
                def unit_hi(k, g, early=False):
                    kind, r, _ = UNITS[k]
                    bank = bank_of(k, g, early)
                    if kind == "q":
                        act.wait_ge(pj_ps, FROM + g * UN + k + 1)
                        act.wait_ge(q_lo, FROM + 4 * g)
                        for c in (2 * r, 2 * r + 1):
                            nc.scalar.activation(qs[:].rearrange("p (t c) -> p c t", c=QC)[:, c, :], ps[:, bank, (c % 2) * 2 * P:(c % 2) * 2 * P + P],
                                                 ACT.Identity, bias=bq[:, c:c + 1]).then_inc(q_a, 1)
                    if kind == "k":
                        act.wait_ge(pj_ps, FROM + g * UN + k + 1)
                        nc.scalar.activation(kTh[:, r * CH:(r + 1) * CH], ps[:, bank, :], ACT.Identity, bias=bh[:, 0:1]).then_inc(k_hi, 1)
                    if kind == "v":
                        act.wait_ge(pj_rd, FROM + KV * g + KN[k] + 1)
                        nc.scalar.activation(v2[:, 2 * r:2 * r + 2, 0, :], vs[:, r % 2, :].rearrange("p (t e) -> p t e", t=2),
                                             ACT.Copy).then_inc(v_hi, 1)

                def q_split(g, n):
                    act.wait_ge(q_rdy, FROM + NQ * g + NQ)
                    c = slice((3 - n) * CH, (4 - n) * CH)
                    nc.scalar.activation(qTh[:, c], qs[:, c], ACT.Copy).then_inc(q_hi, 1)

                def wk_split(g):
                    act.wait_ge(k_in, FROM + 16 * g + 16)
                    nc.scalar.activation(wkh[:], kst[:, 0:WK], ACT.Copy).then_inc(wk_hi, 1)
                    nc.scalar.activation(wv[:, :, 0, :], kst[:, WK:2 * WK].rearrange("p (k e) -> p k e", k=KT), ACT.Copy).then_inc(wv_hi, 1)
                    nc.scalar.activation(bh[:, 0:1], bk[:, bass.ds(g, 1)], ACT.Copy).then_inc(bk_rdy, 1)
                    act.wait_ge(bk_rdy, FROM + g + 1)

                def hi(p, k, h):
                    c = chunks(p)[k]
                    n = cumc[p] + k
                    w = group(p, c)
                    act.wait_ge(T_ps, FROM + h * NC + n + 1)
                    if p % 2 == 0:
                        act.wait_ge(pv_ps, FROM + h * NPV + reader(p, c))
                    nc.scalar.activation(pth[:, c * TC:c * TC + w, p % 2, :], ps[:, 4 + n % 2, 0:w * P].rearrange("p (t e) -> p t e", t=w),
                                         ACT.Copy).then_inc(pt_hi, 1)

                def exps(p, q, h, start=False):
                    w = pair(p, q)
                    if q == PR[p] - 1:
                        act.wait_ge(nb_rdy, FROM + h * NP + p + 1)
                        if not start and p != 1:
                            act.wait_ge(T_ps, FROM + h * NC + (cumc[p - 1] if p else -CK[NP - 1]))
                            act.wait_ge(rs_rdy, FROM + h * NP + p - 1)
                        if p == 1:
                            act.wait_ge(T_ps, FROM + h * NC)
                            act.wait_ge(rs_rdy, FROM + h * NP)
                    nc.scalar.activation(pr[:, p % 2, q * 2 * CH:q * 2 * CH + w],
                                         ps[:, 2 * q:2 * q + 2, :].rearrange("p a b -> p (a b)")[:, 0:w], ACT.Exp,
                                         bias=nb[:, p % 2:p % 2 + 1], scale=SCALE,
                                         accum_out=rs[:, p % 2, q:q + 1]).then_inc(ex_rdy, 1)

                def out_hi(m, h):
                    act.wait_ge(pv_ps, FROM + h * NPV + (cumv[m + 1] if m >= 0 else 0))
                    act.wait_ge(y_ps, FROM + h * NPA + m)
                    nc.scalar.activation(oTh[:], ps[:, 6, 0:2 * P], ACT.Copy).then_inc(o_hi, 1)

                def step(i, h, first, last):
                    if i + 1 < NP:
                        b, g = i + 1, h
                    else:
                        b, g = 0, h + 1
                    early = 1 if i % 2 == 0 and i else 2
                    m = pair_at(i, 2, first)
                    if i == 0 and m is not None:
                        out_hi(m, h)
                    for k in range(min(early, CK[i])):
                        hi(i, k, h)
                    if b or not last:
                        exps(b, PR[b] - 1, g)
                    for k in range(early, min(2, CK[i])):
                        hi(i, k, h)
                    if PR[b] == 2 and (b or not last):
                        exps(b, 0, g)
                    if i and m is not None and CK[2 * m] < 3:
                        out_hi(m, h)
                    if i == QNEXT and not last:
                        q_split(h + 1, 0)
                    if i == 0:
                        for k in range(UN - OWN, UN):
                            unit_hi(k, h)
                    if i in MID and not last:
                        unit_hi(MID[i], h + 1)
                    for k in range(2, CK[i]):
                        hi(i, k, h)
                    if m is not None and CK[2 * m] > 2:
                        out_hi(m, h)
                    if i == 2:
                        act.wait_ge(y_ps, FROM + h * NPA)
                        act.wait_ge(o_in, FROM + 16 * h + 16)
                        nc.scalar.activation(woh[:], ost[:], ACT.Copy).then_inc(wo_hi, 1)
                    if i in QAT:
                        q_split(h, QAT[i])
                    if i == 1 and not last:
                        wk_split(h + 1)
                    if i in END and not last:
                        unit_hi(END[i], h + 1)

                act.wait_ge(b_in, FROM + 48)
                wk_split(0)
                nc.scalar.activation(czb[:], cz[:], ACT.Copy).then_inc(b_bf, 1)
                nc.scalar.activation(idb[:], ident[:], ACT.Copy).then_inc(b_bf, 1)
                for k in range(UN - OWN):
                    if k == FIRST_Q:
                        for kt in range(KT):
                            act.wait_ge(wq_in, FROM + 32)
                            nc.scalar.activation(wqh[:, kt, :], pr[:, kt, :], ACT.Copy).then_inc(wq_hi, 1)
                    if k == FIRST_Q + 2:
                        act.wait_ge(r_mx, FROM + 1)
                        nc.scalar.activation(ex, ex, ACT.Exp).then_inc(r_ex, 1)
                    unit_hi(k, 0, True)
                q_split(0, 0)
                exps(0, 1, 0, True)
                exps(0, 0, 0, True)
                for i in range(NP):
                    step(i, 0, True, False)
                with act.Fori(1, NH - 1) as h:
                    for i in range(NP):
                        step(i, h, False, False)
                for i in range(NP):
                    step(i, NH - 1, False, True)
                out_hi(NPA - 1, NH - 1)

            @block.gpsimd
            def _(pool):
                def wk_split(g):
                    pool.wait_ge(wk_hi, FROM + g + 1)
                    pool.wait_ge(wv_hi, FROM + g + 1)
                    pool.wait_ge(pj_rd, FROM + KV * g)
                    nc.gpsimd.tensor_tensor(wkl[:], kst[:, 0:WK], wkh[:].bitcast(F32), ALU.subtract).then_inc(wk_lo, 1)
                    nc.gpsimd.tensor_tensor(wv[:, :, 1, :], kst[:, WK:2 * WK].rearrange("p (k e) -> p k e", k=KT),
                                            wv[:, :, 0, :].bitcast(F32), ALU.subtract).then_inc(wv_lo, 1)
                    nc.gpsimd.tensor_copy(bvb[:], kst[:, 2 * WK:]).then_inc(bv_rdy, 1)
                    for b in range(2):
                        nc.gpsimd.tensor_copy(xq[:, :, b, :], x[b][:, :, bass.ds(g * P, P)].bitcast(F32)).then_inc(xq_rdy, 1)

                def unit_lo(k, g):
                    kind, r, bank = UNITS[k]
                    if kind == "v":
                        pool.wait_ge(v_hi, FROM + VN * g + VN - r)
                        nc.gpsimd.tensor_tensor(v2[:, 2 * r:2 * r + 2, 1, :], vs[:, r % 2, :].rearrange("p (t e) -> p t e", t=2),
                                                v2[:, 2 * r:2 * r + 2, 0, :].bitcast(F32), ALU.subtract).then_inc(v_lo, 1)

                def step(i, h, last):
                    if i == 0:
                        for k in range(UN - OWN, UN):
                            unit_lo(k, h)
                    if i == 2:
                        pool.wait_ge(wo_hi, FROM + h + 1)
                        nc.gpsimd.tensor_tensor(wol[:], ost[:], woh[:].bitcast(F32), ALU.subtract).then_inc(wo_lo, 1)
                    if i == 1 and not last:
                        wk_split(h + 1)
                    for at in (MID, END):
                        if i in at and not last:
                            unit_lo(at[i], h + 1)

                wk_split(0)
                for k in range(UN - OWN):
                    unit_lo(k, 0)
                for i in range(NP):
                    step(i, 0, False)
                with pool.Fori(1, NH - 1) as h:
                    for i in range(NP):
                        step(i, h, False)
                for i in range(NP):
                    step(i, NH - 1, True)

            @block.vector
            def _(dve):
                def unit_lo(k, g, early=False):
                    kind, r, _ = UNITS[k]
                    bank = bank_of(k, g, early)
                    if kind == "q":
                        dve.wait_ge(q_a, FROM + QC * g + 2 * r + 2)
                        q = qs[:].rearrange("p (t c) -> p c t", c=QC)[:, 2 * r:2 * r + 2, :]
                        nc.vector.tensor_tensor(q, q, ps[:, bank, :].rearrange("p (c s t) -> p c s t", c=2, s=2)[:, :, 1, :],
                                                ALU.add).then_inc(q_rdy, 1)
                        return
                    if kind == "k":
                        dve.wait_ge(k_hi, FROM + g * 4 + 4 - r)
                        s = slice(r * CH, (r + 1) * CH)
                        nc.vector.scalar_tensor_tensor(kTl[:, s], ps[:, bank, :], bh[:, 0:1], kTh[:, s].bitcast(F32),
                                                       ALU.add, ALU.subtract).then_inc(pj_rd, 1)
                    else:
                        dve.wait_ge(pj_ps, FROM + g * UN + k + 1)
                        dve.wait_ge(bv_rdy, FROM + g + 1)
                        dve.wait_ge(v_lo, FROM + VN * g + max(VN - r - 2, 0))
                        v = vs[:, r % 2, :].rearrange("p (t e) -> p t e", t=2)
                        o = ps[:, bank, :].rearrange("p (t s e) -> p t s e", t=2, s=2)
                        nc.vector.tensor_tensor(v, o[:, :, 0, :], bvb[:].unsqueeze(1).broadcast_to([P, 2, HD]), ALU.add).then_inc(v_a, 1)
                        dve.wait_ge(v_a, FROM + VN * g + VN - r)
                        nc.vector.tensor_tensor(v, v, o[:, :, 1, :], ALU.add).then_inc(pj_rd, 1)

                def q_split(g, n):
                    c = slice((3 - n) * CH, (4 - n) * CH)
                    dve.wait_ge(q_hi, FROM + 4 * g + n + 1)
                    nc.vector.tensor_tensor(qTl[:, c], qs[:, c], qTh[:, c].bitcast(F32), ALU.subtract).then_inc(q_lo, 1)

                def maximum(p, q, h):
                    dve.wait_ge(s_ps, FROM + h * NPR + cump[p] + PR[p] - q)
                    nc.vector.tensor_reduce(mx[:, p % 2, q:q + 1], ps[:, 2 * q:2 * q + 2, :].rearrange("p a b -> p (a b)")[:, 0:pair(p, q)],
                                            AX.X, ALU.max).then_inc(mx_s, 1)

                def bias(p, h):
                    dve.wait_ge(mx_s, FROM + h * NPR + cump[p + 1])
                    if PR[p] == 2:
                        nc.vector.tensor_scalar(nb[:, p % 2:p % 2 + 1], mx[:, p % 2, 0:1], mx[:, p % 2, 1:2], -SCALE,
                                                ALU.max, ALU.mult).then_inc(nb_rdy, 1)
                    else:
                        nc.vector.tensor_scalar(nb[:, p % 2:p % 2 + 1], mx[:, p % 2, 0:1], -SCALE, None, ALU.mult).then_inc(nb_rdy, 1)

                def lo(p, k, h):
                    c = chunks(p)[k]
                    n = cumc[p] + k
                    w = group(p, c)
                    dve.wait_ge(pt_hi, FROM + h * NC + n + 1)
                    s = slice(c * TC, c * TC + w)
                    nc.vector.tensor_tensor(ptl[:, s, p % 2, :], ps[:, 4 + n % 2, 0:w * P].rearrange("p (t e) -> p t e", t=w),
                                            pth[:, s, p % 2, :].bitcast(F32), ALU.subtract).then_inc(pt_lo, 1)

                def row_sum(q, h):
                    dve.wait_ge(ex_rdy, FROM + h * NPR + cump[q + 1])
                    src = rs[:, q % 2, 0:1]
                    if PR[q] == 2:
                        nc.vector.tensor_tensor(src, src, rs[:, q % 2, 1:2], ALU.add).then_inc(rsum, 1)
                        dve.wait_ge(rsum, FROM + h * TWO + q + 1)
                    nc.vector.reciprocal(ri[:, q % 8:q % 8 + 1], src).then_inc(rs_rdy, 1)

                def out_lo(m, h):
                    dve.wait_ge(o_hi, FROM + h * NPA + m + 1)
                    nc.vector.tensor_tensor(oTl[:], ps[:, 6, 0:2 * P], oTh[:].bitcast(F32), ALU.subtract).then_inc(o_lo, 1)

                def add(f, h):
                    q = f % NP
                    t = TILE[q]
                    dve.wait_ge(y_ps, FROM + h * NPA + f // 2 + 1)
                    dve.wait_ge(rs_rdy, FROM + h * NP + f + 1)
                    dve.wait_ge(y_add, FROM + h * NP + max(f - 1, 0) if f >= 0 else FROM + h * NP + f - 1)
                    nc.vector.scalar_tensor_tensor(acc[:, t, :], ps[:, 7, (f % 2) * D:(f % 2 + 1) * D], ri[:, q % 8:q % 8 + 1],
                                                   acc[:, t, :], ALU.mult, ALU.add).then_inc(y_add, 1)

                def step(i, h, first, last):
                    b, g = (i + 1, h) if i + 1 < NP else (0, h + 1)
                    los = list(range(CK[i]))
                    o, m = pair_at(i, 2, first), pair_at(i, 4, first)
                    if i == 0 and not first:
                        out_lo(o, h)
                        add(2 * m, h)
                        add(2 * m + 1, h)
                    if b or not last:
                        maximum(b, PR[b] - 1, g)
                        if PR[b] == 2:
                            if i % 2 or i == 0:
                                lo(i, los.pop(0), h)
                            maximum(b, 0, g)
                        bias(b, g)
                    while los and los[0] < 2:
                        lo(i, los.pop(0), h)
                    if i and o is not None and CK[2 * o] < 3:
                        out_lo(o, h)
                    if i and m is not None:
                        add(2 * m, h)
                        add(2 * m + 1, h)
                    row_sum(i, h)
                    if i == QNEXT and not last:
                        q_split(h + 1, 0)
                    if i == 0:
                        for k in range(UN - OWN, UN):
                            unit_lo(k, h)
                    if i in MID and not last:
                        unit_lo(MID[i], h + 1)
                    for k in los:
                        lo(i, k, h)
                    if o is not None and CK[2 * o] > 2:
                        out_lo(o, h)
                    if i in QAT:
                        q_split(h, QAT[i])
                    if i in END and not last:
                        unit_lo(END[i], h + 1)

                def head(h, first, last):
                    for i in range(NP):
                        step(i, h, first, last)

                def step_of(k, ins):
                    ins.then_inc(r_v, 1)
                    dve.wait_ge(r_v, FROM + k)

                def route_groups():
                    nc.vector.tensor_reduce(m1, lg[:], AX.X, ALU.max).then_inc(r_v, 1)
                    dve.wait_ge(r_v, FROM + 1)
                    nc.vector.tensor_tensor(ex, lg[:], m1.unsqueeze(2).broadcast_to([P, NT, E]), ALU.subtract).then_inc(r_mx, 1)
                    dve.wait_ge(r_ex, FROM + 1)
                    step_of(2, nc.vector.tensor_reduce(m1, ex, AX.X, ALU.add))
                    step_of(3, nc.vector.reciprocal(m1, m1))
                    step_of(4, nc.vector.tensor_tensor(sc, ex, m1.unsqueeze(2).broadcast_to([P, NT, E]), ALU.mult))
                    step_of(5, nc.vector.tensor_reduce(gm, sc.rearrange("p t (g e) -> p t g e", g=G), AX.X, ALU.max))
                    row = gm.unsqueeze(3).broadcast_to([P, NT, G, G])
                    col = gm.unsqueeze(2).broadcast_to([P, NT, G, G])
                    dve.wait_ge(tie_in, FROM + 16)
                    nc.vector.tensor_tensor(c0, col, row, ALU.is_gt).then_inc(r_c, 1)
                    step_of(6, nc.vector.tensor_tensor(c1, col, row, ALU.is_equal))
                    step_of(7, nc.vector.tensor_tensor(c1, c1, tie[:, 0:G, 0:G].unsqueeze(1).broadcast_to([P, NT, G, G]), ALU.mult))
                    dve.wait_ge(r_c, FROM + 1)
                    step_of(8, nc.vector.tensor_tensor(c0, c0, c1, ALU.add))
                    step_of(9, nc.vector.tensor_reduce(keep, c0, AX.X, ALU.add))
                    step_of(10, nc.vector.tensor_scalar(keep, keep, 2.0, None, ALU.is_lt))
                    kb = keep.unsqueeze(3).broadcast_to([P, NT, G, E // G])
                    step_of(11, nc.vector.tensor_tensor(mk.rearrange("p t (g e) -> p t g e", g=G),
                                                        sc.rearrange("p t (g e) -> p t g e", g=G), kb, ALU.mult))
                    step_of(12, nc.vector.scalar_tensor_tensor(
                        mk.rearrange("p t (g e) -> p (t g) e", g=G), kb.rearrange("p t g e -> p (t g) e"), -1.0,
                        mk.rearrange("p t (g e) -> p (t g) e", g=G), ALU.add, ALU.add))

                def route_experts(n):
                    s = slice(n * TC, (n + 1) * TC)
                    row = mk[:, s, :].unsqueeze(3).broadcast_to([P, TC, E, E])
                    col = mk[:, s, :].unsqueeze(2).broadcast_to([P, TC, E, E])
                    k = 13 + 4 * n
                    nc.vector.tensor_tensor(e0, col, row, ALU.is_gt).then_inc(r_c, 1)
                    step_of(k, nc.vector.tensor_tensor(e1, col, row, ALU.is_equal))
                    step_of(k + 1, nc.vector.tensor_tensor(e1, e1, tie.unsqueeze(1).broadcast_to([P, TC, E, E]), ALU.mult))
                    dve.wait_ge(r_c, FROM + n + 2)
                    step_of(k + 2, nc.vector.tensor_tensor(e0, e0, e1, ALU.add))
                    step_of(k + 3, nc.vector.tensor_reduce(rk[:, s, :], e0, AX.X, ALU.add))
                    nc.vector.scalar_tensor_tensor(cb[:, s, 0:E], rk[:, s, :], 4.0, sc[:, s, :], ALU.is_lt, ALU.mult)

                dve.wait_ge(b_in, FROM + 48)
                for k in range(UN - OWN):
                    if k == FIRST_Q:
                        for kt in range(KT):
                            dve.wait_ge(wq_hi, FROM + kt + 1)
                            nc.vector.tensor_tensor(wql[:, kt, :], pr[:, kt, :], wqh[:, kt, :].bitcast(F32), ALU.subtract).then_inc(wq_lo, 1)
                    if k == FIRST_Q + 2:
                        dve.wait_ge(wq_lo, FROM + KT)
                        route_groups()
                    if k > FIRST_Q + 3 and (k - FIRST_Q) % 3 == 2:
                        route_experts((k - FIRST_Q) // 3 - 1)
                    unit_lo(k, 0, True)
                q_split(0, 0)
                maximum(0, 1, 0)
                maximum(0, 0, 0)
                bias(0, 0)
                head(0, True, False)
                with dve.Fori(1, NH - 1) as h:
                    head(h, False, False)
                head(NH - 1, False, True)
                h = NH - 1
                add(NP - 4, h)
                add(NP - 3, h)
                out_lo(NPA - 1, h)
                add(NP - 2, h)
                add(NP - 1, h)


def experts(nc, d, acc, xTh, xTl, ident, cb, ps, sem, sems, sbuf):
    RING = 3
    U = NCH * GT
    W1, W3, W2, SEL = 0, KT * P, 2 * KT * P, GW
    TWC = GW + P
    LAG = 2
    with ExitStack() as st:
        wst = sbuf(st, "est", [P, GT, TWC], F32)
        wh = sbuf(st, "ewh", [P, GT, TWC], FR)
        wl = sbuf(st, "ewl", [P, GT, TWC], FR)
        cT32 = sbuf(st, "cT32", [P, TC, P], F32)
        cTh = sbuf(st, "cTh", [P, T], FR)
        cTl = sbuf(st, "cTl", [P, T], FR)
        th = sbuf(st, "eth", [P, 2, CH], F32)
        h32 = sbuf(st, "eh32", [P, 3, CH], F32)
        hh = sbuf(st, "ehh", [P, RING, CH], FR)
        hl = sbuf(st, "ehl", [P, RING, CH], FR)
        w, x, c, hp = (wh, wl), (xTh, xTl), (cTh, cTl), (hh, hl)
        (cp, cT_ps, ct_hi, ct_lo, w_in, w_hi, w_lo, g_ps, u_ps, c_ps, th_rdy, s_rdy, h_rdy, hc_rdy, h_hi, h_lo, y_ps, y_add) = [
            sems["e_" + s] for s in SEMS["e"]]

        with nc.Block() as block:
            @block.sync
            def _(sp):
                sp.dma_start(wst[:], d["wexp"][:, 0:GT, :]).then_inc(w_in, 16)
                with sp.Fori(1, NG) as g:
                    sp.wait_ge(w_hi, FROM + g * GT)
                    sp.wait_ge(w_lo, FROM + g * GT)
                    sp.dma_start(wst[:], d["wexp"][:, bass.ds(g * GT, GT), :]).then_inc(w_in, 16)

            @block.tensor
            def _(pe):
                for n in range(NCH):
                    pe.wait_ge(cp, FROM + n + 2)
                    if n:
                        pe.wait_ge(ct_lo, FROM + n)
                    for j in range(TC):
                        m = nc.tensor.transpose(ps[:, 0, j * P:(j + 1) * P], cT32[:, j, :], ident[:])
                    m.then_inc(cT_ps, 1)
                pe.wait_ge(ct_lo, FROM + NCH)
                with pe.Fori(0, NG) as g:
                    def up(u):
                        ch, k = divmod(u, GT)
                        if ch == 0:
                            pe.wait_ge(w_hi, FROM + g * GT + k + 1)
                            pe.wait_ge(w_lo, FROM + g * GT + k + 1)
                        if u >= 2:
                            pe.wait_ge(hc_rdy, FROM + g * U + u - 1)
                        else:
                            pe.wait_ge(hc_rdy, FROM + g * U)
                        bank = 3 * (u % 2)
                        for z, (col, s) in enumerate(((W1, g_ps), (W3, u_ps))):
                            i = 0
                            for kt in range(KT):
                                for a, b in PARTS:
                                    m = nc.tensor.matmul(ps[:, bank + z, :], w[a][:, k, col + kt * P:col + (kt + 1) * P],
                                                         x[b][:, kt, ch * CH:(ch + 1) * CH], start=i == 0, stop=i == 5)
                                    i += 1
                            m.then_inc(s, 1)
                        for i in range(2):
                            m = nc.tensor.matmul(ps[:, bank + 2, :], wh[:, k, SEL:SEL + P], c[i][:, ch * CH:(ch + 1) * CH],
                                                 start=i == 0, stop=i == 1)
                        m.then_inc(c_ps, 1)

                    def down(u):
                        ch, k = divmod(u, GT)
                        pe.wait_ge(h_lo, FROM + g * U + u + 1)
                        if k == 0:
                            pe.wait_ge(y_add, FROM + g * NCH + ch)
                        for t in range(TC):
                            for i, (a, b) in enumerate(PARTS):
                                m = nc.tensor.matmul(ps[:, 6 + t // 2, (t % 2) * D:(t % 2 + 1) * D],
                                                     hp[a][:, u % RING, t * P:(t + 1) * P], w[b][:, k, W2:W2 + D],
                                                     start=k == 0 and i == 0 and t % 2 == 0, stop=k == GT - 1 and i == 2,
                                                     skip_group_check=True)
                        m.then_inc(y_ps, 1)

                    for u in range(U + LAG):
                        if u < U:
                            up(u)
                        if u >= LAG:
                            down(u - LAG)

            @block.scalar
            def _(act):
                for n in range(NCH):
                    act.wait_ge(cT_ps, FROM + n + 1)
                    nc.scalar.activation(cTh[:, n * CH:(n + 1) * CH], ps[:, 0, :], ACT.Copy).then_inc(ct_hi, 1)

                with act.Fori(0, NG) as g:
                    act.wait_ge(w_in, FROM + 16 * g + 16)
                    for k in range(GT):
                        act.wait_ge(y_ps, FROM + g * U)
                        nc.scalar.activation(wh[:, k, :], wst[:, k, :], ACT.Copy).then_inc(w_hi, 1)

                    def split(u):
                        act.wait_ge(hc_rdy, FROM + g * U + u + 1)
                        if u >= RING:
                            act.wait_ge(y_ps, FROM + g * U + u - RING + 1)
                        nc.scalar.activation(hh[:, u % RING, :], h32[:, u % 3, :], ACT.Copy).then_inc(h_hi, 1)

                    for u in range(U + 1):
                        if u < U:
                            act.wait_ge(g_ps, FROM + g * U + u + 1)
                            act.wait_ge(h_rdy, FROM + g * U + max(u - 1, 0))
                            nc.scalar.activation(th[:, u % 2, :], ps[:, 3 * (u % 2), :], ACT.Tanh, scale=0.5).then_inc(th_rdy, 1)
                        if u:
                            split(u - 1)

            @block.gpsimd
            def _(pool):
                with pool.Fori(0, NG) as g:
                    for u in range(U):
                        pool.wait_ge(h_hi, FROM + g * U + u + 1)
                        nc.gpsimd.tensor_tensor(hl[:, u % RING, :], h32[:, u % 3, :], hh[:, u % RING, :].bitcast(F32),
                                                ALU.subtract).then_inc(h_lo, 1)

            @block.vector
            def _(dve):
                nc.vector.memset(cT32[:], 0.0).then_inc(cp, 1)
                dve.wait_ge(cp, FROM + 1)
                for n in range(NCH):
                    if n:
                        dve.wait_ge(cT_ps, FROM + n)
                    nc.vector.tensor_copy(cT32[:, :, 0:E + 1], cb[:, n * TC:(n + 1) * TC, :]).then_inc(cp, 1)
                    dve.wait_ge(ct_hi, FROM + n + 1)
                    nc.vector.tensor_tensor(cTl[:, n * CH:(n + 1) * CH], ps[:, 0, :], cTh[:, n * CH:(n + 1) * CH].bitcast(F32),
                                            ALU.subtract).then_inc(ct_lo, 1)
                with dve.Fori(0, NG) as g:
                    for k in range(GT):
                        dve.wait_ge(w_hi, FROM + g * GT + k + 1)
                        nc.vector.tensor_tensor(wl[:, k, :], wst[:, k, :], wh[:, k, :].bitcast(F32), ALU.subtract).then_inc(w_lo, 1)
                    for u in range(U):
                        n = g * U + u
                        ch, k = divmod(u, GT)
                        bank = 3 * (u % 2)
                        t = th[:, u % 2, :]
                        h = h32[:, u % 3, :]
                        dve.wait_ge(th_rdy, FROM + n + 1)
                        nc.vector.scalar_tensor_tensor(t, t, 1.0, ps[:, bank, :], ALU.add, ALU.mult).then_inc(s_rdy, 1)
                        dve.wait_ge(s_rdy, FROM + n + 1)
                        dve.wait_ge(u_ps, FROM + n + 1)
                        dve.wait_ge(h_lo, FROM + g * U + max(u - 2, 0))
                        nc.vector.scalar_tensor_tensor(h, t, 0.5, ps[:, bank + 1, :], ALU.mult, ALU.mult).then_inc(h_rdy, 1)
                        dve.wait_ge(h_rdy, FROM + n + 1)
                        dve.wait_ge(c_ps, FROM + n + 1)
                        nc.vector.tensor_tensor(h, h, ps[:, bank + 2, :], ALU.mult).then_inc(hc_rdy, 1)

                        def add(chunk):
                            a = acc[:, chunk * TC:(chunk + 1) * TC, :].rearrange("p a b -> p (a b)")
                            dve.wait_ge(y_ps, FROM + g * U + (chunk + 1) * GT)
                            dve.wait_ge(y_add, FROM + g * NCH + chunk)
                            nc.vector.tensor_tensor(a, a, ps[:, 6:8, :].rearrange("p a b -> p (a b)"), ALU.add).then_inc(y_add, 1)

                        if k == 1 and ch:
                            add(ch - 1)
                        if u == U - 1:
                            add(ch)


_OUTS = [((1, T, D), "float32")]


def kernel(**inputs):
    import numpy as np
    import concourse.bacc as bacc
    from concourse.bass_utils import run_bass_kernel_spmd

    g = {k: np.asarray(v) for k, v in inputs.items()}

    def rows(w):
        return w.reshape(-1, P, w.shape[1]).transpose(1, 0, 2)

    gate = g["L0_ffn_w_gate"].reshape(KT, P, SG, P, 4).transpose(1, 2, 4, 0, 3)
    up = g["L0_ffn_w_up"].reshape(KT, P, SG, P, 4).transpose(1, 2, 4, 0, 3)
    down = g["L0_ffn_w_down"].reshape(SG, P, 4, D).transpose(1, 0, 2, 3)
    w0 = np.concatenate([
        rows(g["L0_attn_q_w"].T).reshape(P, -1), rows(g["L0_attn_o_w"].T).reshape(P, -1),
        np.concatenate([rows(g["L0_attn_k_w"].T), rows(g["L0_attn_v_w"].T)], 2).reshape(P, -1),
        np.stack([gate, up], 3).reshape(P, -1), down.reshape(P, -1)], 1)

    wk = rows(g["L1_attn_Wk"]).reshape(P, KT, NH, HD).transpose(0, 2, 1, 3)
    wv = rows(g["L1_attn_Wv"]).reshape(P, KT, NH, HD).transpose(0, 2, 1, 3)
    wo = g["L1_attn_Wo"].reshape(NH, HD, D).transpose(1, 0, 2)
    bv = np.broadcast_to(g["L1_attn_bv"].reshape(1, NH, HD), (P, NH, HD))
    wkv = np.concatenate([wk.reshape(P, NH, -1), wv.reshape(P, NH, -1), bv], 2)
    wq = rows(g["L1_attn_Wq"]).reshape(P, -1)

    pad = NI1 * P - ROWS
    zero = np.zeros((pad, D), g["L1_ffn_W1"].dtype)

    def units(routed, shared):
        return np.concatenate([routed.reshape(-1, D), shared, zero], 0)

    w1 = units(g["L1_ffn_W1"], g["L1_ffn_Ws1"]).reshape(NI1, P, KT, P).transpose(3, 0, 2, 1)
    w3 = units(g["L1_ffn_W3"], g["L1_ffn_Ws3"]).reshape(NI1, P, KT, P).transpose(3, 0, 2, 1)
    w2 = units(g["L1_ffn_W2"].transpose(0, 2, 1), g["L1_ffn_Ws2"].T).reshape(NI1, P, D).transpose(1, 0, 2)
    owner = np.minimum(np.arange(ROWS) // INTER1, E)
    sel = np.zeros((P, NI1 * P), np.float32)
    sel[owner, np.arange(ROWS)] = 1.0
    wexp = np.concatenate([w1.reshape(P, NI1, -1), w3.reshape(P, NI1, -1), w2, sel.reshape(P, NI1, P)], 2)

    i = np.arange(P)
    data = {
        "x": g["L0_attn_hidden_states"], "w0": w0, "bq0": g["L0_attn_q_b"].reshape(KT, P).T,
        "bkv0": np.concatenate([g["L0_attn_k_b"], g["L0_attn_v_b"]]), "bo0": g["L0_attn_o_b"],
        "wq": wq, "wkv1": wkv, "wo1": wo, "bq1": g["L1_attn_bq"].reshape(QC, HD).T, "bk1": g["L1_attn_bk"].reshape(NH, HD).T,
        "bo1": g["L1_attn_bo"], "wg": rows(g["L1_ffn_Wg"].T), "wexp": wexp,
        "ident": np.eye(P, dtype=np.float32), "bd": (i[:, None] // 16 == i[None, :] // 16).astype(np.float32),
        "causal": np.where(i[None, :] > i[:, None], np.float32(NEG), np.float32(0.0)),
        "tie": (i[None, :E] < i[:E, None]).astype(np.float32).reshape(-1),
    }
    nc = bacc.Bacc("TRN2", target_bir_lowering=False, num_devices=1)
    arrays, aps = {}, {}
    for name, a in data.items():
        a = np.ascontiguousarray(a)
        arrays["in_" + name] = a
        aps[name] = nc.dram_tensor("in_" + name, a.shape, mybir.dt.from_np(a.dtype), kind="ExternalInput").ap()
    out = nc.dram_tensor("out", _OUTS[0][0], F32, kind="ExternalOutput").ap()
    build(nc, aps, out)
    r = run_bass_kernel_spmd(nc, [arrays], core_ids=[0])
    return r.results[0]["out"]
```
